# Optimizing a Trainium2 kernel written in Bass

```python
import numpy as np
import jax
import jax.numpy as jnp

def _softmax(x, axis=-1):
    return jax.nn.softmax(x, axis=axis)

def _gelu(x):
    return jax.nn.gelu(x, approximate=True)

def _silu(x):
    return jax.nn.silu(x)

def _sigmoid(x):
    return jax.nn.sigmoid(x)

def _layernorm(x, axis=-1, eps=1e-05):
    m = jnp.mean(x, axis=axis, keepdims=True)
    v = jnp.var(x, axis=axis, keepdims=True)
    return (x - m) / jnp.sqrt(v + eps)

def _scatter_add(tgt, idx, src, axis=0):
    return tgt.at[idx].add(src)

def _segment_sum(src, seg, n):
    return jax.ops.segment_sum(src, seg, n)
kernel_name = 'mk_metaformer_d2_conv_nchw1024_r4_f7f9a3'

def setup_inputs(seed: int=0):
    np.random.seed(seed)
    _w = jnp.asarray

    def _rec_inputs():
        import jax
        import jax.numpy as jnp
        _gk = jax.random.key(seed)
        x = -0.0002023 + 1 * jax.random.normal(jax.random.fold_in(_gk, 1), (32, 256, 14, 14), jnp.float32)
        return x
    x = _rec_inputs()

    def _L0_conv_setup():
        import jax, jax.numpy as jnp
        import numpy as np
        EPS = 1e-05

        def _extract3x3(x, stride=1):
            B, C, H, W = x.shape
            xp = jnp.pad(x, ((0, 0), (0, 0), (1, 1), (1, 1)))
            Ho = (H + 2 - 3) // stride + 1
            Wo = (W + 2 - 3) // stride + 1
            pats = [xp[:, :, i:i + (Ho - 1) * stride + 1:stride, j:j + (Wo - 1) * stride + 1:stride] for i in range(3) for j in range(3)]
            return jnp.stack(pats, axis=2).reshape(B, C * 9, Ho, Wo)

        def _amm(patches, centroids, lut, inv_temp):
            B, D, H, W = patches.shape
            ncb, k, sub = centroids.shape
            v = patches.reshape(B, ncb, sub, H * W).transpose(0, 3, 1, 2)
            scores = 2.0 * jnp.einsum('blcs,cks->blck', v, centroids) - jnp.sum(centroids * centroids, -1)[None, None]
            attn = jax.nn.softmax(scores * inv_temp, axis=-1)
            out = jnp.einsum('blck,cko->blo', attn, lut)
            return out.transpose(0, 2, 1).reshape(B, -1, H, W)

        def _bn(x, g, b):
            m = x.mean((0, 2, 3), keepdims=True)
            v = x.var((0, 2, 3), keepdims=True)
            return g[None, :, None, None] * (x - m) * jax.lax.rsqrt(v + EPS) + b[None, :, None, None]
        key = jax.random.key(seed)
        ks = jax.random.split(key, 8)
        B, C, H, W = (32, 256, 14, 14)
        width, out_c, K = (64, 256, 16)
        return {'x': jax.random.normal(ks[0], (B, C, H, W), jnp.float32), 'c1_centroids': jax.random.normal(ks[1], (C // 4, K, 4), jnp.float32), 'c1_lut': jax.random.normal(ks[2], (C // 4, K, width), jnp.float32) * 0.05, 'c1_invt': jnp.ones((), jnp.float32), 'c2_centroids': jax.random.normal(ks[3], (width, K, 9), jnp.float32), 'c2_lut': jax.random.normal(ks[4], (width, K, width), jnp.float32) * 0.05, 'c2_invt': jnp.ones((), jnp.float32), 'c3_centroids': jax.random.normal(ks[5], (width // 4, K, 4), jnp.float32), 'c3_lut': jax.random.normal(ks[6], (width // 4, K, out_c), jnp.float32) * 0.05, 'c3_invt': jnp.ones((), jnp.float32), 'bn1_g': jnp.ones((width,), jnp.float32), 'bn1_b': jnp.zeros((width,), jnp.float32), 'bn2_g': jnp.ones((width,), jnp.float32), 'bn2_b': jnp.zeros((width,), jnp.float32), 'bn3_g': jnp.ones((out_c,), jnp.float32), 'bn3_b': jnp.zeros((out_c,), jnp.float32)}
    _L0_conv_all = _L0_conv_setup()
    _L0_conv_in = {k: v for k, v in _L0_conv_all.items() if k in ('c1_centroids', 'c1_lut', 'c1_invt', 'c2_centroids', 'c2_lut', 'c2_invt', 'c3_centroids', 'c3_lut', 'c3_invt', 'bn1_g', 'bn1_b', 'bn2_g', 'bn2_b', 'bn3_g', 'bn3_b')}
    del _L0_conv_all

    def _L0_ffn_setup():
        import jax, jax.numpy as jnp
        import numpy as np
        TOP_K = 2
        key = jax.random.key(seed)
        k1, k2, k3 = jax.random.split(key, 3)
        B, S, H, E, D = (4, 256, 256, 32, 256)
        x = jax.random.normal(k1, (B, S, H), dtype=jnp.float32)
        router_w = jax.random.normal(k2, (E, H), dtype=jnp.float32) * (1.0 / np.sqrt(H))
        bound = float(np.sqrt(6.0 / ((1.0 + 0.01 ** 2) * H)))
        expert_weights = jax.random.uniform(k3, (E, H, D), dtype=jnp.float32, minval=-bound, maxval=bound)
        return {'x': x, 'router_w': router_w, 'expert_weights': expert_weights}
    _L0_ffn_all = _L0_ffn_setup()
    _L0_ffn_in = {k: v for k, v in _L0_ffn_all.items() if k in ('router_w', 'expert_weights')}
    del _L0_ffn_all

    def _L1_conv_setup():
        import jax, jax.numpy as jnp
        import numpy as np
        key = jax.random.key(seed)
        ks = jax.random.split(key, 7)
        B, C, H, W = (16, 256, 32, 32)
        E, R = (8, 16)
        return {'x': jax.random.normal(ks[0], (B, C, H, W), dtype=jnp.float32), 'W1': jax.random.normal(ks[1], (E, R, C), dtype=jnp.float32) * 0.03, 'b1': jax.random.normal(ks[2], (E, R), dtype=jnp.float32) * 0.01, 'W2': jax.random.normal(ks[3], (E, C, R), dtype=jnp.float32) * 0.03, 'b2': jax.random.normal(ks[4], (E, C), dtype=jnp.float32) * 0.01, 'Wg': jax.random.normal(ks[5], (E, C), dtype=jnp.float32) * 0.03, 'bg': jax.random.normal(ks[6], (E,), dtype=jnp.float32) * 0.01}
    _L1_conv_all = _L1_conv_setup()
    _L1_conv_in = {k: v for k, v in _L1_conv_all.items() if k in ('W1', 'b1', 'W2', 'b2', 'Wg', 'bg')}
    del _L1_conv_all

    def _L1_ffn_setup():
        import jax, jax.numpy as jnp
        import numpy as np
        BS, L, D = (4, 512, 256)
        H, E, K = (8, 16, 2)
        HD = D // H
        I = 1024 // H
        key = jax.random.key(seed)
        ks = jax.random.split(key, 10)
        s = lambda k, shp, fan: jax.random.normal(k, shp, jnp.float32) / np.sqrt(fan)
        return {'x': jax.random.normal(ks[0], (BS, L, D), jnp.float32), 'Wm': s(ks[1], (D, D), D), 'bm': jnp.zeros((D,), jnp.float32), 'expert_emb': jax.random.normal(ks[2], (HD, E), jnp.float32), 'W1': s(ks[3], (E, HD, I), HD), 'b1': jnp.zeros((E, I), jnp.float32), 'W2': s(ks[4], (E, I, HD), I), 'b2': jnp.zeros((E, HD), jnp.float32), 'Wo': s(ks[5], (D, D), D), 'bo': jnp.zeros((D,), jnp.float32)}
    _L1_ffn_all = _L1_ffn_setup()
    _L1_ffn_in = {k: v for k, v in _L1_ffn_all.items() if k in ('Wm', 'bm', 'expert_emb', 'W1', 'b1', 'W2', 'b2', 'Wo', 'bo')}
    del _L1_ffn_all
    return {'x': x, 'L0_conv_c1_centroids': _L0_conv_in['c1_centroids'], 'L0_conv_c1_lut': _L0_conv_in['c1_lut'], 'L0_conv_c1_invt': _L0_conv_in['c1_invt'], 'L0_conv_c2_centroids': _L0_conv_in['c2_centroids'], 'L0_conv_c2_lut': _L0_conv_in['c2_lut'], 'L0_conv_c2_invt': _L0_conv_in['c2_invt'], 'L0_conv_c3_centroids': _L0_conv_in['c3_centroids'], 'L0_conv_c3_lut': _L0_conv_in['c3_lut'], 'L0_conv_c3_invt': _L0_conv_in['c3_invt'], 'L0_conv_bn1_g': _L0_conv_in['bn1_g'], 'L0_conv_bn1_b': _L0_conv_in['bn1_b'], 'L0_conv_bn2_g': _L0_conv_in['bn2_g'], 'L0_conv_bn2_b': _L0_conv_in['bn2_b'], 'L0_conv_bn3_g': _L0_conv_in['bn3_g'], 'L0_conv_bn3_b': _L0_conv_in['bn3_b'], 'L0_ffn_router_w': _L0_ffn_in['router_w'], 'L0_ffn_expert_weights': _L0_ffn_in['expert_weights'], 'L1_conv_W1': _L1_conv_in['W1'], 'L1_conv_b1': _L1_conv_in['b1'], 'L1_conv_W2': _L1_conv_in['W2'], 'L1_conv_b2': _L1_conv_in['b2'], 'L1_conv_Wg': _L1_conv_in['Wg'], 'L1_conv_bg': _L1_conv_in['bg'], 'L1_ffn_Wm': _L1_ffn_in['Wm'], 'L1_ffn_bm': _L1_ffn_in['bm'], 'L1_ffn_expert_emb': _L1_ffn_in['expert_emb'], 'L1_ffn_W1': _L1_ffn_in['W1'], 'L1_ffn_b1': _L1_ffn_in['b1'], 'L1_ffn_W2': _L1_ffn_in['W2'], 'L1_ffn_b2': _L1_ffn_in['b2'], 'L1_ffn_Wo': _L1_ffn_in['Wo'], 'L1_ffn_bo': _L1_ffn_in['bo']}

def reference(x, L0_conv_c1_centroids, L0_conv_c1_lut, L0_conv_c1_invt, L0_conv_c2_centroids, L0_conv_c2_lut, L0_conv_c2_invt, L0_conv_c3_centroids, L0_conv_c3_lut, L0_conv_c3_invt, L0_conv_bn1_g, L0_conv_bn1_b, L0_conv_bn2_g, L0_conv_bn2_b, L0_conv_bn3_g, L0_conv_bn3_b, L0_ffn_router_w, L0_ffn_expert_weights, L1_conv_W1, L1_conv_b1, L1_conv_W2, L1_conv_b2, L1_conv_Wg, L1_conv_bg, L1_ffn_Wm, L1_ffn_bm, L1_ffn_expert_emb, L1_ffn_W1, L1_ffn_b1, L1_ffn_W2, L1_ffn_b2, L1_ffn_Wo, L1_ffn_bo):
    import jax
    import jax.numpy as jnp

    def _L0_conv_ref(x, c1_centroids, c1_lut, c1_invt, c2_centroids, c2_lut, c2_invt, c3_centroids, c3_lut, c3_invt, bn1_g, bn1_b, bn2_g, bn2_b, bn3_g, bn3_b):
        import jax, jax.numpy as jnp
        import numpy as np
        EPS = 1e-05

        def _extract3x3(x, stride=1):
            B, C, H, W = x.shape
            xp = jnp.pad(x, ((0, 0), (0, 0), (1, 1), (1, 1)))
            Ho = (H + 2 - 3) // stride + 1
            Wo = (W + 2 - 3) // stride + 1
            pats = [xp[:, :, i:i + (Ho - 1) * stride + 1:stride, j:j + (Wo - 1) * stride + 1:stride] for i in range(3) for j in range(3)]
            return jnp.stack(pats, axis=2).reshape(B, C * 9, Ho, Wo)

        def _amm(patches, centroids, lut, inv_temp):
            B, D, H, W = patches.shape
            ncb, k, sub = centroids.shape
            v = patches.reshape(B, ncb, sub, H * W).transpose(0, 3, 1, 2)
            scores = 2.0 * jnp.einsum('blcs,cks->blck', v, centroids) - jnp.sum(centroids * centroids, -1)[None, None]
            attn = jax.nn.softmax(scores * inv_temp, axis=-1)
            out = jnp.einsum('blck,cko->blo', attn, lut)
            return out.transpose(0, 2, 1).reshape(B, -1, H, W)

        def _bn(x, g, b):
            m = x.mean((0, 2, 3), keepdims=True)
            v = x.var((0, 2, 3), keepdims=True)
            return g[None, :, None, None] * (x - m) * jax.lax.rsqrt(v + EPS) + b[None, :, None, None]
        identity = x
        out = _amm(x, c1_centroids, c1_lut, c1_invt)
        out = jax.nn.relu(_bn(out, bn1_g, bn1_b))
        out = _amm(_extract3x3(out, 1), c2_centroids, c2_lut, c2_invt)
        out = jax.nn.relu(_bn(out, bn2_g, bn2_b))
        out = _amm(out, c3_centroids, c3_lut, c3_invt)
        out = _bn(out, bn3_g, bn3_b)
        return jax.nn.relu(out + identity)

    def _L0_ffn_ref(x, router_w, expert_weights):
        import jax, jax.numpy as jnp
        import numpy as np
        TOP_K = 2
        B, S, H = x.shape
        E = router_w.shape[0]
        T = B * S
        logits = jnp.einsum('bsh,eh->bse', x, router_w)
        rw = jax.nn.softmax(logits, axis=-1).reshape(T, E)
        x_flat = x.reshape(T, H)
        vals, idx = jax.lax.top_k(rw, TOP_K)
        w_masked = jnp.zeros_like(rw).at[jnp.arange(T)[:, None], idx].set(vals)

        def body(acc, we):
            w_e, W_e = we
            return (acc + x_flat * w_e[:, None] @ W_e, None)
        out_flat, _ = jax.lax.scan(body, jnp.zeros((T, H), dtype=x.dtype), (w_masked.T, expert_weights))
        return out_flat.reshape(B, S, H)

    def _L1_conv_ref(x, W1, b1, W2, b2, Wg, bg):
        import jax, jax.numpy as jnp
        import numpy as np
        y = jnp.mean(x, axis=(2, 3))
        gate = jax.nn.softmax(y @ Wg.T + bg, axis=1)
        h = jax.nn.relu(jnp.einsum('bc,erc->ber', y, W1) + b1)
        s = jnp.einsum('ber,ecr->bec', h, W2) + b2
        scale = jax.nn.sigmoid(jnp.einsum('bec,be->bc', s, gate))
        return x * scale[:, :, None, None]

    def _L1_ffn_ref(x, Wm, bm, expert_emb, W1, b1, W2, b2, Wo, bo):
        import jax, jax.numpy as jnp
        import numpy as np
        BS, L, D = (4, 512, 256)
        H, E, K = (8, 16, 2)
        HD = D // H
        I = 1024 // H
        bs, L_, d = x.shape
        h = x @ Wm + bm
        t = h.reshape(bs * L_ * H, HD)
        logits = t @ expert_emb
        w = jax.nn.softmax(logits, axis=-1)
        topw, topi = jax.lax.top_k(w, K)
        hmid = jax.nn.gelu(jnp.einsum('td,edi->tei', t, W1) + b1, approximate=False)
        eo = jnp.einsum('tei,eio->teo', hmid, W2) + b2
        sel = jnp.take_along_axis(eo, topi[:, :, None], axis=1)
        comb = (sel * topw[:, :, None]).sum(axis=1)
        out = comb.reshape(bs, L_, d)
        return out @ Wo + bo

    def _gn(v, G=32, eps=1e-05):
        B_, C_, H_, W_ = v.shape
        g = v.reshape(B_, G, C_ // G, H_, W_)
        m = jnp.mean(g, axis=(2, 3, 4), keepdims=True)
        s = jnp.var(g, axis=(2, 3, 4), keepdims=True)
        return ((g - m) / jnp.sqrt(s + eps)).reshape(v.shape)

    def _ln_c(v, eps=1e-06):
        m = jnp.mean(v, axis=1, keepdims=True)
        s = jnp.var(v, axis=1, keepdims=True)
        return (v - m) / jnp.sqrt(s + eps)

    def _ln_t(v, eps=1e-05):
        m = jnp.mean(v, axis=-1, keepdims=True)
        s = jnp.var(v, axis=-1, keepdims=True)
        return (v - m) / jnp.sqrt(s + eps)

    def _to_tokens(v):
        B_, C_, H_, W_ = v.shape
        return v.reshape(B_, C_, H_ * W_).transpose(0, 2, 1)

    def _from_tokens(t, like):
        B_, C_, H_, W_ = like.shape
        return t.transpose(0, 2, 1).reshape(B_, C_, H_, W_)
    x = x + _L0_conv_ref(_ln_c(x), L0_conv_c1_centroids, L0_conv_c1_lut, L0_conv_c1_invt, L0_conv_c2_centroids, L0_conv_c2_lut, L0_conv_c2_invt, L0_conv_c3_centroids, L0_conv_c3_lut, L0_conv_c3_invt, L0_conv_bn1_g, L0_conv_bn1_b, L0_conv_bn2_g, L0_conv_bn2_b, L0_conv_bn3_g, L0_conv_bn3_b)
    t = _to_tokens(x)
    t = t + _L0_ffn_ref(_ln_t(t), L0_ffn_router_w, L0_ffn_expert_weights)
    x = _from_tokens(t, x)
    x = x + _L1_conv_ref(_ln_c(x), L1_conv_W1, L1_conv_b1, L1_conv_W2, L1_conv_b2, L1_conv_Wg, L1_conv_bg)
    t = _to_tokens(x)
    t = t + _L1_ffn_ref(_ln_t(t), L1_ffn_Wm, L1_ffn_bm, L1_ffn_expert_emb, L1_ffn_W1, L1_ffn_b1, L1_ffn_W2, L1_ffn_b2, L1_ffn_Wo, L1_ffn_bo)
    x = _from_tokens(t, x)
    return x

_drawn_inputs = setup_inputs


def setup_inputs(seed=0):
    import zlib

    import numpy as np

    out = dict(_drawn_inputs(seed))
    spreads = {'L0_conv_bn1_g': (1.0, 0.2),
     'L0_conv_bn1_b': (0.0, 0.1),
     'L0_conv_bn2_g': (1.0, 0.2),
     'L0_conv_bn2_b': (0.0, 0.1),
     'L0_conv_bn3_g': (1.0, 0.2),
     'L0_conv_bn3_b': (0.0, 0.1),
     'L1_ffn_bm': (0.0, 0.1),
     'L1_ffn_b1': (0.0, 0.314),
     'L1_ffn_b2': (0.0, 0.1),
     'L1_ffn_bo': (0.0, 0.1)}
    factors = {'L1_conv_W1': 43.34,
     'L1_conv_b1': 64.0,
     'L1_conv_W2': 33.655,
     'L1_conv_b2': 64.0,
     'L1_conv_Wg': 64.0,
     'L1_conv_bg': 64.0}
    for name, (base, spread) in spreads.items():
        noise = np.random.default_rng([zlib.crc32(name.encode()), seed]).standard_normal(out[name].shape)
        drawn = base * np.exp(spread * noise) if base else spread * noise
        out[name] = jnp.asarray(drawn.astype(out[name].dtype))
    for name, factor in factors.items():
        out[name] = (out[name] * factor).astype(out[name].dtype)
    return out
```

```python
from contextlib import ExitStack

import concourse.bass as bass
from concourse import mybir

F32 = mybir.dt.float32
F32R = mybir.dt.float32r
U32 = mybir.dt.uint32
ALU = mybir.AluOpType
ACT = mybir.ActivationFunctionType
AX = mybir.AxisListType

B, C, HH = 32, 256, 14
HW = HH * HH
IMGS = 2
CH = IMGS * HW
T = B // IMGS
SUB = 98
NSUB = CH // SUB
PADW = 16
PADHW = PADW * PADW
WID = 64
KC = 16
E0 = 32
NH, NE, HD, HID = 8, 16, 32, 128
NEG = -3.0e38
EPS_LN_C, EPS_LN_T, EPS_BN = 1e-6, 1e-5, 1e-5
SLOTS = 10


def wait(eng, sem, value):
    if not (isinstance(value, int) and value <= 0):
        eng.wait_ge(sem, value)


def staged(eng, front, back, count=T, slots=SLOTS):
    def step(a, b):
        for k in range(slots):
            if a is not None:
                front(k, *a)
            if b is not None:
                back(k, *b)
    step((0, 0, 0), None)
    step((1, 0, 1), (0, 0, 0))
    with eng.Fori(0, count // 2 - 1) as i:
        step((i * 2 + 2, i + 1, 0), (i * 2 + 1, i, 1))
        step((i * 2 + 3, i + 1, 1), (i * 2 + 2, i + 1, 0))
    step(None, (count - 1, count // 2 - 1, 1))


def nothing(k, t, n, u):
    pass


def at_chunk(t, size=1):
    return slice(t * size, (t + 1) * size) if isinstance(t, int) else bass.ds(t * size, size)


def build(nc, x, c1T, c2T, c3T, invts, lut1, lut2, lut3, bn1, bn2, bn3, routerT, w_moe,
          se_w1T, se_b1, se_w2T, se_b2, se_wgT, se_bg, wm, bm, emb, w1, b1, w2, b2, wo, bo, out):
    with ExitStack() as ctx:
        def sb(name, shape, dt=F32):
            return ctx.enter_context(nc.sbuf_tensor(name, shape, dt))

        owner = [ctx]

        def sem(name):
            return nc.alloc_semaphore(name=name)

        def phase():
            stack = ctx.enter_context(ExitStack())
            before_ = nc.snapshot_sems()

            def give_back():
                nc.clear_and_free_semaphores(nc.allocated_since(before_))
                nc.all_engine_barrier()
            stack.callback(give_back)
            owner.append(stack)
            stack.callback(owner.pop)
            return stack

        V = sb("V", [128, 2, T, CH])
        BIG = sb("BIG", [128, E0 * 2 * C])
        OUT = BIG[:, 0:2 * T * CH].rearrange("p (h t c) -> p h t c", h=2, t=T)
        YS = sb("YS", [128, T, 2, IMGS])
        xs = sb("xs", [128, 2, 2, CH])
        vv = sb("vv", [128, 2, 2, CH])
        vr = sb("vr", [128, 2, CH], F32R)
        sq = sb("sq", [128, 2, CH])
        rs = sb("rs", [128, CH])
        nm = sb("nm", [SUB, NSUB, 64])
        nmT = sb("nmT", [64, 2, CH], F32R)
        ex = sb("ex", [128, 2, CH])
        at = sb("at", [128, 2, CH])
        rz = sb("rz", [128, 2, CH])
        stats = sb("stats", [128, 2, T, 6])
        aggr = sb("aggr", [128, 2, 2])
        bns = sb("bns", [128, 2])
        bnb = sb("bnb", [128, 2])
        bnt = sb("bnt", [128, 2])
        gb1 = sb("gb1", [64, 2])
        gb2 = sb("gb2", [64, 2])
        gb3 = sb("gb3", [128, 2, 2])
        inv = sb("inv", [128, 3])
        inv2 = sb("inv2", [128, 3])
        mean_w = sb("mean_w", [128, 128])
        ident = sb("ident", [128, 128])
        ones_c = sb("ones_c", [128, 1])
        ones_r = sb("ones_r", [128, 128], F32R)
        group_w = sb("group_w", [128, 128])
        ind = sb("ind", [64, 1024])
        ind_r = sb("ind_r", [64, 1024], F32R)
        eps_c = sb("eps_c", [128, 1])
        eps_t = sb("eps_t", [128, 1])

        psM = ctx.enter_context(nc.psum_tensor("psM", [128, 512], F32))
        psN = ctx.enter_context(nc.psum_tensor("psN", [128, 2, 512], F32))
        psS = ctx.enter_context(nc.psum_tensor("psS", [128, 2, 512], F32))
        psZ = ctx.enter_context(nc.psum_tensor("psZ", [128, 2, 512], F32))
        psO = ctx.enter_context(nc.psum_tensor("psO", [128, 512], F32))

        ypad_d = nc.dram_tensor("ypad_d", [WID, B * PADHW + 64], F32)
        x_v = x.rearrange("(t b) (h p) w -> t p h b w", b=IMGS, h=2)
        out_v = out.rearrange("(t b) (h p) w -> t p h b w", b=IMGS, h=2)

        s_const = sem("s_const")
        s_go = sem("s_go")

        def wait_alone(eng, s, value):
            if isinstance(value, int):
                wait(eng, s, value)
            else:
                count = eng.snap(eng.to_reg(value))
                eng.wait_ge(s_go, 1)
                eng.wait_ge(s, count)

        def dma_x(eng, t, n, u, free, need, landed):
            wait(eng, free, need)
            for h in range(2):
                src = x_v[t:t + 1] if isinstance(t, int) else x_v[bass.ds(t, 1)]
                eng.dma_start(xs[:, u, h].rearrange("p (b w) -> p b w", b=IMGS),
                              src[0, :, h]).then_inc(landed[u], 16)

        s_set = sem("s_set")
        s_iota = sem("s_iota")
        with nc.Block() as block:
            @block.sync
            def _(eng):
                eng.dma_start(inv[:], invts.partition_broadcast(128)).then_inc(s_const, 16)
                eng.dma_start(gb1[:], bn1).then_inc(s_const, 16)
                eng.dma_start(gb2[:], bn2).then_inc(s_const, 16)
                eng.dma_start(gb3[:], bn3.rearrange("(h p) k -> p h k", p=128)).then_inc(s_const, 16)
                eng.wait_ge(s_const, 64)

            @block.gpsimd
            def _(eng):
                eng.memset(mean_w[:], 1.0 / C)
                eng.memset(ones_c[:], 1.0)
                eng.memset(eps_c[:], EPS_LN_C)
                eng.memset(eps_t[:], EPS_LN_T)
                eng.memset(ident[:], 0.0)
                eng.memset(group_w[:], 1.0)
                eng.memset(ind[:], 1.0).then_inc(s_iota, 1)
                eng.wait_ge(s_iota, 1)
                eng.affine_select(out=ident[:], in_=ident[:], compare_op=ALU.not_equal, fill=1.0, base=0,
                                  pattern=[[-1, 128]], channel_multiplier=1)
                eng.affine_select(out=ind[:], in_=ind[:], compare_op=ALU.is_ge, fill=0.0, base=0,
                                  pattern=[[1, 1024]], channel_multiplier=-KC)
                gv = group_w[:].rearrange("p (a b) -> p a b", b=KC)
                eng.affine_select(out=gv, in_=gv, compare_op=ALU.is_ge, fill=0.0, base=0,
                                  pattern=[[-KC, 8], [0, KC]], channel_multiplier=1).then_inc(s_iota, 1)
                eng.wait_ge(s_iota, 2)
                eng.affine_select(out=ind[:], in_=ind[:], compare_op=ALU.is_ge, fill=0.0, base=KC - 1,
                                  pattern=[[-1, 1024]], channel_multiplier=KC)
                eng.affine_select(out=gv, in_=gv, compare_op=ALU.is_ge, fill=0.0, base=KC - 1,
                                  pattern=[[KC, 8], [0, KC]], channel_multiplier=-1).then_inc(s_iota, 1)
                eng.wait_ge(s_iota, 3)
                eng.tensor_copy(ind_r[:], ind[:])
                eng.tensor_copy(ones_r[:], ones_c[:].to_broadcast([128, 128])).then_inc(s_iota, 1)

            @block.vector
            def _(eng):
                eng.wait_ge(s_const, 64)
                eng.tensor_scalar(inv2[:], inv[:], 2.0, None, ALU.mult).then_inc(s_set, 1)
                eng.wait_ge(s_set, 1)
                eng.tensor_scalar(inv[:], inv[:], -1.0, None, ALU.mult).then_inc(s_go, 1)

            @block.scalar
            def _(eng):
                eng.preload_act_table_set("natural_log_exp_and_others")

        class Norm:

            def __init__(self, name, eps):
                self.eps = eps
                self.mean, self.dev, self.sqr, self.var, self.log, self.rstd, self.done = (
                    sem(f"{name}_{x}") for x in ("mean", "dev", "sqr", "var", "log", "rstd", "done"))

            def pe_mean(self, eng, t, src):
                for h in range(2):
                    m = eng.matmul(psM[:, 0:CH], mean_w[:], src[:, h], start=(h == 0), stop=(h == 1))
                m.then_inc(self.mean, 1)

            def dve_dev(self, eng, t, src, dst):
                wait(eng, self.mean, t + 1)
                eng.tensor_tensor(dst, src, psM[:, 0:CH].unsqueeze(1).to_broadcast([128, 2, CH]),
                                  ALU.subtract).then_inc(self.dev, 1)

            def act_square(self, eng, t, d):
                wait(eng, self.dev, t + 1)
                eng.activation(sq[:], d, ACT.Square).then_inc(self.sqr, 1)

            def pe_var(self, eng, t):
                wait(eng, self.sqr, t + 1)
                for h in range(2):
                    m = eng.matmul(psM[:, 0:CH], mean_w[:], sq[:, h], start=(h == 0), stop=(h == 1))
                m.then_inc(self.var, 1)

            def act_rstd(self, eng, t):
                wait(eng, self.var, t + 1)
                wait(eng, self.done, t)
                eng.activation(rs[:], psM[:, 0:CH], ACT.Ln, bias=self.eps[:, 0:1]).then_inc(self.log, 1)
                wait(eng, self.log, t + 1)
                eng.activation(rs[:], rs[:], ACT.Exp, scale=-0.5).then_inc(self.rstd, 1)

            def dve_norm(self, eng, t, d, dst):
                wait_alone(eng, self.rstd, t + 1)
                return eng.tensor_tensor(dst, d, rs[:].unsqueeze(1).to_broadcast([128, 2, CH]), ALU.mult)

        def amm(name, J, KP, ncb, O, which, cT, lut, blocks, extent, n_scores, t_scores, prep, out_half):
            cols = ncb * KC
            with phase() as c2:
                def sb2(n, shape, dt=F32):
                    return c2.enter_context(nc.sbuf_tensor(f"{name}_{n}", shape, dt))

                cen = sb2("cen", [KP, blocks, KC])
                per = cols // blocks // KC
                wb = sb2("wb", [KP, blocks, per, KC])
                cb = sb2("cb", [KP, blocks, per, KC])
                wb_r = sb2("wb_r", [KP, blocks, per * KC], F32R)
                cb_r = sb2("cb_r", [KP, blocks, per * KC], F32R)
                lut_s = sb2("lut_s", [128, J, O])
                bias_t = sb2("bias_t", [128, J])
                mem = prep["memory"](sb2)
                S = {x: sem(f"{name}_{x}") for x in (
                    "cen", "w", "bias", "src", "nsc", "max", "tr", "nmt", "sc", "exp", "z", "rec", "div", "lut",
                    "out", "relu")}
                ld = [sem(f"{name}_ld{u}") for u in range(2)]
                norm = Norm(name, eps_c) if prep.get("norm") else None
                env = dict(S=S, ld=ld, norm=norm, mem=mem)

                with nc.Block() as block:
                    @block.sync
                    def _(eng):
                        eng.dma_start(cen[:], cT).then_inc(S["cen"], 16)
                        eng.dma_start(lut_s[:], lut.rearrange("(j p) o -> p j o", p=128)).then_inc(S["cen"], 16)
                        if "setup_dma" in prep:
                            prep["setup_dma"](eng, env)
                        eng.wait_ge(S["cen"], 32)

                    @block.vector
                    def _(eng):
                        if "setup_dve" in prep:
                            prep["setup_dve"](eng, env)
                        eng.memset(nmT[:].bitcast(F32), 0.0)
                        eng.wait_ge(S["cen"], 32)
                        for b in range(blocks):
                            cin = cen[:, b].unsqueeze(1).to_broadcast([KP, per, KC])
                            eng.tensor_scalar(wb[:, b], cin, inv2[0:KP, which:which + 1], None, ALU.mult)
                            m = eng.tensor_tensor(cb[:, b], cin, cin, ALU.mult)
                        m.then_inc(S["w"], 1)
                        eng.wait_ge(S["w"], 1)
                        eng.tensor_scalar(cb[:], cb[:], inv[0:KP, which:which + 1], None, ALU.mult).then_inc(S["w"], 1)
                        eng.wait_ge(S["w"], 4)
                        eng.tensor_copy(wb_r[:], wb[:].rearrange("p b a k -> p b (a k)"))
                        eng.tensor_copy(cb_r[:], cb[:].rearrange("p b a k -> p b (a k)")).then_inc(S["w"], 1)
                        eng.wait_ge(S["bias"], 1)
                        eng.tensor_copy(bias_t[:], psO[:, 0:J]).then_inc(S["bias"], 1)

                    @block.gpsimd
                    def _(eng):
                        eng.wait_ge(S["w"], 2)
                        for w_ in (wb, cb):
                            for b in range(blocks):
                                m = eng.affine_select(out=w_[:, b], in_=w_[:, b], compare_op=ALU.is_ge, fill=0.0,
                                                      base=0, pattern=[[-extent, per], [0, KC]],
                                                      channel_multiplier=1)
                        m.then_inc(S["w"], 1)
                        eng.wait_ge(S["w"], 3)
                        for w_ in (wb, cb):
                            for b in range(blocks):
                                m = eng.affine_select(out=w_[:, b], in_=w_[:, b], compare_op=ALU.is_ge, fill=0.0,
                                                      base=extent - 1, pattern=[[extent, per], [0, KC]],
                                                      channel_multiplier=-1)
                        m.then_inc(S["w"], 1)

                    @block.tensor
                    def _(eng):
                        eng.wait_ge(S["w"], 4)
                        cbf = cb[:].rearrange("p b a k -> p (b a k)")
                        per_tile = 128
                        for j in range(J):
                            m = eng.matmul(psO[:, j:j + 1], cbf[:, j * per_tile:(j + 1) * per_tile],
                                           ones_c[0:KP, :], start=True, stop=True)
                        m.then_inc(S["bias"], 1)

                    @block.scalar
                    def _(eng):
                        if "setup_act" in prep:
                            prep["setup_act"](eng, env)

                Zb = 2 if O <= 64 else 1
                outs = [psO] if O <= 64 else [psO, psZ[:, 1]]
                OP = min(O, 128)

                with nc.Block() as block:
                    @block.sync
                    def _(eng):
                        if "sync" in prep:
                            staged(eng, lambda k, t, n, u: prep["sync"](eng, env, k, t, n, u), nothing)
                        if "sync_end" in prep:
                            prep["sync_end"](eng, env)

                    @block.gpsimd
                    def _(eng):
                        def back(k, t, n, u):
                            if 1 <= k <= J:
                                g = t * J + k - 1
                                wait(eng, S["rec"], g + 1)
                                wait(eng, S["lut"], g - 1)
                                eng.tensor_tensor(at[:, (k - 1) % 2], ex[:, (k - 1) % 2], rz[:, (k - 1) % 2],
                                                  ALU.mult).then_inc(S["div"], 1)
                        staged(eng, lambda k, t, n, u: prep["pool"](eng, env, k, t, n, u), back)

                    @block.tensor
                    def _(eng):
                        def front(k, t, n, u):
                            if "pe" in prep:
                                prep["pe"](eng, env, k, t, n, u)
                            if 2 <= k < 2 + NSUB:
                                s = k - 2
                                if s == 0:
                                    wait_alone(eng, S["src"], t + 1)
                                wait_alone(eng, S["max"], t * NSUB + s)
                                for dst, src, b, lo, hi in n_scores(env, u, s):
                                    K = src.shape[0]
                                    eng.matmul(dst, src, wb_r[0:K, b, lo:hi], start=True, stop=False)
                                    m = eng.matmul(dst, ones_r[0:K, 0:SUB], cb_r[0:K, b, lo:hi],
                                                   start=False, stop=True)
                                m.then_inc(S["nsc"], 1)
                            if k == 2 + NSUB:
                                wait_alone(eng, S["max"], t * NSUB + NSUB)
                                wait_alone(eng, S["nmt"], t)
                                for s in range(NSUB):
                                    m = eng.transpose(psM[0:ncb, s * SUB:(s + 1) * SUB], nm[:, s, 0:ncb],
                                                      ident[0:SUB, 0:SUB])
                                m.then_inc(S["tr"], 1)

                        def back(k, t, n, u):
                            if k < J:
                                g = t * J + k
                                if k == 0:
                                    wait_alone(eng, S["nmt"], t + 1)
                                wait_alone(eng, S["exp"], g - 1)
                                w_, src = t_scores(env, wb, k, u)
                                eng.matmul(psS[:, k % 2, 0:CH], w_, src, start=True, stop=False)
                                eng.matmul(psS[:, k % 2, 0:CH], ind_r[:, k * 128:(k + 1) * 128],
                                           nmT[:, u, :], start=False, stop=True).then_inc(S["sc"], 1)
                            if 1 <= k <= J:
                                g = t * J + k - 1
                                wait(eng, S["exp"], g + 1)
                                wait(eng, S["rec"], g + 1 - Zb)
                                eng.matmul(psZ[:, (k - 1) % Zb, 0:CH], group_w[:], ex[:, (k - 1) % 2],
                                           start=True, stop=True).then_inc(S["z"], 1)
                            if 2 <= k <= J + 1:
                                j = k - 2
                                wait_alone(eng, S["div"], t * J + j + 1)
                                if j == 0:
                                    wait_alone(eng, S["out"], t)
                                for o, dst in enumerate(outs):
                                    m = eng.matmul(dst[0:OP, 0:CH], lut_s[:, j, o * 128:o * 128 + OP],
                                                   at[:, j % 2], start=(j == 0), stop=(j == J - 1))
                                m.then_inc(S["lut"], 1)
                        staged(eng, front, back)

                    @block.vector
                    def _(eng):
                        def front(k, t, n, u):
                            if "dve" in prep:
                                prep["dve"](eng, env, k, t, n, u)
                            if 2 <= k < 2 + NSUB:
                                s = k - 2
                                wait(eng, S["nsc"], t * NSUB + s + 1)
                                if s == 0:
                                    wait(eng, S["tr"], t)
                                flat = psN[0:SUB].rearrange("p a b -> p (a b)")[:, 0:cols]
                                eng.tensor_reduce(nm[:, s, 0:ncb], flat.rearrange("p (c k) -> p c k", k=KC), AX.X,
                                                  ALU.max, negate=True).then_inc(S["max"], 1)

                        def back(k, t, n, u):
                            if 1 <= k <= J:
                                g = t * J + k - 1
                                wait(eng, S["z"], g + 1)
                                wait(eng, S["div"], g - 1)
                                eng.reciprocal(rz[:, (k - 1) % 2], psZ[:, (k - 1) % Zb, 0:CH]).then_inc(S["rec"], 1)
                            if k == SLOTS - 1:
                                wait_alone(eng, S["lut"], t * J + J)
                                for o, dst in enumerate(outs):
                                    oh = out_half if len(outs) == 1 else o
                                    ts = slice(t, t + 1) if isinstance(t, int) else bass.ds(t, 1)
                                    eng.bn_stats(stats[0:OP, o, ts], dst[0:OP, 0:CH])
                                    m = eng.tensor_copy(OUT[0:OP, oh, ts],
                                                        dst[0:OP, 0:CH].unsqueeze(1))
                                m.then_inc(S["out"], 1)
                        staged(eng, front, back)

                    @block.scalar
                    def _(eng):
                        def front(k, t, n, u):
                            if "act" in prep:
                                prep["act"](eng, env, k, t, n, u)
                            if k == 2 + NSUB:
                                wait(eng, S["tr"], t + 1)
                                eng.activation(nmT[0:ncb, u], psM[0:ncb, 0:CH], ACT.Copy).then_inc(S["nmt"], 1)

                        def back(k, t, n, u):
                            if k < J:
                                g = t * J + k
                                wait(eng, S["sc"], g + 1)
                                wait(eng, S["div"], g - 1)
                                eng.activation(ex[:, k % 2], psS[:, k % 2, 0:CH], ACT.Exp,
                                               bias=bias_t[:, k:k + 1]).then_inc(S["exp"], 1)
                        staged(eng, front, back)

        def bn_coefs(name, halves, P, gb):
            s = sem(f"{name}_bn")
            with nc.Block() as block:
                @block.vector
                def _(eng):
                    for h in range(halves):
                        m = eng.bn_aggr(aggr[0:P, h], stats[0:P, h].rearrange("p t k -> p (t k)"))
                    m.then_inc(s, 1)
                    eng.wait_ge(s, 3)
                    g = gb[0:P].unsqueeze(1) if halves == 1 else gb[:]
                    eng.tensor_tensor(bns[0:P, 0:halves], bnt[0:P, 0:halves], g[:, :, 0], ALU.mult).then_inc(s, 1)
                    eng.wait_ge(s, 4)
                    eng.tensor_tensor(bnt[0:P, 0:halves], aggr[0:P, 0:halves, 0], bns[0:P, 0:halves],
                                      ALU.mult).then_inc(s, 1)
                    eng.wait_ge(s, 5)
                    eng.tensor_tensor(bnb[0:P, 0:halves], g[:, :, 1], bnt[0:P, 0:halves], ALU.subtract).then_inc(s, 1)

                @block.scalar
                def _(eng):
                    eng.wait_ge(s, 1)
                    eng.activation(bnt[0:P, 0:halves], aggr[0:P, 0:halves, 1], ACT.Ln,
                                   bias=eps_t[0:P, 0:1]).then_inc(s, 1)
                    eng.wait_ge(s, 2)
                    eng.activation(bnt[0:P, 0:halves], bnt[0:P, 0:halves], ACT.Exp, scale=-0.5).then_inc(s, 1)

        def a_sync(eng, env, k, t, n, u):
            if k == 0:
                dma_x(eng, t, n, u, env["norm"].dev, t - 1, env["ld"])

        def a_pe(eng, env, k, t, n, u):
            if k == 0:
                wait(eng, env["ld"][u], (n + 1) * 32)
                wait(eng, env["S"]["nmt"], t)
                env["norm"].pe_mean(eng, t, xs[:, u])
            if k == 1:
                env["norm"].pe_var(eng, t)

        def a_dve(eng, env, k, t, n, u):
            if k == 0:
                wait(eng, env["S"]["lut"], (t - 1) * 8)
                env["norm"].dve_dev(eng, t, xs[:, u], vv[:, u])
            if k == 1:
                env["norm"].dve_norm(eng, t, vv[:, u], vv[:, u]).then_inc(env["norm"].done, 1)

        def a_act(eng, env, k, t, n, u):
            if k == 0:
                wait(eng, env["norm"].var, t)
                env["norm"].act_square(eng, t, vv[:, u])
            if k == 1:
                env["norm"].act_rstd(eng, t)

        def a_pool(eng, env, k, t, n, u):
            if k == 1:
                wait_alone(eng, env["norm"].done, t + 1)
                wait_alone(eng, env["S"]["nsc"], t * NSUB)
                eng.tensor_copy(vr[:], vv[:, u]).then_inc(env["S"]["src"], 1)
                ts = slice(t, t + 1) if isinstance(t, int) else bass.ds(t, 1)
                eng.tensor_copy(V[:, :, ts].rearrange("p h t c -> p h (t c)"), vv[:, u])

        def a_n(env, u, s):
            for b in range(2):
                yield (psN[0:SUB, b, :], vr[:, b, s * SUB:(s + 1) * SUB], b, 0, 512)

        def a_t(env, wb, j, u):
            q = 32 * (j % 4)
            w_ = wb[:].rearrange("p b a k -> p b (a k)")[q:q + 32, j // 4, (j % 4) * 128:(j % 4) * 128 + 128]
            return w_, vv[q:q + 32, u, j // 4, :]

        amm("a", 8, 128, 64, WID, 0, c1T.rearrange("(h p) k -> p h k", p=128), lut1, 2, 4, a_n, a_t,
            dict(memory=lambda sb2: None, norm=True, sync=a_sync, pe=a_pe, dve=a_dve, act=a_act, pool=a_pool), 0)
        bn_coefs("a", 1, WID, gb1)

        with nc.sbuf_tensor("ypad", [WID, B, PADW, PADW], F32) as ypad:
            s_pad0, s_pad, s_padst = sem("s_pad0"), sem("s_pad"), sem("s_padst")
            with nc.Block() as block:
                @block.vector
                def _(eng):
                    eng.memset(ypad[:], 0.0).then_inc(s_pad0, 1)

                @block.scalar
                def _(eng):
                    eng.wait_ge(s_pad0, 1)
                    for t in range(T):
                        src = OUT[0:WID, 0, t].rearrange("p (b r w) -> p b r w", b=IMGS, r=HH)
                        for b in range(IMGS):
                            m = eng.activation(ypad[:, t * IMGS + b, 1:1 + HH, 1:1 + HH], src[:, b], ACT.Relu,
                                               bias=bnb[0:WID, 0:1], scale=bns[0:WID, 0:1])
                    m.then_inc(s_pad, 1)

                @block.sync
                def _(eng):
                    eng.wait_ge(s_pad, 1)
                    flat = ypad[:].rearrange("p b r w -> p (b r w)")
                    eng.dma_start(ypad_d.ap()[:, 0:B * PADHW], flat).then_inc(s_padst, 16)
                    eng.dma_start(ypad_d.ap()[:, B * PADHW:], flat[:, 0:64]).then_inc(s_padst, 16)
                    eng.wait_ge(s_padst, 32)

        def b_memory(sb2):
            size = 8 * IMGS * HH * PADW
            free = BIG[0:72, 2 * T * CH:2 * T * CH + size].rearrange("p (g c) -> p g c", g=8)
            return dict(pat=[free, sb2("pat", [72, 8, IMGS * HH * PADW])], pat_r=sb2("pat_r", [72, 8, CH], F32R))

        def b_sync(eng, env, k, t, n, u):
            if k == 0:
                wait(eng, env["S"]["lut"], (t - 1) * 8)
                pat = env["mem"]["pat"]
                for tap in range(9):
                    off = (tap // 3) * PADW + tap % 3
                    src = ypad_d.ap()[:, off:off + B * PADHW].rearrange("(g c) (t b r) -> t c g b r", g=8, b=IMGS, r=PADHW)
                    src = (src[t:t + 1] if isinstance(t, int) else src[bass.ds(t, 1)])[0]
                    for b in range(IMGS):
                        eng.dma_start(pat[u][tap:tap + 64:9, :, b * HH * PADW:(b + 1) * HH * PADW],
                                      src[:, :, b, 0:HH * PADW]).then_inc(env["ld"][u], 16)

        def b_pool(eng, env, k, t, n, u):
            if k == 1:
                wait_alone(eng, env["ld"][u], (n + 1) * 16 * 9 * IMGS)
                wait_alone(eng, env["S"]["nsc"], t * NSUB)
                src = env["mem"]["pat"][u].rearrange("p g (r w) -> p g r w", w=PADW)[:, :, :, 0:HH]
                dst = env["mem"]["pat_r"][:].rearrange("p g (r w) -> p g r w", w=HH)
                eng.tensor_copy(dst, src).then_inc(env["S"]["src"], 1)

        def b_n(env, u, s):
            flat = psN[0:SUB].rearrange("p a b -> p (a b)")
            for g in range(8):
                v = env["mem"]["pat_r"][:, g, s * SUB:(s + 1) * SUB]
                yield (flat[:, g * 128:(g + 1) * 128], v, g, 0, 128)

        def b_t(env, wb, j, u):
            v = env["mem"]["pat"][u][:, j].rearrange("p (r w) -> p r w", w=PADW)[:, :, 0:HH]
            return wb[:, j].rearrange("p a k -> p (a k)"), v

        amm("b", 8, 72, 64, WID, 1, c2T, lut2, 8, 9, b_n, b_t,
            dict(memory=b_memory, sync=b_sync, pool=b_pool), 1)
        bn_coefs("b", 1, WID, gb2)

        def c_memory(sb2):
            return dict(y=sb2("y", [WID, 2, CH]), y_r=sb2("y_r", [WID, CH], F32R))

        def c_act(eng, env, k, t, n, u):
            if k == 0:
                wait_alone(eng, env["S"]["lut"], (t - 1) * 2)
                ts = slice(t, t + 1) if isinstance(t, int) else bass.ds(t, 1)
                eng.activation(env["mem"]["y"][:, u], OUT[0:WID, 1, ts].rearrange("p t c -> p (t c)"), ACT.Relu,
                               bias=bnb[0:WID, 0:1], scale=bns[0:WID, 0:1]).then_inc(env["S"]["relu"], 1)

        def c_pool(eng, env, k, t, n, u):
            if k == 1:
                wait_alone(eng, env["S"]["relu"], t + 1)
                wait_alone(eng, env["S"]["nsc"], t * NSUB)
                eng.tensor_copy(env["mem"]["y_r"][:], env["mem"]["y"][:, u]).then_inc(env["S"]["src"], 1)

        def c_n(env, u, s):
            yield (psN[0:SUB, 0, 0:256], env["mem"]["y_r"][:, s * SUB:(s + 1) * SUB], 0, 0, 256)

        def c_t(env, wb, j, u):
            w_ = wb[:].rearrange("p b a k -> p (b a k)")[32 * j:32 * j + 32, j * 128:(j + 1) * 128]
            return w_, env["mem"]["y"][32 * j:32 * j + 32, u]

        amm("c", 2, 64, 16, C, 2, c3T.rearrange("p (b k) -> p b k", b=1), lut3, 1, 4, c_n, c_t,
            dict(memory=c_memory, act=c_act, pool=c_pool), 0)
        bn_coefs("c", 2, 128, gb3)

        NT = T * NSUB
        ROWS = 128
        TILES = -(-2 * B * HW // ROWS) + E0
        TILES += TILES % 2
        RT = 19
        xn_d = nc.dram_tensor("xn_d", [NT * SUB, C], F32)
        xg_d = nc.dram_tensor("xg_d", [TILES * ROWS, C], F32)
        yg_d = nc.dram_tensor("yg_d", [TILES * ROWS, C], F32)
        d_ctx = phase()

        def sbd(name, shape, dt=F32):
            return d_ctx.enter_context(nc.sbuf_tensor(name, shape, dt))
        w_moe_s = BIG
        router_s = sbd("router_s", [128, 2, E0])
        before = sbd("before", [SUB, SUB])
        ones_s = sbd("ones_s", [SUB, SUB])
        iota_i = sbd("iota_i", [SUB, 192], U32)
        rev = sbd("rev", [SUB, E0])
        xnb = sbd("xnb", [SUB, 2, NSUB, C])
        lg = sbd("lg", [SUB, 11, NSUB, E0])
        LG, EQ, M1, LG2, M2, MASK, DL, EX, TMP = range(9)
        sc_ = sbd("sc_", [SUB, 8, NSUB])
        seen = sbd("seen", [SUB, 2, E0])
        P12 = sbd("P12", [SUB, T, NSUB, 2])
        MK = sbd("MK", [SUB, 2, NT])
        POS = sbd("POS", [SUB, 2, NT])
        SLOT = sbd("SLOT", [SUB, T, NSUB, 2], U32)
        EID = sbd("EID", [SUB, TILES], U32)

        dn = Norm("d", eps_t)
        D = {k: sem(f"d_{k}") for k in ("w", "set", "pre", "relu", "x1", "vst", "tr", "ev", "lgd", "rt", "exp",
                                        "pfx", "mid")}
        d_ld = [sem(f"d_ld{u}") for u in range(2)]
        d_xst = [sem(f"d_xst{u}") for u in range(2)]
        with nc.Block() as block:
            @block.sync
            def _(eng):
                eng.dma_start(router_s[:], routerT.rearrange("(h p) e -> p h e", p=128)).then_inc(D["w"], 16)
                eng.wait_ge(D["w"], 16)

            @block.gpsimd
            def _(eng):
                eng.memset(ones_s[:], 1.0)
                eng.memset(before[:], 1.0).then_inc(D["set"], 1)
                eng.iota(iota_i[:, 0:E0], pattern=[[-1, E0]], base=E0, channel_multiplier=0).then_inc(D["set"], 1)
                eng.wait_ge(D["set"], 2)
                eng.affine_select(out=before[:], in_=before[:], compare_op=ALU.is_ge, fill=0.0, base=-1,
                                  pattern=[[1, SUB]], channel_multiplier=-1)
                eng.tensor_copy(rev[:], iota_i[:, 0:E0])

            @block.vector
            def _(eng):
                eng.memset(seen[:], 0.0)

        with nc.Block() as block:
            @block.sync
            def _(eng):
                def front(k, t, n, u):
                    if k == 0:
                        wait(eng, D["vst"], t - 1)
                        dma_x(eng, t, n, u, dn.dev, t - 1, d_ld)

                def back(k, t, n, u):
                    if k == 4:
                        wait(eng, D["ev"], t * NSUB + NSUB)
                        dst = xn_d.ap().rearrange("(t s p) c -> t p s c", p=SUB, s=NSUB)[at_chunk(t)][0]
                        eng.dma_start(dst, xnb[:, u]).then_inc(d_xst[u], 16)
                staged(eng, front, back)
                for u in range(2):
                    eng.wait_ge(d_xst[u], T // 2 * 16)

            @block.vector
            def _(eng):
                def front(k, t, n, u):
                    ts = at_chunk(t)
                    if k == 0:
                        wait_alone(eng, D["lgd"], t - 1)
                        for h in range(2):
                            m = eng.scalar_tensor_tensor(out=vv[:, u, h], in0=OUT[:, h, ts].squeeze(1), scalar=bns[:, h:h + 1],
                                                         in1=V[:, h, ts].squeeze(1), op0=ALU.mult, op1=ALU.add)
                        m.then_inc(D["pre"], 1)
                    if k == 1:
                        wait(eng, d_ld[u], (n + 1) * 32)
                        wait(eng, D["relu"], t + 1)
                        eng.tensor_tensor(xs[:, u], xs[:, u], vv[:, u], ALU.add).then_inc(D["x1"], 1)
                    if k == 2:
                        dn.dve_dev(eng, t, xs[:, u], vv[:, u])
                    if k == 3:
                        dn.dve_norm(eng, t, vv[:, u], vv[:, u]).then_inc(dn.done, 1)

                def back(k, t, n, u):
                    if k not in (4, 5, 6):
                        return
                    count = [{4: 0, 5: 13, 6: 15}[k]]

                    def step(ins):
                        ins.then_inc(D["rt"], 1)
                        count[0] += 1
                        wait_alone(eng, D["rt"], t * RT + count[0])
                    L = lambda i: lg[:, i]
                    many = lambda i: sc_[:, i].unsqueeze(2).to_broadcast([SUB, NSUB, E0])
                    revb = rev[:].unsqueeze(1).to_broadcast([SUB, NSUB, E0])
                    if k == 4:
                        wait(eng, D["lgd"], t + 1)
                        step(eng.tensor_copy(L(LG), psN[0:SUB, 0, 0:NSUB * E0].rearrange("p (s e) -> p s e", s=NSUB)))
                        src = LG
                        for j, mask in ((0, M1), (1, M2)):
                            step(eng.tensor_reduce(sc_[:, j], L(src), AX.X, ALU.max))
                            step(eng.tensor_tensor(L(EQ), L(src), many(j), ALU.is_equal))
                            step(eng.tensor_tensor(L(EQ), L(EQ), revb, ALU.mult))
                            mk = MK[:, j, at_chunk(t, NSUB)]
                            step(eng.tensor_reduce(sc_[:, 2 + j], L(EQ), AX.X, ALU.max))
                            eng.tensor_copy(mk, sc_[:, 2 + j])
                            if j == 0:
                                step(eng.tensor_tensor(L(M1), L(EQ), many(2), ALU.is_equal))
                                eng.tensor_tensor(L(DL), L(LG), many(0), ALU.subtract)
                                step(eng.scalar_tensor_tensor(out=L(LG2), in0=L(M1), scalar=NEG, in1=L(LG), op0=ALU.mult,
                                                              op1=ALU.add))
                                src = LG2
                        eng.tensor_tensor(L(M2), L(EQ), many(3), ALU.is_equal).then_inc(D["rt"], 1)
                        assert count[0] == 11
                    if k == 5:
                        wait_alone(eng, D["rt"], t * RT + 12)
                        eng.tensor_tensor(L(MASK), L(M1), L(M2), ALU.add).then_inc(D["rt"], 1)
                        wait_alone(eng, D["exp"], t + 1)
                        eng.tensor_reduce(sc_[:, 4], L(EX), AX.X, ALU.add)
                        step(eng.tensor_tensor(L(TMP), L(EX), L(M2), ALU.mult))
                        eng.reciprocal(sc_[:, 5], sc_[:, 4])
                        step(eng.tensor_reduce(sc_[:, 6], L(TMP), AX.X, ALU.add))
                        eng.tensor_copy(P12[:, at_chunk(t), :, 0].squeeze(1), sc_[:, 5])
                        eng.tensor_tensor(P12[:, at_chunk(t), :, 1].squeeze(1), sc_[:, 6], sc_[:, 5], ALU.mult)
                    if k == 6:
                        wait_alone(eng, D["pfx"], t + 1)
                        pos = psN[0:SUB, 1, 0:NSUB * E0].rearrange("p (s e) -> p s e", s=NSUB)
                        step(eng.tensor_tensor(L(TMP), L(M1), pos, ALU.mult))
                        eng.tensor_reduce(POS[:, 0, at_chunk(t, NSUB)], L(TMP), AX.X, ALU.add)
                        step(eng.tensor_tensor(L(EQ), L(M2), pos, ALU.mult))
                        eng.tensor_reduce(POS[:, 1, at_chunk(t, NSUB)], L(EQ), AX.X, ALU.add)
                        step(eng.tensor_reduce(seen[:, 1], L(MASK).rearrange("p s e -> p e s"), AX.X, ALU.add))
                        step(eng.tensor_tensor(seen[:, 0], seen[:, 0], seen[:, 1], ALU.add))
                        assert count[0] == RT
                staged(eng, front, back)

            @block.scalar
            def _(eng):
                def front(k, t, n, u):
                    if k == 0:
                        wait(eng, D["pre"], t + 1)
                        for h in range(2):
                            m = eng.activation(vv[:, u, h], vv[:, u, h], ACT.Relu, bias=bnb[:, h:h + 1])
                        m.then_inc(D["relu"], 1)
                    if k == 2:
                        wait(eng, dn.var, t)
                        dn.act_square(eng, t, vv[:, u])
                    if k == 3:
                        dn.act_rstd(eng, t)

                def back(k, t, n, u):
                    if k < NSUB:
                        wait(eng, D["tr"], t * NSUB + k + 1)
                        if k == 0:
                            wait(eng, d_xst[u], n * 16)
                        eng.activation(xnb[:, u, k], psS[0:SUB, k % 2, 0:C], ACT.Copy).then_inc(D["ev"], 1)
                    if k == 4:
                        wait(eng, D["rt"], t * RT + 12)
                        eng.activation(lg[:, EX], lg[:, DL], ACT.Exp).then_inc(D["exp"], 1)
                staged(eng, front, back)

            @block.gpsimd
            def _(eng):
                def front(k, t, n, u):
                    if k == 1:
                        wait_alone(eng, D["x1"], t + 1)
                        eng.tensor_copy(V[:, :, at_chunk(t)].rearrange("p h t c -> p h (t c)"),
                                        xs[:, u]).then_inc(D["vst"], 1)
                staged(eng, front, nothing)

            @block.tensor
            def _(eng):
                def front(k, t, n, u):
                    if k == 1:
                        wait(eng, D["x1"], t + 1)
                        wait(eng, dn.log, t)
                        dn.pe_mean(eng, t, xs[:, u])
                    if k == 2:
                        dn.pe_var(eng, t)

                def back(k, t, n, u):
                    if k < NSUB:
                        s = k
                        if s == 0:
                            wait_alone(eng, dn.done, t + 1)
                            wait_alone(eng, D["rt"], t * RT)
                        wait_alone(eng, D["ev"], t * NSUB + s - 1)
                        sub = slice(s * SUB, (s + 1) * SUB)
                        for h in range(2):
                            m = eng.transpose(psS[0:SUB, s % 2, h * 128:(h + 1) * 128], vv[:, u, h, sub], ident[:])
                        m.then_inc(D["tr"], 1)
                        for h in range(2):
                            m = eng.matmul(psN[0:SUB, 0, s * E0:(s + 1) * E0], vv[:, u, h, sub], router_s[:, h],
                                           start=(h == 0), stop=(h == 1))
                        if s == NSUB - 1:
                            m.then_inc(D["lgd"], 1)
                    if k == 5:
                        wait_alone(eng, D["rt"], t * RT + 13)
                        for s in range(NSUB):
                            dst = psN[0:SUB, 1, s * E0:(s + 1) * E0]
                            eng.matmul(dst, before[:], lg[:, MASK, s], start=True, stop=False)
                            for s2 in range(s):
                                eng.matmul(dst, ones_s[:], lg[:, MASK, s2], start=False, stop=False)
                            m = eng.matmul(dst, ones_s[:], seen[:, 0], start=False, stop=True)
                        m.then_inc(D["pfx"], 1)
                staged(eng, front, back)

        flat = OUT.rearrange("p a t c -> p (a t c)")
        NK = B * HW // ROWS + 1
        with nc.Block() as block:
            @block.tensor
            def _(eng):
                eng.matmul(psN[0:SUB, 1, 0:E0], ones_s[:], seen[:, 0], start=True, stop=True).then_inc(D["pfx"], 1)

            @block.gpsimd
            def _(eng):
                eng.iota(iota_i[:, 0:NK], pattern=[[ROWS, NK]], base=0, channel_multiplier=0)
                eng.iota(iota_i[:, NK:NK + TILES], pattern=[[1, TILES]], base=0, channel_multiplier=0).then_inc(D["set"], 1)

            @block.vector
            def _(eng):
                count = [0]

                def step(ins):
                    ins.then_inc(D["mid"], 1)
                    count[0] += 1
                    eng.wait_ge(D["mid"], count[0])
                cnt, tl, base, ends = (flat[0:SUB, 32 * i:32 * i + 32] for i in range(4))
                steps_k = flat[0:SUB, 128:128 + NK + TILES]
                lower = flat[0:SUB, 512:512 + E0 * E0].rearrange("p (a b) -> p a b", a=E0)
                big = flat[0:SUB, 2048:2048 + E0 * TILES]
                bs = flat[0:SUB, 1536:1536 + NT]
                eng.wait_ge(D["pfx"], T + 1)
                eng.wait_ge(D["set"], 3)
                step(eng.tensor_copy(cnt, psN[0:SUB, 1, 0:E0]))
                step(eng.tensor_copy(steps_k, iota_i[:, 0:NK + TILES]))
                b1_ = big[:, 0:E0 * NK].rearrange("p (e k) -> p e k", e=E0)
                step(eng.tensor_tensor(b1_, cnt.unsqueeze(2).to_broadcast([SUB, E0, NK]),
                                       steps_k[:, 0:NK].unsqueeze(1).to_broadcast([SUB, E0, NK]), ALU.is_gt))
                step(eng.tensor_reduce(tl, b1_, AX.X, ALU.add))
                step(eng.tensor_tensor(lower, rev[:].unsqueeze(1).to_broadcast([SUB, E0, E0]),
                                       rev[:].unsqueeze(2).to_broadcast([SUB, E0, E0]), ALU.is_gt))
                step(eng.tensor_tensor(lower, lower, tl.unsqueeze(1).to_broadcast([SUB, E0, E0]), ALU.mult))
                step(eng.tensor_reduce(base, lower, AX.X, ALU.add))
                step(eng.tensor_tensor(ends, base, tl, ALU.add))
                step(eng.tensor_scalar(base, base, float(ROWS), None, ALU.mult))
                b2_ = big.rearrange("p (t e) -> p t e", e=E0)
                step(eng.tensor_tensor(b2_, ends.unsqueeze(1).to_broadcast([SUB, TILES, E0]),
                                       steps_k[:, NK:NK + TILES].unsqueeze(2).to_broadcast([SUB, TILES, E0]), ALU.is_le))
                te = steps_k[:, 0:TILES]
                step(eng.tensor_reduce(te, b2_, AX.X, ALU.add))
                step(eng.tensor_scalar(te, te, float(E0 - 1), None, ALU.min))
                step(eng.tensor_copy(EID[:], te))
                b3_ = big[:, 0:NT * E0].rearrange("p (t e) -> p t e", e=E0)
                for j in range(2):
                    step(eng.tensor_tensor(b3_, rev[:].unsqueeze(1).to_broadcast([SUB, NT, E0]),
                                           MK[:, j].unsqueeze(2).to_broadcast([SUB, NT, E0]), ALU.is_equal))
                    step(eng.tensor_tensor(b3_, b3_, base.unsqueeze(1).to_broadcast([SUB, NT, E0]), ALU.mult))
                    step(eng.tensor_reduce(bs, b3_, AX.X, ALU.add))
                    step(eng.tensor_tensor(bs, bs, POS[:, j], ALU.add))
                    step(eng.tensor_copy(SLOT[:].rearrange("p t s j -> p (t s) j")[:, :, j], bs))

        G = {k: sem(f"g_{k}") for k in ("z", "zf", "ix", "ix2")}
        g_ld = [sem(f"g_ld{u}") for u in range(2)]
        g_sc = [sem(f"g_sc{u}") for u in range(2)]
        ZF = TILES * ROWS * C // (4 * 128)
        idx = sbd("idx", [SUB, 2, NSUB * 2], U32)
        pc = sbd("pc", [SUB, 2, NSUB * 2])
        with nc.Block() as block:
            @block.vector
            def _(eng):
                eng.memset(flat[:, 0:ZF], 0.0).then_inc(G["z"], 1)

                def front(k, t, n, u):
                    if k == 0:
                        wait_alone(eng, g_sc[u], n * 16 * NSUB * 2)
                        eng.tensor_copy(idx[:, u], SLOT[:, at_chunk(t)].rearrange("p t s j -> p (t s j)")).then_inc(G["ix"], 1)
                staged(eng, front, nothing, slots=1)

            @block.sync
            def _(eng):
                eng.wait_ge(G["z"], 1)
                all_xg = xg_d.ap().rearrange("r c -> (r c)").rearrange("(q p f) -> q p f", q=4, p=128)
                for q in range(4):
                    eng.dma_start(all_xg[q], flat[:, 0:ZF]).then_inc(G["zf"], 16)

                def front(k, t, n, u):
                    if k == 0:
                        wait(eng, g_sc[u], n * 16 * NSUB * 2)
                        src = xn_d.ap().rearrange("(t s p) c -> t p s c", p=SUB, s=NSUB)[at_chunk(t)][0]
                        eng.dma_start(xnb[:, u], src).then_inc(g_ld[u], 16)
                staged(eng, front, nothing, slots=1)
                eng.wait_ge(G["zf"], 64)
                for q in range(16):
                    eng.dma_start(w_moe_s[:].rearrange("p (e h c) -> p e h c", e=E0, h=2)[:, 2 * q:2 * q + 2],
                                  w_moe[2 * q:2 * q + 2].rearrange("e (h p) c -> p e h c", p=128)).then_inc(D["w"], 16)
                eng.wait_ge(D["w"], 17 * 16)

            @block.gpsimd
            def _(eng):
                eng.wait_ge(G["zf"], 64)

                def front(k, t, n, u):
                    if k == 0:
                        wait_alone(eng, G["ix"], t + 1)
                        wait_alone(eng, g_ld[u], (n + 1) * 16)
                        for s in range(NSUB):
                            for j in range(2):
                                eng.indirect_dma_start(
                                    xg_d.ap(), bass.IndirectOffsetOnAxis(ap=idx[:, u, 2 * s + j:2 * s + j + 1], axis=0),
                                    xnb[:, u, s], None).then_inc(g_sc[u], 16)
                staged(eng, front, nothing, slots=1)
                for u in range(2):
                    eng.wait_ge(g_sc[u], T // 2 * 16 * NSUB * 2)

        X = {k: sem(f"x_{k}") for k in ("tr", "ev", "mm", "y")}
        x_ld = [sem(f"x_ld{u}") for u in range(2)]
        x_st = [sem(f"x_st{u}") for u in range(2)]
        xr = vv[:].rearrange("p u h c -> p u (h c)")[:, :, 0:C]
        xt = xs[:].rearrange("p u h c -> p u (h c)")[:, :, 0:C]
        yr = ex[:, :, 0:C]
        with nc.Block() as block:
            @block.sync
            def _(eng):
                def front(k, t, n, u):
                    wait(eng, X["tr"], t - 1)
                    eng.dma_start(xr[:, u], xg_d.ap()[at_chunk(t, ROWS)]).then_inc(x_ld[u], 16)
                staged(eng, front, nothing, TILES, 1)

            @block.tensor
            def _(eng):
                def front(k, t, n, u):
                    wait_alone(eng, x_ld[u], (n + 1) * 16)
                    wait_alone(eng, X["ev"], t - 1)
                    for h in range(2):
                        m = eng.transpose(psS[:, u, h * 128:(h + 1) * 128], xr[:, u, h * 128:(h + 1) * 128], ident[:])
                    m.then_inc(X["tr"], 1)

                def back(k, t, n, u):
                    e = eng.value_load(EID[0:1, at_chunk(t)], min_val=0, max_val=E0 - 1)
                    wait(eng, X["ev"], t + 1)
                    wait(eng, X["y"], t - 1)
                    for h in range(2):
                        m = eng.matmul(psZ[:, u, 0:C], xt[:, u, h * 128:(h + 1) * 128],
                                       w_moe_s[:, bass.ds(e * (2 * C) + h * C, C)], start=(h == 0), stop=(h == 1))
                    m.then_inc(X["mm"], 1)
                staged(eng, front, back, TILES, 1)

            @block.scalar
            def _(eng):
                def front(k, t, n, u):
                    wait(eng, X["tr"], t + 1)
                    wait(eng, X["mm"], t - 1)
                    eng.activation(xt[:, u], psS[:, u, 0:C], ACT.Copy).then_inc(X["ev"], 1)
                staged(eng, front, nothing, TILES, 1)

            @block.vector
            def _(eng):
                def back(k, t, n, u):
                    wait(eng, X["mm"], t + 1)
                    wait(eng, x_st[u], n * 16)
                    eng.tensor_copy(yr[:, u], psZ[:, u, 0:C]).then_inc(X["y"], 1)
                staged(eng, nothing, back, TILES, 1)

            @block.gpsimd
            def _(eng):
                def back(k, t, n, u):
                    wait(eng, X["y"], t + 1)
                    eng.dma_start(yg_d.ap()[at_chunk(t, ROWS)], yr[:, u]).then_inc(x_st[u], 16)
                staged(eng, nothing, back, TILES, 1)
                for u in range(2):
                    eng.wait_ge(x_st[u], TILES // 2 * 16)

        gn = Norm("h", eps_c)
        H = {k: sem(f"h_{k}") for k in ("ix", "y0", "y", "tr", "x2", "vst", "sum")}
        h_g = [sem(f"h_g{u}") for u in range(2)]
        gath = sbd("gath", [SUB, 2, NSUB * 2, C])
        yn = xnb
        with nc.Block() as block:
            @block.gpsimd
            def _(eng):
                def front(k, t, n, u):
                    if k == 0:
                        wait_alone(eng, H["ix"], t + 1)
                        wait_alone(eng, H["y"], t - 1)
                        for s in range(NSUB):
                            for j in range(2):
                                i = 2 * s + j
                                eng.indirect_dma_start(gath[:, u, i], None, yg_d.ap(),
                                                       bass.IndirectOffsetOnAxis(ap=idx[:, u, i:i + 1], axis=0)).then_inc(h_g[u], 16)

                def back(k, t, n, u):
                    if k == 2:
                        wait_alone(eng, H["x2"], t + 1)
                        eng.tensor_copy(V[:, :, at_chunk(t)].rearrange("p h t c -> p h (t c)"), xs[:, u]).then_inc(H["vst"], 1)
                    if k == 5:
                        wait_alone(eng, gn.done, t + 1)
                        eng.tensor_copy(OUT[:, :, at_chunk(t)].rearrange("p h t c -> p h (t c)"), vv[:, u]).then_inc(H["vst"], 1)
                staged(eng, front, back)

            @block.vector
            def _(eng):
                def front(k, t, n, u):
                    if k == 0:
                        wait_alone(eng, h_g[u], n * 16 * NSUB * 2)
                        eng.tensor_copy(idx[:, u], SLOT[:, at_chunk(t)].rearrange("p t s j -> p (t s j)")).then_inc(H["ix"], 1)
                        eng.tensor_copy(pc[:, u], P12[:, at_chunk(t)].rearrange("p t s j -> p (t s j)")).then_inc(H["y0"], 1)
                    if k == 9:
                        wait(eng, h_g[u], (n + 1) * 16 * NSUB * 2)
                        wait(eng, H["y0"], t * 2 + 1)
                        wait(eng, H["tr"], t - 1)
                        for s in range(NSUB):
                            m = eng.tensor_scalar(yn[:, u, s], gath[:, u, 2 * s], pc[:, u, 2 * s:2 * s + 1], None, ALU.mult)
                        m.then_inc(H["y0"], 1)
                        wait(eng, H["y0"], t * 2 + 2)
                        for s in range(NSUB):
                            m = eng.scalar_tensor_tensor(out=yn[:, u, s], in0=gath[:, u, 2 * s + 1],
                                                         scalar=pc[:, u, 2 * s + 1:2 * s + 2], in1=yn[:, u, s],
                                                         op0=ALU.mult, op1=ALU.add)
                        m.then_inc(H["y"], 1)

                def back(k, t, n, u):
                    if k == 1:
                        wait_alone(eng, H["tr"], t + 1)
                        wait_alone(eng, H["vst"], t * 2 - 2)
                        eng.tensor_tensor(xs[:, u], V[:, :, at_chunk(t)].rearrange("p h t c -> p h (t c)"),
                                          psN[:, :, 0:CH], ALU.add).then_inc(H["x2"], 1)
                    if k == 3:
                        gn.dve_dev(eng, t, xs[:, u], vv[:, u])
                    if k == 4:
                        gn.dve_norm(eng, t, vv[:, u], vv[:, u]).then_inc(gn.done, 1)
                        wait_alone(eng, gn.done, t + 1)
                        eng.tensor_reduce(YS[:, at_chunk(t)].rearrange("p t h b -> p (t h b)"),
                                          vv[:, u].rearrange("p h (b w) -> p (h b) w", b=IMGS), AX.X, ALU.add)
                staged(eng, front, back)

            @block.scalar
            def _(eng):
                def back(k, t, n, u):
                    if k == 3:
                        wait(eng, gn.var, t)
                        gn.act_square(eng, t, vv[:, u])
                    if k == 4:
                        gn.act_rstd(eng, t)
                staged(eng, nothing, back)

            @block.tensor
            def _(eng):
                def back(k, t, n, u):
                    if k == 0:
                        wait_alone(eng, H["y"], t + 1)
                        wait_alone(eng, H["x2"], t)
                        for s in range(NSUB):
                            for h in range(2):
                                m = eng.transpose(psN[:, h, s * SUB:(s + 1) * SUB], yn[:, u, s, h * 128:(h + 1) * 128],
                                                  ident[0:SUB, 0:SUB])
                        m.then_inc(H["tr"], 1)
                    if k == 2:
                        wait(eng, H["x2"], t + 1)
                        wait(eng, gn.log, t)
                        gn.pe_mean(eng, t, xs[:, u])
                    if k == 3:
                        gn.pe_var(eng, t)
                staged(eng, nothing, back)
        d_ctx.close()

        SE_E, SE_R = 8, 16
        SC = sb("SC", [128, T, 2, IMGS])
        s_se = {k: sem(f"se_{k}") for k in ("w", "dve", "pe", "act")}
        with ExitStack() as c3:
            def sb3(name, shape):
                return c3.enter_context(nc.sbuf_tensor(name, shape, F32))
            w1t = sb3("w1t", [128, 2, 128])
            wgt = sb3("wgt", [128, 2, SE_E])
            w2t = sb3("w2t", [128, C])
            b1t = sb3("b1t", [128, 1])
            b2t = sb3("b2t", [SE_E, C])
            bgt = sb3("bgt", [B, SE_E])
            ym = sb3("ym", [128, 2, B])
            hid = sb3("hid", [128, B])
            gate = sb3("gate", [B, 3, SE_E])
            gs = sb3("gs", [B, 3])
            gT = sb3("gT", [SE_E, B])
            gB = sb3("gB", [128, B])
            sg = sb3("sg", [128, 2, B])
            with nc.Block() as block:
                @block.sync
                def _(eng):
                    eng.dma_start(w1t[:], se_w1T.rearrange("(h p) e -> p h e", p=128)).then_inc(s_se["w"], 16)
                    eng.dma_start(wgt[:], se_wgT.rearrange("(h p) e -> p h e", p=128)).then_inc(s_se["w"], 16)
                    eng.dma_start(w2t[:], se_w2T).then_inc(s_se["w"], 16)
                    eng.dma_start(b1t[:], se_b1).then_inc(s_se["w"], 16)
                    eng.dma_start(b2t[:], se_b2).then_inc(s_se["w"], 16)
                    eng.dma_start(bgt[:], se_bg.partition_broadcast(B)).then_inc(s_se["w"], 16)
                    eng.wait_ge(s_se["w"], 96)

                @block.vector
                def _(eng):
                    count = [0]

                    def step(ins):
                        ins.then_inc(s_se["dve"], 1)
                        count[0] += 1
                        eng.wait_ge(s_se["dve"], count[0])
                    step(eng.tensor_scalar(ym[:].rearrange("p h (t b) -> p h t b", b=IMGS),
                                           YS[:].rearrange("p t h b -> p h t b"), 1.0 / HW, None, ALU.mult))
                    eng.wait_ge(s_se["w"], 96)
                    eng.wait_ge(s_se["pe"], 1)
                    step(eng.tensor_tensor(gate[:, 0], psM[0:B, 0:SE_E], bgt[:], ALU.add))
                    step(eng.tensor_reduce(gs[:, 0:1], gate[:, 0], AX.X, ALU.max, negate=True))
                    eng.wait_ge(s_se["act"], 1)
                    step(eng.reciprocal(gs[:, 2:3], gs[:, 1:2]))
                    step(eng.tensor_scalar(gate[:, 2], gate[:, 1], gs[:, 2:3], None, ALU.mult))
                    eng.wait_ge(s_se["pe"], 3)
                    step(eng.tensor_copy(gT[:], psM[0:SE_E, 64:64 + B]))
                    eng.wait_ge(s_se["pe"], 4)
                    eng.wait_ge(s_se["act"], 2)
                    step(eng.tensor_tensor(hid[:], hid[:], psM[:, 128:128 + B], ALU.mult))
                    eng.wait_ge(s_se["act"], 4)
                    step(eng.tensor_scalar(sg[:], sg[:], 1.0, None, ALU.add))
                    step(eng.reciprocal(SC[:].rearrange("p t h b -> p h t b"),
                                        sg[:].rearrange("p h (t b) -> p h t b", b=IMGS)))

                @block.tensor
                def _(eng):
                    eng.wait_ge(s_se["w"], 96)
                    eng.wait_ge(s_se["dve"], 1)
                    for h in range(2):
                        m = eng.matmul(psM[0:B, 0:SE_E], ym[:, h], wgt[:, h], start=(h == 0), stop=(h == 1))
                    m.then_inc(s_se["pe"], 1)
                    for h in range(2):
                        m = eng.matmul(psO[:, 0:B], w1t[:, h], ym[:, h], start=(h == 0), stop=(h == 1))
                    m.then_inc(s_se["pe"], 1)
                    eng.wait_ge(s_se["dve"], 5)
                    eng.transpose(psM[0:SE_E, 64:64 + B], gate[:, 2], ident[0:B, 0:B]).then_inc(s_se["pe"], 1)
                    eng.wait_ge(s_se["dve"], 6)
                    eng.matmul(psM[:, 128:128 + B], ind[0:SE_E, 0:128], gT[:], start=True, stop=True).then_inc(s_se["pe"], 1)
                    eng.wait_ge(s_se["dve"], 7)
                    for h in range(2):
                        dst = psZ[:, h, 0:B]
                        eng.matmul(dst, w2t[:, h * 128:(h + 1) * 128], hid[:], start=True, stop=False)
                        m = eng.matmul(dst, b2t[:, h * 128:(h + 1) * 128], gT[:], start=False, stop=True)
                    m.then_inc(s_se["pe"], 1)

                @block.scalar
                def _(eng):
                    eng.wait_ge(s_se["dve"], 3)
                    eng.activation(gate[:, 1], gate[:, 0], ACT.Exp, bias=gs[:, 0:1], accum_out=gs[:, 1:2]).then_inc(s_se["act"], 1)
                    eng.wait_ge(s_se["pe"], 2)
                    eng.wait_ge(s_se["w"], 96)
                    eng.activation(hid[:], psO[:, 0:B], ACT.Relu, bias=b1t[:, 0:1]).then_inc(s_se["act"], 1)
                    eng.wait_ge(s_se["pe"], 5)
                    for h in range(2):
                        eng.activation(sg[:, h], psZ[:, h, 0:B], ACT.Exp, scale=-1.0).then_inc(s_se["act"], 1)

        hs_d = nc.dram_tensor("hs_d", [T, C, CH], F32)
        wt_d = nc.dram_tensor("wt_d", [T, NH * NE, CH], F32)
        HE = NH * NE
        f_ctx = phase()

        def sbf(name, shape, dt=F32):
            return f_ctx.enter_context(nc.sbuf_tensor(name, shape, dt))
        wm_s = sbf("wm_s", [128, 2, C])
        bm_s = sbf("bm_s", [128, 2])
        embd = sbf("embd", [128, 4, NE])
        hs = BIG[:, 2 * T * CH:2 * T * CH + 4 * CH].rearrange("p (u h c) -> p u h c", u=2, h=2)
        wts = sbf("wts", [128, 2, CH])
        rt = sbf("rt", [SUB, 9, NSUB * NH, NE])
        rs16 = sbf("rs16", [SUB, 7, NSUB * NH])
        rev16 = sbf("rev16", [SUB, NE])
        rev_i = sbf("rev_i", [SUB, NE], U32)
        fn = Norm("f", eps_t)
        FD = {k: sem(f"f_{k}") for k in ("w", "set", "x3", "vst", "lin", "hs", "lgd", "rt", "exp", "tr", "wt")}
        f_hst = [sem(f"f_hst{u}") for u in range(2)]
        f_wst = [sem(f"f_wst{u}") for u in range(2)]
        FR = 17
        with nc.Block() as block:
            @block.sync
            def _(eng):
                eng.dma_start(wm_s[:], wm.rearrange("(h p) e -> p h e", p=128)).then_inc(FD["w"], 16)
                eng.dma_start(bm_s[:], bm).then_inc(FD["w"], 16)
                eng.wait_ge(FD["set"], 1)
                for q in range(4):
                    eng.dma_start(embd[32 * q:32 * q + 32, q], emb).then_inc(FD["w"], 16)
                eng.wait_ge(FD["w"], 96)

            @block.gpsimd
            def _(eng):
                eng.memset(embd[:], 0.0).then_inc(FD["set"], 1)
                eng.iota(rev_i[:], pattern=[[-1, NE]], base=NE, channel_multiplier=0).then_inc(FD["set"], 1)
                eng.wait_ge(FD["set"], 2)
                eng.tensor_copy(rev16[:], rev_i[:])

        with nc.Block() as block:
            @block.vector
            def _(eng):
                def front(k, t, n, u):
                    if k == 0:
                        wait_alone(eng, FD["vst"], t - 1)
                        for h in range(2):
                            for b in range(IMGS):
                                w_ = slice(b * HW, (b + 1) * HW)
                                m = eng.scalar_tensor_tensor(
                                    out=xs[:, u, h, w_], in0=OUT[:, h, at_chunk(t), w_].squeeze(1),
                                    scalar=SC[:, at_chunk(t), h, b], in1=V[:, h, at_chunk(t), w_].squeeze(1),
                                    op0=ALU.mult, op1=ALU.add)
                        m.then_inc(FD["x3"], 1)
                    if k == 1:
                        wait(eng, FD["lin"], t - 1)
                        fn.dve_dev(eng, t, xs[:, u], vv[:, u])
                    if k == 2:
                        fn.dve_norm(eng, t, vv[:, u], vv[:, u]).then_inc(fn.done, 1)

                def back(k, t, n, u):
                    if k not in (4, 5):
                        return
                    count = [{4: 0, 5: 13}[k]]

                    def step(ins):
                        ins.then_inc(FD["rt"], 1)
                        count[0] += 1
                        wait_alone(eng, FD["rt"], t * FR + count[0])
                    L = lambda i: rt[:, i]
                    many = lambda i: rs16[:, i].unsqueeze(2).to_broadcast([SUB, NSUB * NH, NE])
                    revb = rev16[:].unsqueeze(1).to_broadcast([SUB, NSUB * NH, NE])
                    LG, EQ, M1, LG2, M2, MASK, DL, EX, TMP = range(9)
                    if k == 4:
                        wait(eng, FD["lgd"], t + 1)
                        step(eng.tensor_copy(L(LG), psN[0:SUB, 0].rearrange("p (s e) -> p s e", e=NE)))
                        src = LG
                        for j, mask in ((0, M1), (1, M2)):
                            step(eng.tensor_reduce(rs16[:, j], L(src), AX.X, ALU.max))
                            step(eng.tensor_tensor(L(EQ), L(src), many(j), ALU.is_equal))
                            step(eng.tensor_tensor(L(EQ), L(EQ), revb, ALU.mult))
                            step(eng.tensor_reduce(rs16[:, 2 + j], L(EQ), AX.X, ALU.max))
                            if j == 0:
                                step(eng.tensor_tensor(L(M1), L(EQ), many(2), ALU.is_equal))
                                eng.tensor_tensor(L(DL), L(LG), many(0), ALU.subtract)
                                step(eng.scalar_tensor_tensor(out=L(LG2), in0=L(M1), scalar=NEG, in1=L(LG), op0=ALU.mult,
                                                              op1=ALU.add))
                                src = LG2
                        step(eng.tensor_tensor(L(M2), L(EQ), many(3), ALU.is_equal))
                        step(eng.tensor_tensor(L(MASK), L(M1), L(M2), ALU.add))
                        assert count[0] == 13
                    if k == 5:
                        wait_alone(eng, FD["exp"], t + 1)
                        step(eng.tensor_reduce(rs16[:, 4], L(EX), AX.X, ALU.add))
                        step(eng.reciprocal(rs16[:, 5], rs16[:, 4]))
                        step(eng.tensor_tensor(L(TMP), L(EX), L(MASK), ALU.mult))
                        step(eng.tensor_tensor(L(EQ), L(TMP), many(5), ALU.mult))
                        assert count[0] == FR
                staged(eng, front, back)

            @block.gpsimd
            def _(eng):
                def front(k, t, n, u):
                    if k == 1:
                        wait_alone(eng, FD["x3"], t + 1)
                        eng.tensor_copy(V[:, :, at_chunk(t)].rearrange("p h t c -> p h (t c)"), xs[:, u]).then_inc(FD["vst"], 1)
                staged(eng, front, nothing)

            @block.sync
            def _(eng):
                def back(k, t, n, u):
                    if k == 1:
                        wait(eng, FD["hs"], t + 1)
                        eng.dma_start(hs_d.ap()[at_chunk(t)][0].rearrange("(h p) c -> p h c", h=2),
                                      hs[:, u]).then_inc(f_hst[u], 16)
                    if k == 7:
                        wait(eng, FD["wt"], t + 1)
                        eng.dma_start(wt_d.ap()[at_chunk(t)][0], wts[:, u]).then_inc(f_wst[u], 16)
                staged(eng, nothing, back)
                for u in range(2):
                    eng.wait_ge(f_hst[u], T // 2 * 16)
                    eng.wait_ge(f_wst[u], T // 2 * 16)

            @block.scalar
            def _(eng):
                def front(k, t, n, u):
                    if k == 1:
                        wait(eng, fn.var, t)
                        fn.act_square(eng, t, vv[:, u])
                    if k == 2:
                        fn.act_rstd(eng, t)

                def back(k, t, n, u):
                    if k == 0:
                        wait(eng, FD["lin"], t + 1)
                        wait_alone(eng, f_hst[u], n * 16)
                        wait_alone(eng, FD["lgd"], t - 1)
                        for m_ in range(2):
                            m = eng.activation(hs[:, u, m_], psS[:, m_, 0:CH], ACT.Identity, bias=bm_s[:, m_:m_ + 1])
                        m.then_inc(FD["hs"], 1)
                    if k == 4:
                        wait(eng, FD["rt"], t * FR + 7)
                        eng.activation(rt[:, 7], rt[:, 6], ACT.Exp).then_inc(FD["exp"], 1)
                    if k == 6:
                        wait_alone(eng, FD["tr"], t + 1)
                        wait_alone(eng, f_wst[u], n * 16)
                        eng.activation(wts[:, u], psO[:, 0:CH], ACT.Copy).then_inc(FD["wt"], 1)
                staged(eng, front, back)

            @block.tensor
            def _(eng):
                def front(k, t, n, u):
                    if k == 1:
                        wait(eng, FD["x3"], t + 1)
                        wait(eng, fn.log, t)
                        fn.pe_mean(eng, t, xs[:, u])
                        fn.pe_var(eng, t)

                def back(k, t, n, u):
                    if k == 0:
                        wait(eng, fn.done, t + 1)
                        wait(eng, FD["hs"], t)
                        for m_ in range(2):
                            for h in range(2):
                                m = eng.matmul(psS[:, m_, 0:CH], wm_s[:, h, m_ * 128:(m_ + 1) * 128], vv[:, u, h],
                                               start=(h == 0), stop=(h == 1))
                        m.then_inc(FD["lin"], 1)
                    if k == 3:
                        wait_alone(eng, FD["hs"], t + 1)
                        wait_alone(eng, FD["rt"], t * FR)
                        for s in range(NSUB):
                            for m_ in range(2):
                                dst = psN[0:SUB, 0, s * HE + m_ * 64:s * HE + m_ * 64 + 64]
                                m = eng.matmul(dst, hs[:, u, m_, s * SUB:(s + 1) * SUB],
                                               embd[:].rearrange("p a e -> p (a e)"), start=True, stop=True)
                        m.then_inc(FD["lgd"], 1)
                    if k == 6:
                        wait_alone(eng, FD["rt"], t * FR + FR)
                        wait_alone(eng, FD["wt"], t)
                        for s in range(NSUB):
                            m = eng.transpose(psO[:, s * SUB:(s + 1) * SUB],
                                              rt[:, 1, s * NH:(s + 1) * NH].rearrange("p h e -> p (h e)"), ident[0:SUB, 0:SUB])
                        m.then_inc(FD["tr"], 1)
                staged(eng, front, back)
        f_ctx.close()

        NI, NP, NS = 8, 16, 64
        w1_s = BIG[:, 0:NE * HID].rearrange("p (e i) -> p e i", e=NE)
        w1_r = sb("w1_r", [128, NE, HID], F32R)
        w2_s = sb("w2_s", [HID, NE, HD])
        b1_s = sb("b1_s", [HID, NE])
        b2_s = sb("b2_s", [128, 4])
        wo_s = sb("wo_s", [128, 2, C])
        bo_s = sb("bo_s", [128, 2])
        foldm = sb("fold", [128, HD])
        x_r = sb("x_r", [128, 2, 4, CH], F32R)
        stk = BIG[:, 0:8 * CH].rearrange("p (a q c) -> p a q c", a=2, q=4)
        wb = BIG[:, 8 * CH:16 * CH].rearrange("p (a q c) -> p a q c", a=2, q=4)
        gsum = BIG[:, 16 * CH:24 * CH].rearrange("p (a q c) -> p a q c", a=2, q=4)
        comb = BIG[:, 24 * CH:26 * CH].rearrange("p (a c) -> p a c", a=2)
        fin = BIG[:, 26 * CH:28 * CH].rearrange("p (a c) -> p a c", a=2)
        hid = [xs[:, 0], xs[:, 1], vv[:, 0], vv[:, 1], ex[:], at[:], rz[:], sq[:]]
        Q = {k: sem(f"q_{k}") for k in ("w", "set", "hi", "lo", "mm1", "gel", "mm2", "gs", "fold", "comb",
                                        "wo", "fin")}
        q_stk = [sem(f"q_stk{a}") for a in range(2)]
        q_wb = [sem(f"q_wb{a}") for a in range(2)]
        q_st = [sem(f"q_st{a}") for a in range(2)]
        psA, psY, psW, psF = (psN, psS), psZ, psM, psO

        def chunks(eng, body, tail):
            body(0)
            with eng.Fori(1, T) as t:
                body(t)
            tail(T)

        with nc.Block() as block:
            @block.sync
            def _(eng):
                for q in range(4):
                    eng.dma_start(w1_s[32 * q:32 * q + 32], w1).then_inc(Q["w"], 16)
                eng.dma_start(w2_s[:], w2).then_inc(Q["w"], 16)
                eng.dma_start(b1_s[:], b1).then_inc(Q["w"], 16)
                eng.dma_start(b2_s[:], b2).then_inc(Q["w"], 16)
                eng.dma_start(wo_s[:], wo.rearrange("(h p) e -> p h e", p=128)).then_inc(Q["w"], 16)
                eng.dma_start(bo_s[:], bo).then_inc(Q["w"], 16)
                eng.wait_ge(Q["w"], 9 * 16)

            @block.gpsimd
            def _(eng):
                eng.memset(foldm[:], 0.0).then_inc(Q["set"], 1)
                for r in range(4):
                    eng.wait_ge(Q["set"], r + 1)
                    eng.affine_select(out=foldm[:], in_=foldm[:], compare_op=ALU.not_equal, fill=1.0,
                                      base=-32 * r, pattern=[[-1, HD]], channel_multiplier=1).then_inc(Q["set"], 1)

            @block.vector
            def _(eng):
                eng.wait_ge(Q["w"], 9 * 16)
                eng.tensor_copy(w1_r[:], w1_s[:]).then_inc(Q["hi"], 1)
                eng.wait_ge(Q["hi"], 1)
                for row in (32, 96):
                    rows = slice(row, row + 32)
                    eng.tensor_tensor(w1_r[rows], w1_s[rows], w1_r[rows].bitcast(F32), ALU.subtract)

            @block.scalar
            def _(eng):
                eng.preload_act_table_set("gelu_and_others")

        with nc.Block() as block:
            @block.sync
            def _(eng):
                def store(t):
                    for m_ in range(2):
                        wait(eng, Q["fin"], t * 2 - 1 + m_)
                        eng.dma_start(out_v[at_chunk(t - 1)][0, :, m_],
                                      fin[:, m_].rearrange("p (b w) -> p b w", b=IMGS)).then_inc(q_st[m_], 16)

                def body(t):
                    for it in range(NI):
                        half, group = it // 4, it % 4
                        if group == 0:
                            wait(eng, Q["lo"], 2 * t + half - 1)
                            for r in range(4):
                                eng.dma_start(stk[32 * r:32 * r + 32, half],
                                              hs_d.ap()[at_chunk(t)][0, half * 128:half * 128 + 128].rearrange(
                                                  "(q p) c -> p q c", q=4)).then_inc(q_stk[half], 16)
                        wait(eng, Q["gs"], (t * NI + it - 1) * 4)
                        for e in range(4):
                            src = wt_d.ap()[at_chunk(t)][0].rearrange("(h e) c -> e h c", h=NH)[group * 4 + e]
                            eng.dma_start(wb[32 * e:32 * e + 32, it % 2],
                                          src[half * 4:half * 4 + 4].partition_broadcast(32)).then_inc(q_wb[it % 2], 16)
                        if it == 4 and not (isinstance(t, int) and t == 0):
                            store(t)
                chunks(eng, body, store)
                for m_ in range(2):
                    eng.wait_ge(q_st[m_], 16 * T)

            @block.gpsimd
            def _(eng):
                def body(t):
                    for half in range(2):
                        wait_alone(eng, q_stk[half], (t + 1) * 64)
                        wait_alone(eng, Q["mm1"], (2 * t + half - 1) * (NS // 2))
                        eng.tensor_copy(x_r[:, half], stk[:, half]).then_inc(Q["hi"], 1)
                        wait_alone(eng, Q["hi"], 2 * t + half + 2)
                        eng.tensor_tensor(x_r[64:128, half], stk[64:128, half], x_r[64:128, half].bitcast(F32),
                                          ALU.subtract).then_inc(Q["lo"], 1)
                chunks(eng, body, lambda t: None)

            @block.tensor
            def _(eng):
                def second(t, P, hh):
                    if hh == 0:
                        wait_alone(eng, Q["gel"], t * NS + P * 4 + 4)
                    wait_alone(eng, Q["gs"], (t * NP + P) * 2 + hh - 1)
                    for e in range(4):
                        mm = eng.matmul(psY[32 * e:32 * e + 32, hh, 0:CH], w2_s[:, (P // 2 % 4) * 4 + e],
                                        hid[(P % 2) * 4 + e][:, hh], start=True, stop=True,
                                        tile_position=(0, 32 * e))
                    mm.then_inc(Q["mm2"], 1)

                def fold(t, it):
                    group = it % 4
                    wait_alone(eng, Q["gs"], (t * NI + it) * 4 + 4)
                    if group == 0:
                        wait_alone(eng, Q["comb"], t * 2 + it // 4)
                    for q in range(4):
                        mm = eng.matmul(psF[32 * q:32 * q + 32, 0:CH], foldm[:], gsum[:, it % 2, q],
                                        start=(group == 0), stop=(group == 3), tile_position=(0, 32 * q))
                    mm.then_inc(Q["fold"], 1)

                def last(t, m_):
                    wait_alone(eng, Q["comb"], t * 2)
                    wait_alone(eng, Q["fin"], t * 2 - 2 + m_)
                    for h in range(2):
                        mm = eng.matmul(psW[:, 0:CH], wo_s[:, h, m_ * 128:(m_ + 1) * 128], comb[:, h],
                                        start=(h == 0), stop=(h == 1))
                    mm.then_inc(Q["wo"], 1)

                def body(t):
                    first = isinstance(t, int) and t == 0
                    for P in range(NP):
                        half, group, pair = P // 8, P // 2 % 4, P % 2
                        if P % 8 == 0:
                            wait_alone(eng, Q["lo"], 2 * t + half + 1)
                        for e in range(4):
                            m = 4 * P + e
                            wait_alone(eng, Q["gel"], t * NS + m - 1)
                            for hh in range(2):
                                mm = eng.matmul(psA[m % 2][:, hh, 0:CH], w1_r[:, group * 4 + e],
                                                x_r[:, half, pair * 2 + hh], start=True, stop=True)
                            mm.then_inc(Q["mm1"], 1)
                            if e in (1, 2):
                                if P > 0:
                                    second(t, P - 1, e - 1)
                                elif not first:
                                    second(t - 1, NP - 1, e - 1)
                        if P >= 3 and P % 2:
                            fold(t, (P - 3) // 2)
                        if P == 1 and not first:
                            fold(t - 1, NI - 1)
                        if P in (3, 5) and not first:
                            last(t, (P - 3) // 2)

                def tail(t):
                    for hh in range(2):
                        second(t - 1, NP - 1, hh)
                    fold(t - 1, NI - 1)
                    for m_ in range(2):
                        last(t, m_)
                chunks(eng, body, tail)

            @block.scalar
            def _(eng):
                def body(t):
                    for m in range(NS):
                        P, e = m // 4, m % 4
                        if e == 0:
                            wait_alone(eng, Q["mm2"], (t * NP + P - 1) * 2)
                        wait_alone(eng, Q["mm1"], t * NS + m + 1)
                        ex_ = (P // 2 % 4) * 4 + e
                        eng.activation(hid[m % 8], psA[m % 2][:, :, 0:CH], ACT.Gelu,
                                       bias=b1_s[:, ex_:ex_ + 1]).then_inc(Q["gel"], 1)
                chunks(eng, body, lambda t: None)

            @block.vector
            def _(eng):
                def combine(t, half):
                    wait_alone(eng, Q["fold"], t * NI + half * 4 + 4)
                    wait_alone(eng, Q["wo"], t * 2)
                    eng.tensor_copy(comb[:, half], psF[:, 0:CH]).then_inc(Q["comb"], 1)

                def finish(t, m_):
                    wait_alone(eng, Q["wo"], t * 2 - 1 + m_)
                    wait_alone(eng, q_st[m_], (t - 1) * 16)
                    eng.scalar_tensor_tensor(out=fin[:, m_], in0=psW[:, 0:CH], scalar=bo_s[:, m_:m_ + 1],
                                             in1=V[:, m_, at_chunk(t - 1)].rearrange("p t c -> p (t c)"),
                                             op0=ALU.add, op1=ALU.add).then_inc(Q["fin"], 1)

                def body(t):
                    first = isinstance(t, int) and t == 0
                    for P in range(NP):
                        it, pair = P // 2, P % 2
                        if P == 2 and not first:
                            combine(t - 1, 1)
                        if P == 10:
                            combine(t, 0)
                        if P in (4, 6) and not first:
                            finish(t, (P - 4) // 2)
                        if pair == 0:
                            wait_alone(eng, q_wb[it % 2], (t * (NI // 2) + it // 2 + 1) * 64)
                            wait_alone(eng, Q["fold"], t * NI + it - 1)
                        for hh in range(2):
                            wait_alone(eng, Q["mm2"], (t * NP + P) * 2 + hh + 1)
                            q = pair * 2 + hh
                            eng.scalar_tensor_tensor(out=gsum[:, it % 2, q], in0=psY[:, hh, 0:CH],
                                                     scalar=b2_s[:, it % 4:it % 4 + 1], in1=wb[:, it % 2, q],
                                                     op0=ALU.add, op1=ALU.mult).then_inc(Q["gs"], 1)

                def tail(t):
                    combine(t - 1, 1)
                    for m_ in range(2):
                        finish(t, m_)
                chunks(eng, body, tail)


def arrays(i):
    import numpy as np
    a = {k: np.asarray(v) for k, v in i.items()}
    ac = np.ascontiguousarray
    r = {}
    r["x"] = a["x"].reshape(B, C, HW)
    r["c1T"] = ac(a["L0_conv_c1_centroids"].transpose(0, 2, 1)).reshape(C, KC)
    r["c2T"] = ac(a["L0_conv_c2_centroids"].reshape(8, 8, KC, 9).transpose(1, 3, 0, 2)).reshape(72, 8, KC)
    r["c3T"] = ac(a["L0_conv_c3_centroids"].transpose(0, 2, 1)).reshape(WID, KC)
    r["invts"] = np.stack([a[f"L0_conv_c{n}_invt"].reshape(()) for n in (1, 2, 3)]).reshape(1, 3)
    r["lut1"] = a["L0_conv_c1_lut"].reshape(-1, WID)
    r["lut2"] = a["L0_conv_c2_lut"].reshape(-1, WID)
    r["lut3"] = a["L0_conv_c3_lut"].reshape(-1, C)
    for n in (1, 2, 3):
        r[f"bn{n}"] = np.stack([a[f"L0_conv_bn{n}_g"], a[f"L0_conv_bn{n}_b"]], 1)
    r["routerT"] = ac(a["L0_ffn_router_w"].T)
    r["w_moe"] = a["L0_ffn_expert_weights"]
    r["se_w1T"] = ac(a["L1_conv_W1"].reshape(128, C).T)
    r["se_b1"] = a["L1_conv_b1"].reshape(128, 1)
    r["se_w2T"] = ac(a["L1_conv_W2"].transpose(0, 2, 1)).reshape(128, C)
    r["se_b2"] = a["L1_conv_b2"]
    r["se_wgT"] = ac(a["L1_conv_Wg"].T)
    r["se_bg"] = a["L1_conv_bg"].reshape(1, 8)
    r["wm"] = a["L1_ffn_Wm"]
    r["bm"] = ac(a["L1_ffn_bm"].reshape(2, 128).T)
    r["emb"] = a["L1_ffn_expert_emb"]
    r["w1"] = ac(a["L1_ffn_W1"].transpose(1, 0, 2))
    r["b1"] = ac(a["L1_ffn_b1"].T)
    r["w2"] = ac(a["L1_ffn_W2"].transpose(1, 0, 2))
    r["b2"] = ac(a["L1_ffn_b2"].reshape(4, 4 * HD).T)
    r["wo"] = a["L1_ffn_Wo"]
    r["bo"] = ac(a["L1_ffn_bo"].reshape(2, 128).T)
    return r


def kernel(**inputs):
    import numpy as _np
    import concourse.bacc as _bacc
    from concourse import mybir as _mybir
    from concourse.bass_utils import run_bass_kernel_spmd as _run

    ins = arrays(inputs)
    nc = _bacc.Bacc("TRN2", target_bir_lowering=False, num_devices=1)
    args = [nc.dram_tensor(k, v.shape, _mybir.dt.from_np(v.dtype), kind="ExternalInput").ap() for k, v in ins.items()]
    args.append(nc.dram_tensor("out", (B, C, HW), _mybir.dt.float32, kind="ExternalOutput").ap())
    build(nc, *args)
    r = _run(nc, [ins], core_ids=[0])
    return _np.asarray(r.results[0]["out"]).reshape(B, C, HH, HH)
```

```python
from contextlib import ExitStack

import concourse.bass as bass
from concourse import mybir

F32 = mybir.dt.float32
F32R = mybir.dt.float32r
U32 = mybir.dt.uint32
ALU = mybir.AluOpType
ACT = mybir.ActivationFunctionType
AX = mybir.AxisListType

B, C, HH = 32, 256, 14
HW = HH * HH
IMGS = 2
CH = IMGS * HW
T = B // IMGS
SUB = 98
NSUB = CH // SUB
PADW = 16
PADHW = PADW * PADW
WID = 64
KC = 16
E0 = 32
NH, NE, HD, HID = 8, 16, 32, 128
NEG = -3.0e38
EPS_LN_C, EPS_LN_T, EPS_BN = 1e-6, 1e-5, 1e-5
SLOTS = 10


def wait(eng, sem, value):
    if not (isinstance(value, int) and value <= 0):
        eng.wait_ge(sem, value)


def staged(eng, front, back, count=T, slots=SLOTS, late=None):
    def step(s, i=0):
        for k in range(slots):
            for lag, part in enumerate((front, back, late)):
                t = s - lag
                if part is not None and (t >= 0 if isinstance(i, int) else True) and t < count:
                    part(k, i * 2 + t, i + t // 2, t % 2)
    first = 2 if late is None else 4
    for s in range(first):
        step(s)
    with eng.Fori(0, (count - first) // 2) as i:
        step(first, i)
        step(first + 1, i)
    for s in range(count, count + (1 if late is None else 2)):
        step(s)


def nothing(k, t, n, u):
    pass


def at_chunk(t, size=1):
    return slice(t * size, (t + 1) * size) if isinstance(t, int) else bass.ds(t * size, size)


def build(nc, x, c1T, c2T, c3T, invts, lut1, lut2, lut3, bn1, bn2, bn3, routerT, w_moe,
          se_w1T, se_b1, se_w2T, se_b2, se_wgT, se_bg, wm, bm, emb, w1, b1, w2, b2, wo, bo, out):
    with ExitStack() as ctx:
        def sb(name, shape, dt=F32):
            return ctx.enter_context(nc.sbuf_tensor(name, shape, dt))

        owner = [ctx]

        def sem(name):
            return nc.alloc_semaphore(name=name)

        def phase():
            stack = ctx.enter_context(ExitStack())
            before_ = nc.snapshot_sems()

            def give_back():
                nc.clear_and_free_semaphores(nc.allocated_since(before_))
                nc.all_engine_barrier()
            stack.callback(give_back)
            owner.append(stack)
            stack.callback(owner.pop)
            return stack

        V = sb("V", [128, 2, T, CH])
        BIG = sb("BIG", [128, E0 * 2 * C])
        OUT = BIG[:, 0:2 * T * CH].rearrange("p (h t c) -> p h t c", h=2, t=T)
        YS = sb("YS", [128, T, 2, IMGS])
        xs = sb("xs", [128, 2, 2, CH])
        vv = sb("vv", [128, 2, 2, CH])
        vr = sb("vr", [128, 2, CH], F32R)
        sq = sb("sq", [128, 2, CH])
        rs = sb("rs", [128, CH])
        nm = sb("nm", [7 * PADW, NSUB, 64])
        nmT = sb("nmT", [64, 2, CH], F32R)
        ex = sb("ex", [128, 2, CH])
        at = sb("at", [128, 2, CH])
        rz = sb("rz", [128, 2, CH])
        rh = sb("rh", [128, CH], F32R)
        rS = sb("rS", [128, CH], F32R)
        stats = sb("stats", [128, 2, T, 6])
        aggr = sb("aggr", [128, 2, 2])
        bns = sb("bns", [128, 2])
        bnb = sb("bnb", [128, 2])
        bnt = sb("bnt", [128, 2])
        gb1 = sb("gb1", [64, 2])
        gb2 = sb("gb2", [64, 2])
        gb3 = sb("gb3", [128, 2, 2])
        inv = sb("inv", [128, 3])
        inv2 = sb("inv2", [128, 3])
        mean_w = sb("mean_w", [128, 128])
        ident = sb("ident", [128, 128])
        ones_c = sb("ones_c", [128, 1])
        ones_r = sb("ones_r", [128, 128], F32R)
        z_sel = sb("z_sel", [128, 3, 32])
        b_sel = sb("b_sel", [128, 2, 128])
        b_sel_r = sb("b_sel_r", [128, 2, 128], F32R)
        second8 = sb("second8", [128, 8])
        second16 = sb("second16", [128, 4])
        in8 = sb("in8", [128, 2])
        lows = sb("lows", [128, 1])
        ind = BIG[0:64, 0:1024]
        ind_s = sb("ind_s", [64, 128])
        ind_r = sb("ind_r", [64, 1024], F32R)
        eps_c = sb("eps_c", [128, 1])
        eps_t = sb("eps_t", [128, 1])

        psM = ctx.enter_context(nc.psum_tensor("psM", [128, 512], F32))
        psN = ctx.enter_context(nc.psum_tensor("psN", [128, 2, 512], F32))
        psS = ctx.enter_context(nc.psum_tensor("psS", [128, 2, 512], F32))
        psZ = ctx.enter_context(nc.psum_tensor("psZ", [128, 2, 512], F32))
        psO = ctx.enter_context(nc.psum_tensor("psO", [128, 512], F32))

        ypad_d = nc.dram_tensor("ypad_d", [WID, B * PADHW + 64], F32)
        x_v = x.rearrange("(t b) (h p) w -> t p h b w", b=IMGS, h=2)
        out_v = out.rearrange("(t b) (h p) w -> t p h b w", b=IMGS, h=2)

        s_const = sem("s_const")
        s_go = sem("s_go")

        def wait_alone(eng, s, value):
            if isinstance(value, int):
                wait(eng, s, value)
            else:
                count = eng.snap(eng.to_reg(value))
                eng.wait_ge(s_go, 1)
                eng.wait_ge(s, count)

        def dma_x(eng, t, n, u, free, need, landed):
            wait(eng, free, need)
            for h in range(2):
                src = x_v[t:t + 1] if isinstance(t, int) else x_v[bass.ds(t, 1)]
                eng.dma_start(xs[:, u, h].rearrange("p (b w) -> p b w", b=IMGS),
                              src[0, :, h]).then_inc(landed[u], 16)

        s_set = sem("s_set")
        s_iota = sem("s_iota")
        with nc.Block() as block:
            @block.sync
            def _(eng):
                eng.dma_start(inv[:], invts.partition_broadcast(128)).then_inc(s_const, 16)
                eng.dma_start(gb1[:], bn1).then_inc(s_const, 16)
                eng.dma_start(gb2[:], bn2).then_inc(s_const, 16)
                eng.dma_start(gb3[:], bn3.rearrange("(h p) k -> p h k", p=128)).then_inc(s_const, 16)
                eng.wait_ge(s_const, 64)

            @block.gpsimd
            def _(eng):
                eng.memset(mean_w[:], 1.0 / C)
                eng.memset(ones_c[:], 1.0)
                eng.memset(eps_c[:], EPS_LN_C)
                eng.memset(eps_t[:], EPS_LN_T)
                eng.memset(ident[:], 0.0)
                eng.memset(z_sel[:, 2], 1.0)
                eng.memset(z_sel[:, 0].rearrange("p (x g b) -> p x g b", g=2, b=8)[:, :, 0], 1.0)
                eng.memset(z_sel[:, 1].rearrange("p (x g b) -> p x g b", g=2, b=8)[:, :, 1], 1.0)
                eng.memset(z_sel[:, 0].rearrange("p (x g b) -> p x g b", g=2, b=8)[:, :, 1], 0.0)
                eng.memset(z_sel[:, 1].rearrange("p (x g b) -> p x g b", g=2, b=8)[:, :, 0], 0.0)
                eng.memset(b_sel[:], 0.0)
                eng.memset(second8[:], 1.0)
                eng.memset(second16[:], 1.0)
                eng.memset(ind[:], 1.0).then_inc(s_iota, 1)
                eng.wait_ge(s_iota, 1)
                eng.affine_select(out=ident[:], in_=ident[:], compare_op=ALU.not_equal, fill=1.0, base=0,
                                  pattern=[[-1, 128]], channel_multiplier=1)
                eng.affine_select(out=ind[:], in_=ind[:], compare_op=ALU.is_ge, fill=0.0, base=0,
                                  pattern=[[1, 1024]], channel_multiplier=-KC)
                zv = z_sel[:].rearrange("p j (x b) -> p (j x) b", b=8)
                eng.affine_select(out=zv, in_=zv, compare_op=ALU.is_ge, fill=0.0, base=0,
                                  pattern=[[0, 12], [-KC, 8]], channel_multiplier=1)
                eng.affine_select(out=second8[:], in_=second8[:], compare_op=ALU.is_ge, fill=0.0, base=-8,
                                  pattern=[[-16, 8]], channel_multiplier=1)
                eng.affine_select(out=second16[:], in_=second16[:], compare_op=ALU.is_ge, fill=0.0, base=-16,
                                  pattern=[[-32, 4]], channel_multiplier=1).then_inc(s_iota, 1)
                eng.wait_ge(s_iota, 2)
                eng.affine_select(out=ind[:], in_=ind[:], compare_op=ALU.is_ge, fill=0.0, base=KC - 1,
                                  pattern=[[-1, 1024]], channel_multiplier=KC)
                eng.affine_select(out=zv, in_=zv, compare_op=ALU.is_ge, fill=0.0, base=KC - 1,
                                  pattern=[[0, 12], [KC, 8]], channel_multiplier=-1)
                eng.affine_select(out=second8[:], in_=second8[:], compare_op=ALU.is_ge, fill=0.0, base=15,
                                  pattern=[[16, 8]], channel_multiplier=-1)
                eng.affine_select(out=second16[:], in_=second16[:], compare_op=ALU.is_ge, fill=0.0, base=31,
                                  pattern=[[32, 4]], channel_multiplier=-1).then_inc(s_iota, 1)
                bv = b_sel[:].rearrange("p g (a b) -> p g a b", b=KC)
                for r in range(16):
                    eng.wait_ge(s_iota, 3 + r)
                    eng.affine_select(out=bv, in_=bv, compare_op=ALU.not_equal, fill=1.0, base=-8 * r,
                                      pattern=[[0, 2], [-1, 8], [0, KC]], channel_multiplier=1).then_inc(s_iota, 1)
                eng.tensor_copy(ind_r[:], ind[:])
                eng.tensor_copy(ind_s[:], ind[:, 0:128])
                eng.tensor_copy(ones_r[:], ones_c[:].to_broadcast([128, 128]))

            @block.vector
            def _(eng):
                eng.wait_ge(s_const, 64)
                eng.tensor_scalar(inv2[:], inv[:], 2.0, None, ALU.mult).then_inc(s_set, 1)
                eng.wait_ge(s_set, 1)
                eng.tensor_scalar(inv[:], inv[:], -1.0, None, ALU.mult).then_inc(s_go, 1)
                eng.wait_ge(s_iota, 3)
                eng.tensor_reduce(in8[:, 1:2], second8[:], AX.X, ALU.max)
                eng.tensor_reduce(lows[:], second16[:], AX.X, ALU.max).then_inc(s_set, 1)
                eng.wait_ge(s_set, 2)
                eng.tensor_scalar(lows[:], lows[:], -1.0, None, ALU.mult)
                eng.tensor_scalar(in8[:, 0:1], in8[:, 1:2], -1.0, 1.0, ALU.mult, ALU.add).then_inc(s_set, 1)
                eng.wait_ge(s_set, 3)
                eng.wait_ge(s_iota, 19)
                for g in range(2):
                    eng.tensor_scalar(b_sel_r[:, g], b_sel[:, g], in8[:, g:g + 1], None, ALU.mult)

            @block.scalar
            def _(eng):
                eng.preload_act_table_set("natural_log_exp_and_others")

        class Norm:

            def __init__(self, name, eps, bank=None):
                self.eps = eps
                self.bank = psM[:] if bank is None else bank
                self.mean, self.dev, self.sqr, self.var, self.log, self.rstd, self.done = (
                    sem(f"{name}_{x}") for x in ("mean", "dev", "sqr", "var", "log", "rstd", "done"))

            def pe_mean(self, eng, t, src):
                for h in range(2):
                    m = eng.matmul(self.bank[:, 0:CH], mean_w[:], src[:, h], start=(h == 0), stop=(h == 1))
                m.then_inc(self.mean, 1)

            def dve_dev(self, eng, t, src, dst):
                wait(eng, self.mean, t + 1)
                eng.tensor_tensor(dst, src, self.bank[:, 0:CH].unsqueeze(1).to_broadcast([128, 2, CH]),
                                  ALU.subtract).then_inc(self.dev, 1)

            def act_square(self, eng, t, d):
                wait(eng, self.dev, t + 1)
                eng.activation(sq[:], d, ACT.Square).then_inc(self.sqr, 1)

            def pe_var(self, eng, t):
                wait(eng, self.sqr, t + 1)
                for h in range(2):
                    m = eng.matmul(self.bank[:, 0:CH], mean_w[:], sq[:, h], start=(h == 0), stop=(h == 1))
                m.then_inc(self.var, 1)

            def act_rstd(self, eng, t):
                wait(eng, self.var, t + 1)
                wait(eng, self.done, t)
                eng.activation(rs[:], self.bank[:, 0:CH], ACT.Ln, bias=self.eps[:, 0:1]).then_inc(self.log, 1)
                wait(eng, self.log, t + 1)
                eng.activation(rs[:], rs[:], ACT.Exp, scale=-0.5).then_inc(self.rstd, 1)

            def dve_norm(self, eng, t, d, dst):
                wait_alone(eng, self.rstd, t + 1)
                return eng.tensor_tensor(dst, d, rs[:].unsqueeze(1).to_broadcast([128, 2, CH]), ALU.mult)

        def amm(name, J, KP, ncb, O, which, cT, lut, blocks, extent, n_scores, t_scores, prep, out_half, n0=2, SR=SUB):
            cols = ncb * KC
            with phase() as c2:
                def sb2(n, shape, dt=F32):
                    return c2.enter_context(nc.sbuf_tensor(f"{name}_{n}", shape, dt))

                cen = sb2("cen", [KP, blocks, KC])
                per = cols // blocks // KC
                wb = sb2("wb", [KP, blocks, per, KC])
                cb = sb2("cb", [KP, blocks, per, KC])
                wb_r = sb2("wb_r", [KP, blocks, per * KC], F32R)
                cb_r = sb2("cb_r", [KP, blocks, per * KC], F32R)
                lut_s = sb2("lut_s", [128, J, O])
                bias_t = sb2("bias_t", [128, J])
                mem = prep["memory"](sb2)
                exs = mem["exs"]
                S = {x: sem(f"{name}_{x}") for x in (
                    "cen", "w", "bias", "src", "nsc", "max", "tr", "nmt", "sc", "exp", "z", "rec", "hi", "inv",
                    "bc", "mul", "lut", "out", "relu", "vst")}
                ld = [sem(f"{name}_ld{u}") for u in range(2)]
                norm = Norm(name, eps_c, psZ[:, 1]) if prep.get("norm") else None
                env = dict(S=S, ld=ld, norm=norm, mem=mem)

                with nc.Block() as block:
                    @block.sync
                    def _(eng):
                        eng.dma_start(cen[:], cT).then_inc(S["cen"], 16)
                        eng.dma_start(lut_s[:], lut.rearrange("(j p) o -> p j o", p=128)).then_inc(S["cen"], 16)
                        if "setup_dma" in prep:
                            prep["setup_dma"](eng, env)
                        eng.wait_ge(S["cen"], 32)

                    @block.vector
                    def _(eng):
                        if "setup_dve" in prep:
                            prep["setup_dve"](eng, env)
                        eng.memset(nmT[:].bitcast(F32), 0.0)
                        eng.wait_ge(S["cen"], 32)
                        for b in range(blocks):
                            cin = cen[:, b].unsqueeze(1).to_broadcast([KP, per, KC])
                            eng.tensor_scalar(wb[:, b], cin, inv2[0:KP, which:which + 1], None, ALU.mult)
                            m = eng.tensor_tensor(cb[:, b], cin, cin, ALU.mult)
                        m.then_inc(S["w"], 1)
                        eng.wait_ge(S["w"], 1)
                        eng.tensor_scalar(cb[:], cb[:], inv[0:KP, which:which + 1], None, ALU.mult).then_inc(S["w"], 1)
                        eng.wait_ge(S["w"], 4)
                        eng.tensor_copy(wb_r[:], wb[:].rearrange("p b a k -> p b (a k)"))
                        eng.tensor_copy(cb_r[:], cb[:].rearrange("p b a k -> p b (a k)")).then_inc(S["w"], 1)
                        eng.wait_ge(S["bias"], 1)
                        eng.tensor_copy(bias_t[:], psO[:, 0:J]).then_inc(S["bias"], 1)

                    @block.gpsimd
                    def _(eng):
                        eng.wait_ge(S["w"], 2)
                        for w_ in (wb, cb):
                            for b in range(blocks):
                                m = eng.affine_select(out=w_[:, b], in_=w_[:, b], compare_op=ALU.is_ge, fill=0.0,
                                                      base=0, pattern=[[-extent, per], [0, KC]],
                                                      channel_multiplier=1)
                        m.then_inc(S["w"], 1)
                        eng.wait_ge(S["w"], 3)
                        for w_ in (wb, cb):
                            for b in range(blocks):
                                m = eng.affine_select(out=w_[:, b], in_=w_[:, b], compare_op=ALU.is_ge, fill=0.0,
                                                      base=extent - 1, pattern=[[extent, per], [0, KC]],
                                                      channel_multiplier=-1)
                        m.then_inc(S["w"], 1)

                    @block.tensor
                    def _(eng):
                        eng.wait_ge(S["w"], 4)
                        cbf = cb[:].rearrange("p b a k -> p (b a k)")
                        per_tile = 128
                        for j in range(J):
                            m = eng.matmul(psO[:, j:j + 1], cbf[:, j * per_tile:(j + 1) * per_tile],
                                           ones_c[0:KP, :], start=True, stop=True)
                        m.then_inc(S["bias"], 1)

                    @block.scalar
                    def _(eng):
                        if "setup_act" in prep:
                            prep["setup_act"](eng, env)

                outs = [psO] if O <= 64 else [psO, psN[:, 1]]
                OP = min(O, 128)
                ZR = 32 * min(J, 4)
                trk = n0 + NSUB
                zk = max(trk + 2, J + 2)
                slots = max(zk + 1, J + 4)

                with nc.Block() as block:
                    @block.sync
                    def _(eng):
                        if "sync" in prep:
                            staged(eng, lambda k, t, n, u: prep["sync"](eng, env, k, t, n, u), None, slots=slots)

                    @block.gpsimd
                    def _(eng):
                        if "pool" in prep:
                            staged(eng, lambda k, t, n, u: prep["pool"](eng, env, k, t, n, u), None, slots=slots)

                    @block.tensor
                    def _(eng):
                        def front(k, t, n, u):
                            if "pe" in prep:
                                prep["pe"](eng, env, k, t, n, u)
                            if n0 <= k < trk:
                                s = k - n0
                                if s == 0 and "landed" not in prep:
                                    wait_alone(eng, S["src"], t + 1)
                                wait_alone(eng, S["max"], t * NSUB + s)
                                for dst, src, b, lo, hi in n_scores(env, u, s):
                                    K = src.shape[0]
                                    eng.matmul(dst, src, wb_r[0:K, b, lo:hi], start=True, stop=False)
                                    m = eng.matmul(dst, ones_r[0:K, 0:SR], cb_r[0:K, b, lo:hi],
                                                   start=False, stop=True)
                                m.then_inc(S["nsc"], 1)
                            if k == trk:
                                wait_alone(eng, S["max"], t * NSUB + NSUB)
                                wait_alone(eng, S["rec"], t - 1)
                                for s in range(NSUB):
                                    m = eng.transpose(psM[0:ncb, s * SR:(s + 1) * SR], nm[0:SR, s, 0:ncb],
                                                      ident[0:SR, 0:SR])
                                m.then_inc(S["tr"], 1)

                        def back(k, t, n, u):
                            if k < J:
                                g = t * J + k
                                if k == 0:
                                    wait_alone(eng, S["nmt"], t + 1)
                                    if "landed" in prep:
                                        wait_alone(eng, ld[u], (n + 1) * prep["landed"])
                                wait_alone(eng, S["exp"], g - 1)
                                w_, src = t_scores(env, wb, k, u)
                                eng.matmul(psS[:, k % 2, 0:CH], w_, src, start=True, stop=False)
                                eng.matmul(psS[:, k % 2, 0:CH], ind_r[:, k * 128:(k + 1) * 128],
                                           nmT[:, u, :], start=False, stop=True).then_inc(S["sc"], 1)
                            if k == zk:
                                wait_alone(eng, S["exp"], t * J + J)
                                wait_alone(eng, S["nmt"], min(t + 2, T) if isinstance(t, int) else t + 2)
                                for j in range(J):
                                    q = 32 * (j % 4)
                                    m = eng.matmul(psM[q:q + 32, 0:CH], z_sel[:, j // 4 if J > 4 else 2], exs[:, u, j],
                                                   start=(j < 4), stop=(j + 4 >= J), tile_position=(0, q))
                                m.then_inc(S["z"], 1)

                        def late(k, t, n, u):
                            if 3 <= k < J + 3:
                                j = k - 3
                                if j == 0:
                                    wait_alone(eng, S["inv"], t + 1)
                                if j == 1 and norm:
                                    wait_alone(eng, norm.log, min(t + 3, T) if isinstance(t, int) else t + 3)
                                wait_alone(eng, S["mul"], t * J + j - 1)
                                q = 32 * (j % 4)
                                eng.matmul(psZ[:, j % 2, 0:CH], b_sel_r[q:q + 32, j // 4], rS[q:q + 32],
                                           start=True, stop=True).then_inc(S["bc"], 1)
                            if 4 <= k < J + 4:
                                j = k - 4
                                wait_alone(eng, S["mul"], t * J + j + 1)
                                if j == 0:
                                    wait_alone(eng, S["out"], t)
                                for o, dst in enumerate(outs):
                                    m = eng.matmul(dst[0:OP, 0:CH], lut_s[:, j, o * 128:o * 128 + OP],
                                                   at[:, j % 2], start=(j == 0), stop=(j == J - 1))
                                m.then_inc(S["lut"], 1)
                        staged(eng, front, back, slots=slots, late=late)

                    @block.vector
                    def _(eng):
                        def front(k, t, n, u):
                            if "dve" in prep:
                                prep["dve"](eng, env, k, t, n, u)
                            if n0 <= k < trk:
                                s = k - n0
                                wait(eng, S["nsc"], t * NSUB + s + 1)
                                if s == 0:
                                    wait(eng, S["tr"], t)
                                flat = psN[0:SR].rearrange("p a b -> p (a b)")[:, 0:cols]
                                eng.tensor_reduce(nm[0:SR, s, 0:ncb], flat.rearrange("p (c k) -> p c k", k=KC), AX.X,
                                                  ALU.max, negate=True).then_inc(S["max"], 1)

                        def late(k, t, n, u):
                            if k == 0:
                                wait(eng, S["z"], t + 1)
                                eng.reciprocal(rz[0:ZR, 0], psM[0:ZR, 0:CH]).then_inc(S["rec"], 1)
                            if k == 1:
                                wait_alone(eng, S["hi"], t + 1)
                                wait_alone(eng, S["bc"], t * J)
                                eng.scalar_tensor_tensor(out=rS[0:ZR], in0=rh[0:ZR].bitcast(F32), scalar=lows[0:ZR, 0:1],
                                                         in1=rz[0:ZR, 0], op0=ALU.mult, op1=ALU.add).then_inc(S["inv"], 1)
                            if 3 <= k < J + 3:
                                j = k - 3
                                wait(eng, S["bc"], t * J + j + 1)
                                wait(eng, S["lut"], t * J + j - 1)
                                eng.tensor_tensor(at[:, j % 2], exs[:, u, j], psZ[:, j % 2, 0:CH],
                                                  ALU.mult).then_inc(S["mul"], 1)
                            if k == J + 3:
                                wait_alone(eng, S["lut"], t * J + J)
                                ts = at_chunk(t)
                                for o, dst in enumerate(outs):
                                    oh = out_half if len(outs) == 1 else o
                                    eng.bn_stats(stats[0:OP, o, ts], dst[0:OP, 0:CH])
                                    m = eng.tensor_copy(OUT[0:OP, oh, ts], dst[0:OP, 0:CH].unsqueeze(1))
                                m.then_inc(S["out"], 1)
                        staged(eng, front, None, slots=slots, late=late)

                    @block.scalar
                    def _(eng):
                        def front(k, t, n, u):
                            if "act" in prep:
                                prep["act"](eng, env, k, t, n, u)
                            if k == trk:
                                wait_alone(eng, S["tr"], t + 1)
                                wait_alone(eng, S["sc"], (t - 1) * J)
                                if SR == SUB:
                                    src, dst = psM[0:ncb, 0:CH], nmT[0:ncb, u]
                                else:
                                    src = psM[0:ncb, 0:NSUB * SR].rearrange("p (r w) -> p r w", w=PADW)[:, :, 0:HH]
                                    dst = nmT[0:ncb, u].rearrange("p (r w) -> p r w", w=HH)
                                eng.activation(dst, src, ACT.Copy).then_inc(S["nmt"], 1)

                        def back(k, t, n, u):
                            if k < J:
                                wait_alone(eng, S["sc"], t * J + k + 1)
                                if k == 0:
                                    wait_alone(eng, S["mul"], (t - 1) * J)
                                eng.activation(exs[:, u, k], psS[:, k % 2, 0:CH], ACT.Exp,
                                               bias=bias_t[:, k:k + 1]).then_inc(S["exp"], 1)

                        def late(k, t, n, u):
                            if k == 1:
                                wait(eng, S["rec"], t + 1)
                                wait(eng, S["inv"], t)
                                eng.activation(rh[0:ZR], rz[0:ZR, 0], ACT.Copy).then_inc(S["hi"], 1)
                        staged(eng, front, back, slots=slots, late=late)

        def bn_coefs(name, halves, P, gb):
            s = sem(f"{name}_bn")
            with nc.Block() as block:
                @block.vector
                def _(eng):
                    for h in range(halves):
                        m = eng.bn_aggr(aggr[0:P, h], stats[0:P, h].rearrange("p t k -> p (t k)"))
                    m.then_inc(s, 1)
                    eng.wait_ge(s, 3)
                    g = gb[0:P].unsqueeze(1) if halves == 1 else gb[:]
                    eng.tensor_tensor(bns[0:P, 0:halves], bnt[0:P, 0:halves], g[:, :, 0], ALU.mult).then_inc(s, 1)
                    eng.wait_ge(s, 4)
                    eng.tensor_tensor(bnt[0:P, 0:halves], aggr[0:P, 0:halves, 0], bns[0:P, 0:halves],
                                      ALU.mult).then_inc(s, 1)
                    eng.wait_ge(s, 5)
                    eng.tensor_tensor(bnb[0:P, 0:halves], g[:, :, 1], bnt[0:P, 0:halves], ALU.subtract).then_inc(s, 1)

                @block.scalar
                def _(eng):
                    eng.wait_ge(s, 1)
                    eng.activation(bnt[0:P, 0:halves], aggr[0:P, 0:halves, 1], ACT.Ln,
                                   bias=eps_t[0:P, 0:1]).then_inc(s, 1)
                    eng.wait_ge(s, 2)
                    eng.activation(bnt[0:P, 0:halves], bnt[0:P, 0:halves], ACT.Exp, scale=-0.5).then_inc(s, 1)

        def a_sync(eng, env, k, t, n, u):
            if k == 0:
                dma_x(eng, t, n, u, env["norm"].dev, t - 1, env["ld"])

        def a_pe(eng, env, k, t, n, u):
            if k == 0:
                wait(eng, env["ld"][u], (n + 1) * 32)
                wait(eng, env["S"]["mul"], (t - 2) * 8)
                env["norm"].pe_mean(eng, t, xs[:, u])
            if k == 2:
                env["norm"].pe_var(eng, t)

        def a_dve(eng, env, k, t, n, u):
            if k == 0:
                wait_alone(eng, env["S"]["sc"], (t - 1) * 8)
                wait_alone(eng, env["S"]["vst"], t - 1)
                env["norm"].dve_dev(eng, t, xs[:, u], vv[:, u])
            if k == 2:
                env["norm"].dve_norm(eng, t, vv[:, u], vv[:, u]).then_inc(env["norm"].done, 1)

        def a_act(eng, env, k, t, n, u):
            if k == 0:
                wait(eng, env["norm"].var, t)
                env["norm"].act_square(eng, t, vv[:, u])
            if k == 2:
                env["norm"].act_rstd(eng, t)

        def a_pool(eng, env, k, t, n, u):
            if k == 2:
                wait_alone(eng, env["norm"].done, t + 1)
                wait_alone(eng, env["S"]["nsc"], t * NSUB)
                eng.tensor_copy(vr[:], vv[:, u]).then_inc(env["S"]["src"], 1)
                eng.tensor_copy(V[:, :, at_chunk(t)].rearrange("p h t c -> p h (t c)"), vv[:, u]).then_inc(env["S"]["vst"], 1)

        def a_n(env, u, s):
            for b in range(2):
                yield (psN[0:SUB, b, :], vr[:, b, s * SUB:(s + 1) * SUB], b, 0, 512)

        def a_t(env, wb, j, u):
            q = 32 * (j % 4)
            w_ = wb[:].rearrange("p b a k -> p b (a k)")[q:q + 32, j // 4, (j % 4) * 128:(j % 4) * 128 + 128]
            return w_, vv[q:q + 32, u, j // 4, :]

        amm("a", 8, 128, 64, WID, 0, c1T.rearrange("(h p) k -> p h k", p=128), lut1, 2, 4, a_n, a_t,
            dict(memory=lambda sb2: dict(exs=sb2("exs", [128, 2, 8, CH])), norm=True, sync=a_sync, pe=a_pe, dve=a_dve, act=a_act, pool=a_pool), 0, n0=5)
        bn_coefs("a", 1, WID, gb1)

        ypad_rd = nc.dram_tensor("ypad_rd", [WID, B * PADHW + 64], F32)
        ypad_r = BIG[0:WID, T * CH:T * CH + B * PADHW].bitcast(F32R)
        with nc.sbuf_tensor("ypad", [WID, B, PADW, PADW], F32) as ypad:
            s_pad0, s_pad, s_padst = sem("s_pad0"), sem("s_pad"), sem("s_padst")
            with nc.Block() as block:
                @block.vector
                def _(eng):
                    eng.memset(ypad[:], 0.0).then_inc(s_pad0, 1)

                    quarter = B // 4 * PADHW
                    for q in range(4):
                        eng.wait_ge(s_pad, q + 1)
                        cols = slice(q * quarter, (q + 1) * quarter)
                        m = eng.tensor_copy(ypad_r[:, cols], ypad[:].rearrange("p b r w -> p (b r w)")[:, cols])
                    m.then_inc(s_pad0, 1)

                @block.scalar
                def _(eng):
                    eng.wait_ge(s_pad0, 1)
                    for t in range(T):
                        src = OUT[0:WID, 0, t].rearrange("p (b r w) -> p b r w", b=IMGS, r=HH)
                        for b in range(IMGS):
                            m = eng.activation(ypad[:, t * IMGS + b, 1:1 + HH, 1:1 + HH], src[:, b], ACT.Relu,
                                               bias=bnb[0:WID, 0:1], scale=bns[0:WID, 0:1])
                        if t % 4 == 3:
                            m.then_inc(s_pad, 1)

                @block.sync
                def _(eng):
                    eng.wait_ge(s_pad, 4)
                    flat = ypad[:].rearrange("p b r w -> p (b r w)")
                    eng.dma_start(ypad_d.ap()[:, 0:B * PADHW], flat).then_inc(s_padst, 16)
                    eng.dma_start(ypad_d.ap()[:, B * PADHW:], flat[:, 0:64]).then_inc(s_padst, 16)
                    eng.wait_ge(s_pad0, 2)
                    eng.dma_start(ypad_rd.ap()[:, 0:B * PADHW], ypad_r.bitcast(F32)).then_inc(s_padst, 16)
                    eng.dma_start(ypad_rd.ap()[:, B * PADHW:], ypad_r[:, 0:64].bitcast(F32)).then_inc(s_padst, 16)
                    eng.wait_ge(s_padst, 64)

        def b_memory(sb2):
            size = 8 * IMGS * HH * PADW
            exs = OUT[:, 0].rearrange("p (a j) c -> p a j c", a=2)
            free = BIG[0:72, 2 * T * CH:2 * T * CH + size].rearrange("p (g c) -> p g c", g=8)
            return dict(exs=exs, pat=[free, sb2("pat", [72, 8, IMGS * HH * PADW])], pat_r=sb2("pat_r", [72, 8, IMGS * HH * PADW], F32R))

        def b_load(eng, t, src_d, dst, landed):
            for tap in range(9):
                off = (tap // 3) * PADW + tap % 3
                src = src_d.ap()[:, off:off + B * PADHW].rearrange("(g c) (t b r) -> t c g b r", g=8, b=IMGS, r=PADHW)
                src = src[at_chunk(t)][0]
                for b in range(IMGS):
                    eng.dma_start(dst[tap:tap + 64:9, :, b * HH * PADW:(b + 1) * HH * PADW],
                                  src[:, :, b, 0:HH * PADW]).then_inc(landed, 16)

        def b_sync(eng, env, k, t, n, u):
            if k == 0:
                wait(eng, env["S"]["nsc"], t * NSUB)
                b_load(eng, t, ypad_rd, env["mem"]["pat_r"][:].bitcast(F32), env["S"]["src"])
                wait(eng, env["S"]["sc"], (t - 1) * 8)
                b_load(eng, t, ypad_d, env["mem"]["pat"][u], env["ld"][u])

        def b_pe(eng, env, k, t, n, u):
            if k == 2:
                wait_alone(eng, env["S"]["src"], (t + 1) * 16 * 9 * IMGS)

        def b_n(env, u, s):
            flat = psN[0:7 * PADW].rearrange("p a b -> p (a b)")
            for g in range(8):
                v = env["mem"]["pat_r"][:, g, s * 7 * PADW:(s + 1) * 7 * PADW]
                yield (flat[:, g * 128:(g + 1) * 128], v, g, 0, 128)

        def b_t(env, wb, j, u):
            v = env["mem"]["pat"][u][:, j].rearrange("p (r w) -> p r w", w=PADW)[:, :, 0:HH]
            return wb[:, j].rearrange("p a k -> p (a k)"), v

        amm("b", 8, 72, 64, WID, 1, c2T, lut2, 8, 9, b_n, b_t,
            dict(memory=b_memory, sync=b_sync, pe=b_pe, landed=16 * 9 * IMGS), 1, SR=7 * PADW)
        bn_coefs("b", 1, WID, gb2)

        def c_memory(sb2):
            return dict(exs=sb2("exs", [128, 2, 2, CH]), y=sb2("y", [WID, 2, CH]), y_r=sb2("y_r", [WID, CH], F32R))

        def c_act(eng, env, k, t, n, u):
            if k == 0:
                wait_alone(eng, env["S"]["sc"], (t - 1) * 2)
                ts = slice(t, t + 1) if isinstance(t, int) else bass.ds(t, 1)
                eng.activation(env["mem"]["y"][:, u], OUT[0:WID, 1, ts].rearrange("p t c -> p (t c)"), ACT.Relu,
                               bias=bnb[0:WID, 0:1], scale=bns[0:WID, 0:1]).then_inc(env["S"]["relu"], 1)

        def c_pool(eng, env, k, t, n, u):
            if k == 1:
                wait_alone(eng, env["S"]["relu"], t + 1)
                wait_alone(eng, env["S"]["nsc"], t * NSUB)
                eng.tensor_copy(env["mem"]["y_r"][:], env["mem"]["y"][:, u]).then_inc(env["S"]["src"], 1)

        def c_n(env, u, s):
            yield (psN[0:SUB, 0, 0:256], env["mem"]["y_r"][:, s * SUB:(s + 1) * SUB], 0, 0, 256)

        def c_t(env, wb, j, u):
            w_ = wb[:].rearrange("p b a k -> p (b a k)")[32 * j:32 * j + 32, j * 128:(j + 1) * 128]
            return w_, env["mem"]["y"][32 * j:32 * j + 32, u]

        amm("c", 2, 64, 16, C, 2, c3T.rearrange("p (b k) -> p b k", b=1), lut3, 1, 4, c_n, c_t,
            dict(memory=c_memory, act=c_act, pool=c_pool), 0)
        bn_coefs("c", 2, 128, gb3)

        NT = T * NSUB
        ROWS = 128
        TILES = -(-2 * B * HW // ROWS) + E0
        TILES += TILES % 2
        RT = 19
        xn_d = nc.dram_tensor("xn_d", [NT * SUB, C], F32)
        xg_d = nc.dram_tensor("xg_d", [TILES * ROWS, C], F32)
        yg_d = nc.dram_tensor("yg_d", [TILES * ROWS, C], F32)
        d_ctx = phase()

        def sbd(name, shape, dt=F32):
            return d_ctx.enter_context(nc.sbuf_tensor(name, shape, dt))
        w_moe_s = BIG
        router_s = sbd("router_s", [128, 2, E0])
        before = sbd("before", [SUB, SUB])
        ones_s = sbd("ones_s", [SUB, SUB])
        iota_i = sbd("iota_i", [SUB, 192], U32)
        rev = sbd("rev", [SUB, E0])
        xnb = sbd("xnb", [SUB, 2, NSUB, C])
        lg = sbd("lg", [SUB, 11, NSUB, E0])
        LG, EQ, M1, LG2, M2, MASK, DL, EX, TMP = range(9)
        sc_ = sbd("sc_", [SUB, 8, NSUB])
        seen = sbd("seen", [SUB, 2, E0])
        P12 = sbd("P12", [SUB, T, NSUB, 2])
        MK = sbd("MK", [SUB, 2, NT])
        POS = sbd("POS", [SUB, 2, NT])
        SLOT = sbd("SLOT", [SUB, T, NSUB, 2], U32)
        EID = sbd("EID", [SUB, TILES], U32)

        dn = Norm("d", eps_t)
        D = {k: sem(f"d_{k}") for k in ("w", "set", "pre", "relu", "x1", "vst", "tr", "ev", "lgd", "rt", "exp",
                                        "pfx", "mid")}
        d_ld = [sem(f"d_ld{u}") for u in range(2)]
        d_xst = [sem(f"d_xst{u}") for u in range(2)]
        with nc.Block() as block:
            @block.sync
            def _(eng):
                eng.dma_start(router_s[:], routerT.rearrange("(h p) e -> p h e", p=128)).then_inc(D["w"], 16)
                eng.wait_ge(D["w"], 16)

            @block.gpsimd
            def _(eng):
                eng.memset(ones_s[:], 1.0)
                eng.memset(before[:], 1.0).then_inc(D["set"], 1)
                eng.iota(iota_i[:, 0:E0], pattern=[[-1, E0]], base=E0, channel_multiplier=0).then_inc(D["set"], 1)
                eng.wait_ge(D["set"], 2)
                eng.affine_select(out=before[:], in_=before[:], compare_op=ALU.is_ge, fill=0.0, base=-1,
                                  pattern=[[1, SUB]], channel_multiplier=-1)
                eng.tensor_copy(rev[:], iota_i[:, 0:E0])

            @block.vector
            def _(eng):
                eng.memset(seen[:], 0.0)

        with nc.Block() as block:
            @block.sync
            def _(eng):
                def front(k, t, n, u):
                    if k == 0:
                        wait(eng, D["vst"], t - 1)
                        dma_x(eng, t, n, u, dn.dev, t - 1, d_ld)

                def back(k, t, n, u):
                    if k == 4:
                        wait(eng, D["ev"], t * NSUB + NSUB)
                        dst = xn_d.ap().rearrange("(t s p) c -> t p s c", p=SUB, s=NSUB)[at_chunk(t)][0]
                        eng.dma_start(dst, xnb[:, u]).then_inc(d_xst[u], 16)
                staged(eng, front, back)
                for u in range(2):
                    eng.wait_ge(d_xst[u], T // 2 * 16)

            @block.vector
            def _(eng):
                def front(k, t, n, u):
                    ts = at_chunk(t)
                    if k == 0:
                        wait_alone(eng, D["lgd"], t - 1)
                        for h in range(2):
                            m = eng.scalar_tensor_tensor(out=vv[:, u, h], in0=OUT[:, h, ts].squeeze(1), scalar=bns[:, h:h + 1],
                                                         in1=V[:, h, ts].squeeze(1), op0=ALU.mult, op1=ALU.add)
                        m.then_inc(D["pre"], 1)
                    if k == 1:
                        wait(eng, d_ld[u], (n + 1) * 32)
                        wait(eng, D["relu"], t + 1)
                        eng.tensor_tensor(xs[:, u], xs[:, u], vv[:, u], ALU.add).then_inc(D["x1"], 1)
                    if k == 2:
                        dn.dve_dev(eng, t, xs[:, u], vv[:, u])
                    if k == 7:
                        dn.dve_norm(eng, t, vv[:, u], vv[:, u]).then_inc(dn.done, 1)

                def back(k, t, n, u):
                    if k not in (4, 5, 6):
                        return
                    count = [{4: 0, 5: 13, 6: 15}[k]]

                    def step(ins):
                        ins.then_inc(D["rt"], 1)
                        count[0] += 1
                        wait_alone(eng, D["rt"], t * RT + count[0])
                    L = lambda i: lg[:, i]
                    many = lambda i: sc_[:, i].unsqueeze(2).to_broadcast([SUB, NSUB, E0])
                    revb = rev[:].unsqueeze(1).to_broadcast([SUB, NSUB, E0])
                    if k == 4:
                        wait(eng, D["lgd"], t + 1)
                        step(eng.tensor_copy(L(LG), psN[0:SUB, 0, 0:NSUB * E0].rearrange("p (s e) -> p s e", s=NSUB)))
                        src = LG
                        for j, mask in ((0, M1), (1, M2)):
                            step(eng.tensor_reduce(sc_[:, j], L(src), AX.X, ALU.max))
                            step(eng.tensor_tensor(L(EQ), L(src), many(j), ALU.is_equal))
                            step(eng.tensor_tensor(L(EQ), L(EQ), revb, ALU.mult))
                            mk = MK[:, j, at_chunk(t, NSUB)]
                            step(eng.tensor_reduce(sc_[:, 2 + j], L(EQ), AX.X, ALU.max))
                            eng.tensor_copy(mk, sc_[:, 2 + j])
                            if j == 0:
                                step(eng.tensor_tensor(L(M1), L(EQ), many(2), ALU.is_equal))
                                eng.tensor_tensor(L(DL), L(LG), many(0), ALU.subtract)
                                step(eng.scalar_tensor_tensor(out=L(LG2), in0=L(M1), scalar=NEG, in1=L(LG), op0=ALU.mult,
                                                              op1=ALU.add))
                                src = LG2
                        eng.tensor_tensor(L(M2), L(EQ), many(3), ALU.is_equal).then_inc(D["rt"], 1)
                        assert count[0] == 11
                    if k == 5:
                        wait_alone(eng, D["rt"], t * RT + 12)
                        eng.tensor_tensor(L(MASK), L(M1), L(M2), ALU.add).then_inc(D["rt"], 1)
                        wait_alone(eng, D["exp"], t + 1)
                        eng.tensor_reduce(sc_[:, 4], L(EX), AX.X, ALU.add)
                        step(eng.tensor_tensor(L(TMP), L(EX), L(M2), ALU.mult))
                        eng.reciprocal(sc_[:, 5], sc_[:, 4])
                        step(eng.tensor_reduce(sc_[:, 6], L(TMP), AX.X, ALU.add))
                        eng.tensor_copy(P12[:, at_chunk(t), :, 0].squeeze(1), sc_[:, 5])
                        eng.tensor_tensor(P12[:, at_chunk(t), :, 1].squeeze(1), sc_[:, 6], sc_[:, 5], ALU.mult)
                    if k == 6:
                        wait_alone(eng, D["pfx"], t + 1)
                        pos = psN[0:SUB, 1, 0:NSUB * E0].rearrange("p (s e) -> p s e", s=NSUB)
                        step(eng.tensor_tensor(L(TMP), L(M1), pos, ALU.mult))
                        eng.tensor_reduce(POS[:, 0, at_chunk(t, NSUB)], L(TMP), AX.X, ALU.add)
                        step(eng.tensor_tensor(L(EQ), L(M2), pos, ALU.mult))
                        eng.tensor_reduce(POS[:, 1, at_chunk(t, NSUB)], L(EQ), AX.X, ALU.add)
                        step(eng.tensor_reduce(seen[:, 1], L(MASK).rearrange("p s e -> p e s"), AX.X, ALU.add))
                        step(eng.tensor_tensor(seen[:, 0], seen[:, 0], seen[:, 1], ALU.add))
                        assert count[0] == RT
                staged(eng, front, back)

            @block.scalar
            def _(eng):
                def front(k, t, n, u):
                    if k == 0:
                        wait(eng, D["pre"], t + 1)
                        for h in range(2):
                            m = eng.activation(vv[:, u, h], vv[:, u, h], ACT.Relu, bias=bnb[:, h:h + 1])
                        m.then_inc(D["relu"], 1)
                    if k == 2:
                        wait(eng, dn.var, t)
                        dn.act_square(eng, t, vv[:, u])
                    if k == 3:
                        dn.act_rstd(eng, t)

                def back(k, t, n, u):
                    if k < NSUB:
                        wait(eng, D["tr"], t * NSUB + k + 1)
                        if k == 0:
                            wait(eng, d_xst[u], n * 16)
                        eng.activation(xnb[:, u, k], psS[0:SUB, k % 2, 0:C], ACT.Copy).then_inc(D["ev"], 1)
                    if k == 4:
                        wait(eng, D["rt"], t * RT + 12)
                        eng.activation(lg[:, EX], lg[:, DL], ACT.Exp).then_inc(D["exp"], 1)
                staged(eng, front, back)

            @block.gpsimd
            def _(eng):
                def front(k, t, n, u):
                    if k == 1:
                        wait_alone(eng, D["x1"], t + 1)
                        eng.tensor_copy(V[:, :, at_chunk(t)].rearrange("p h t c -> p h (t c)"),
                                        xs[:, u]).then_inc(D["vst"], 1)
                staged(eng, front, nothing)

            @block.tensor
            def _(eng):
                def front(k, t, n, u):
                    if k == 1:
                        wait(eng, D["x1"], t + 1)
                        wait(eng, dn.log, t)
                        dn.pe_mean(eng, t, xs[:, u])
                    if k == 2:
                        dn.pe_var(eng, t)

                def back(k, t, n, u):
                    if k < NSUB:
                        s = k
                        if s == 0:
                            wait_alone(eng, dn.done, t + 1)
                            wait_alone(eng, D["rt"], t * RT)
                        wait_alone(eng, D["ev"], t * NSUB + s - 1)
                        sub = slice(s * SUB, (s + 1) * SUB)
                        for h in range(2):
                            m = eng.transpose(psS[0:SUB, s % 2, h * 128:(h + 1) * 128], vv[:, u, h, sub], ident[:])
                        m.then_inc(D["tr"], 1)
                        for h in range(2):
                            m = eng.matmul(psN[0:SUB, 0, s * E0:(s + 1) * E0], vv[:, u, h, sub], router_s[:, h],
                                           start=(h == 0), stop=(h == 1))
                        if s == NSUB - 1:
                            m.then_inc(D["lgd"], 1)
                    if k == 5:
                        wait_alone(eng, D["rt"], t * RT + 13)
                        for s in range(NSUB):
                            dst = psN[0:SUB, 1, s * E0:(s + 1) * E0]
                            eng.matmul(dst, before[:], lg[:, MASK, s], start=True, stop=False)
                            for s2 in range(s):
                                eng.matmul(dst, ones_s[:], lg[:, MASK, s2], start=False, stop=False)
                            m = eng.matmul(dst, ones_s[:], seen[:, 0], start=False, stop=True)
                        m.then_inc(D["pfx"], 1)
                staged(eng, front, back)

        flat = OUT.rearrange("p a t c -> p (a t c)")
        NK = B * HW // ROWS + 1
        with nc.Block() as block:
            @block.tensor
            def _(eng):
                eng.matmul(psN[0:SUB, 1, 0:E0], ones_s[:], seen[:, 0], start=True, stop=True).then_inc(D["pfx"], 1)

            @block.gpsimd
            def _(eng):
                eng.iota(iota_i[:, 0:NK], pattern=[[ROWS, NK]], base=0, channel_multiplier=0)
                eng.iota(iota_i[:, NK:NK + TILES], pattern=[[1, TILES]], base=0, channel_multiplier=0).then_inc(D["set"], 1)

            @block.vector
            def _(eng):
                count = [0]

                def step(ins):
                    ins.then_inc(D["mid"], 1)
                    count[0] += 1
                    eng.wait_ge(D["mid"], count[0])
                cnt, tl, base, ends = (flat[0:SUB, 32 * i:32 * i + 32] for i in range(4))
                steps_k = flat[0:SUB, 128:128 + NK + TILES]
                lower = flat[0:SUB, 512:512 + E0 * E0].rearrange("p (a b) -> p a b", a=E0)
                big = flat[0:SUB, 2048:2048 + E0 * TILES]
                bs = flat[0:SUB, 1536:1536 + NT]
                eng.wait_ge(D["pfx"], T + 1)
                eng.wait_ge(D["set"], 3)
                step(eng.tensor_copy(cnt, psN[0:SUB, 1, 0:E0]))
                step(eng.tensor_copy(steps_k, iota_i[:, 0:NK + TILES]))
                b1_ = big[:, 0:E0 * NK].rearrange("p (e k) -> p e k", e=E0)
                step(eng.tensor_tensor(b1_, cnt.unsqueeze(2).to_broadcast([SUB, E0, NK]),
                                       steps_k[:, 0:NK].unsqueeze(1).to_broadcast([SUB, E0, NK]), ALU.is_gt))
                step(eng.tensor_reduce(tl, b1_, AX.X, ALU.add))
                step(eng.tensor_tensor(lower, rev[:].unsqueeze(1).to_broadcast([SUB, E0, E0]),
                                       rev[:].unsqueeze(2).to_broadcast([SUB, E0, E0]), ALU.is_gt))
                step(eng.tensor_tensor(lower, lower, tl.unsqueeze(1).to_broadcast([SUB, E0, E0]), ALU.mult))
                step(eng.tensor_reduce(base, lower, AX.X, ALU.add))
                step(eng.tensor_tensor(ends, base, tl, ALU.add))
                step(eng.tensor_scalar(base, base, float(ROWS), None, ALU.mult))
                b2_ = big.rearrange("p (t e) -> p t e", e=E0)
                step(eng.tensor_tensor(b2_, ends.unsqueeze(1).to_broadcast([SUB, TILES, E0]),
                                       steps_k[:, NK:NK + TILES].unsqueeze(2).to_broadcast([SUB, TILES, E0]), ALU.is_le))
                te = steps_k[:, 0:TILES]
                step(eng.tensor_reduce(te, b2_, AX.X, ALU.add))
                step(eng.tensor_scalar(te, te, float(E0 - 1), None, ALU.min))
                step(eng.tensor_copy(EID[:], te))
                b3_ = big[:, 0:NT * E0].rearrange("p (t e) -> p t e", e=E0)
                for j in range(2):
                    step(eng.tensor_tensor(b3_, rev[:].unsqueeze(1).to_broadcast([SUB, NT, E0]),
                                           MK[:, j].unsqueeze(2).to_broadcast([SUB, NT, E0]), ALU.is_equal))
                    step(eng.tensor_tensor(b3_, b3_, base.unsqueeze(1).to_broadcast([SUB, NT, E0]), ALU.mult))
                    step(eng.tensor_reduce(bs, b3_, AX.X, ALU.add))
                    step(eng.tensor_tensor(bs, bs, POS[:, j], ALU.add))
                    step(eng.tensor_copy(SLOT[:].rearrange("p t s j -> p (t s) j")[:, :, j], bs))

        G = {k: sem(f"g_{k}") for k in ("z", "zf", "ix", "ix2")}
        g_ld = [sem(f"g_ld{u}") for u in range(2)]
        g_sc = [sem(f"g_sc{u}") for u in range(2)]
        ZF = TILES * ROWS * C // (4 * 128)
        idx = sbd("idx", [SUB, 2, NSUB * 2], U32)
        pc = sbd("pc", [SUB, 2, NSUB * 2])
        with nc.Block() as block:
            @block.vector
            def _(eng):
                eng.memset(flat[:, 0:ZF], 0.0).then_inc(G["z"], 1)

                def front(k, t, n, u):
                    if k == 0:
                        wait_alone(eng, g_sc[u], n * 16 * NSUB * 2)
                        eng.tensor_copy(idx[:, u], SLOT[:, at_chunk(t)].rearrange("p t s j -> p (t s j)")).then_inc(G["ix"], 1)
                staged(eng, front, nothing, slots=1)

            @block.sync
            def _(eng):
                eng.wait_ge(G["z"], 1)
                all_xg = xg_d.ap().rearrange("r c -> (r c)").rearrange("(q p f) -> q p f", q=4, p=128)
                for q in range(4):
                    eng.dma_start(all_xg[q], flat[:, 0:ZF]).then_inc(G["zf"], 16)

                def front(k, t, n, u):
                    if k == 0:
                        wait(eng, g_sc[u], n * 16 * NSUB * 2)
                        src = xn_d.ap().rearrange("(t s p) c -> t p s c", p=SUB, s=NSUB)[at_chunk(t)][0]
                        eng.dma_start(xnb[:, u], src).then_inc(g_ld[u], 16)
                staged(eng, front, nothing, slots=1)
                eng.wait_ge(G["zf"], 64)
                for q in range(16):
                    eng.dma_start(w_moe_s[:].rearrange("p (e h c) -> p e h c", e=E0, h=2)[:, 2 * q:2 * q + 2],
                                  w_moe[2 * q:2 * q + 2].rearrange("e (h p) c -> p e h c", p=128)).then_inc(D["w"], 16)
                eng.wait_ge(D["w"], 17 * 16)

            @block.gpsimd
            def _(eng):
                eng.wait_ge(G["zf"], 64)

                def front(k, t, n, u):
                    if k == 0:
                        wait_alone(eng, G["ix"], t + 1)
                        wait_alone(eng, g_ld[u], (n + 1) * 16)
                        for s in range(NSUB):
                            for j in range(2):
                                eng.indirect_dma_start(
                                    xg_d.ap(), bass.IndirectOffsetOnAxis(ap=idx[:, u, 2 * s + j:2 * s + j + 1], axis=0),
                                    xnb[:, u, s], None).then_inc(g_sc[u], 16)
                staged(eng, front, nothing, slots=1)
                for u in range(2):
                    eng.wait_ge(g_sc[u], T // 2 * 16 * NSUB * 2)

        X = {k: sem(f"x_{k}") for k in ("tr", "ev", "mm", "y")}
        x_ld = [sem(f"x_ld{u}") for u in range(2)]
        x_st = [sem(f"x_st{u}") for u in range(2)]
        xr = vv[:].rearrange("p u h c -> p u (h c)")[:, :, 0:C]
        xt = xs[:].rearrange("p u h c -> p u (h c)")[:, :, 0:C]
        yr = ex[:, :, 0:C]
        with nc.Block() as block:
            @block.sync
            def _(eng):
                def front(k, t, n, u):
                    wait(eng, X["tr"], t - 1)
                    eng.dma_start(xr[:, u], xg_d.ap()[at_chunk(t, ROWS)]).then_inc(x_ld[u], 16)
                staged(eng, front, nothing, TILES, 1)

            @block.tensor
            def _(eng):
                def front(k, t, n, u):
                    wait_alone(eng, x_ld[u], (n + 1) * 16)
                    wait_alone(eng, X["ev"], t - 1)
                    for h in range(2):
                        m = eng.transpose(psS[:, u, h * 128:(h + 1) * 128], xr[:, u, h * 128:(h + 1) * 128], ident[:])
                    m.then_inc(X["tr"], 1)

                def back(k, t, n, u):
                    e = eng.value_load(EID[0:1, at_chunk(t)], min_val=0, max_val=E0 - 1)
                    wait(eng, X["ev"], t + 1)
                    wait(eng, X["y"], t - 1)
                    for h in range(2):
                        m = eng.matmul(psZ[:, u, 0:C], xt[:, u, h * 128:(h + 1) * 128],
                                       w_moe_s[:, bass.ds(e * (2 * C) + h * C, C)], start=(h == 0), stop=(h == 1))
                    m.then_inc(X["mm"], 1)
                staged(eng, front, back, TILES, 1)

            @block.scalar
            def _(eng):
                def front(k, t, n, u):
                    wait(eng, X["tr"], t + 1)
                    wait(eng, X["mm"], t - 1)
                    eng.activation(xt[:, u], psS[:, u, 0:C], ACT.Copy).then_inc(X["ev"], 1)
                staged(eng, front, nothing, TILES, 1)

            @block.vector
            def _(eng):
                def back(k, t, n, u):
                    wait(eng, X["mm"], t + 1)
                    wait(eng, x_st[u], n * 16)
                    eng.tensor_copy(yr[:, u], psZ[:, u, 0:C]).then_inc(X["y"], 1)
                staged(eng, nothing, back, TILES, 1)

            @block.gpsimd
            def _(eng):
                def back(k, t, n, u):
                    wait(eng, X["y"], t + 1)
                    eng.dma_start(yg_d.ap()[at_chunk(t, ROWS)], yr[:, u]).then_inc(x_st[u], 16)
                staged(eng, nothing, back, TILES, 1)
                for u in range(2):
                    eng.wait_ge(x_st[u], TILES // 2 * 16)

        gn = Norm("h", eps_c)
        H = {k: sem(f"h_{k}") for k in ("ix", "y0", "y", "tr", "x2", "vst", "sum")}
        h_g = [sem(f"h_g{u}") for u in range(2)]
        gath = sbd("gath", [SUB, 2, NSUB * 2, C])
        yn = xnb
        with nc.Block() as block:
            @block.gpsimd
            def _(eng):
                def front(k, t, n, u):
                    if k == 0:
                        wait_alone(eng, H["ix"], t + 1)
                        wait_alone(eng, H["y"], t - 1)
                        for s in range(NSUB):
                            for j in range(2):
                                i = 2 * s + j
                                eng.indirect_dma_start(gath[:, u, i], None, yg_d.ap(),
                                                       bass.IndirectOffsetOnAxis(ap=idx[:, u, i:i + 1], axis=0)).then_inc(h_g[u], 16)

                def back(k, t, n, u):
                    if k == 2:
                        wait_alone(eng, H["x2"], t + 1)
                        eng.tensor_copy(V[:, :, at_chunk(t)].rearrange("p h t c -> p h (t c)"), xs[:, u]).then_inc(H["vst"], 1)
                    if k == 5:
                        wait_alone(eng, gn.done, t + 1)
                        eng.tensor_copy(OUT[:, :, at_chunk(t)].rearrange("p h t c -> p h (t c)"), vv[:, u]).then_inc(H["vst"], 1)
                staged(eng, front, back)

            @block.vector
            def _(eng):
                def front(k, t, n, u):
                    if k == 0:
                        wait_alone(eng, h_g[u], n * 16 * NSUB * 2)
                        eng.tensor_copy(idx[:, u], SLOT[:, at_chunk(t)].rearrange("p t s j -> p (t s j)")).then_inc(H["ix"], 1)
                        eng.tensor_copy(pc[:, u], P12[:, at_chunk(t)].rearrange("p t s j -> p (t s j)")).then_inc(H["y0"], 1)
                    if k == 9:
                        wait(eng, h_g[u], (n + 1) * 16 * NSUB * 2)
                        wait(eng, H["y0"], t * 2 + 1)
                        wait(eng, H["tr"], t - 1)
                        for s in range(NSUB):
                            m = eng.tensor_scalar(yn[:, u, s], gath[:, u, 2 * s], pc[:, u, 2 * s:2 * s + 1], None, ALU.mult)
                        m.then_inc(H["y0"], 1)
                        wait(eng, H["y0"], t * 2 + 2)
                        for s in range(NSUB):
                            m = eng.scalar_tensor_tensor(out=yn[:, u, s], in0=gath[:, u, 2 * s + 1],
                                                         scalar=pc[:, u, 2 * s + 1:2 * s + 2], in1=yn[:, u, s],
                                                         op0=ALU.mult, op1=ALU.add)
                        m.then_inc(H["y"], 1)

                def back(k, t, n, u):
                    if k == 1:
                        wait_alone(eng, H["tr"], t + 1)
                        wait_alone(eng, H["vst"], t * 2 - 2)
                        eng.tensor_tensor(xs[:, u], V[:, :, at_chunk(t)].rearrange("p h t c -> p h (t c)"),
                                          psN[:, :, 0:CH], ALU.add).then_inc(H["x2"], 1)
                    if k == 3:
                        gn.dve_dev(eng, t, xs[:, u], vv[:, u])
                    if k == 4:
                        gn.dve_norm(eng, t, vv[:, u], vv[:, u]).then_inc(gn.done, 1)
                        wait_alone(eng, gn.done, t + 1)
                        eng.tensor_reduce(YS[:, at_chunk(t)].rearrange("p t h b -> p (t h b)"),
                                          vv[:, u].rearrange("p h (b w) -> p (h b) w", b=IMGS), AX.X, ALU.add)
                staged(eng, front, back)

            @block.scalar
            def _(eng):
                def back(k, t, n, u):
                    if k == 3:
                        wait(eng, gn.var, t)
                        gn.act_square(eng, t, vv[:, u])
                    if k == 4:
                        gn.act_rstd(eng, t)
                staged(eng, nothing, back)

            @block.tensor
            def _(eng):
                def back(k, t, n, u):
                    if k == 0:
                        wait_alone(eng, H["y"], t + 1)
                        wait_alone(eng, H["x2"], t)
                        for s in range(NSUB):
                            for h in range(2):
                                m = eng.transpose(psN[:, h, s * SUB:(s + 1) * SUB], yn[:, u, s, h * 128:(h + 1) * 128],
                                                  ident[0:SUB, 0:SUB])
                        m.then_inc(H["tr"], 1)
                    if k == 2:
                        wait(eng, H["x2"], t + 1)
                        wait(eng, gn.log, t)
                        gn.pe_mean(eng, t, xs[:, u])
                    if k == 3:
                        gn.pe_var(eng, t)
                staged(eng, nothing, back)
        d_ctx.close()

        SE_E, SE_R = 8, 16
        SC = sb("SC", [128, T, 2, IMGS])
        s_se = {k: sem(f"se_{k}") for k in ("w", "dve", "pe", "act")}
        with ExitStack() as c3:
            def sb3(name, shape):
                return c3.enter_context(nc.sbuf_tensor(name, shape, F32))
            w1t = sb3("w1t", [128, 2, 128])
            wgt = sb3("wgt", [128, 2, SE_E])
            w2t = sb3("w2t", [128, C])
            b1t = sb3("b1t", [128, 1])
            b2t = sb3("b2t", [SE_E, C])
            bgt = sb3("bgt", [B, SE_E])
            ym = sb3("ym", [128, 2, B])
            hid = sb3("hid", [128, B])
            gate = sb3("gate", [B, 3, SE_E])
            gs = sb3("gs", [B, 3])
            gT = sb3("gT", [SE_E, B])
            gB = sb3("gB", [128, B])
            sg = sb3("sg", [128, 2, B])
            with nc.Block() as block:
                @block.sync
                def _(eng):
                    eng.dma_start(w1t[:], se_w1T.rearrange("(h p) e -> p h e", p=128)).then_inc(s_se["w"], 16)
                    eng.dma_start(wgt[:], se_wgT.rearrange("(h p) e -> p h e", p=128)).then_inc(s_se["w"], 16)
                    eng.dma_start(w2t[:], se_w2T).then_inc(s_se["w"], 16)
                    eng.dma_start(b1t[:], se_b1).then_inc(s_se["w"], 16)
                    eng.dma_start(b2t[:], se_b2).then_inc(s_se["w"], 16)
                    eng.dma_start(bgt[:], se_bg.partition_broadcast(B)).then_inc(s_se["w"], 16)
                    eng.wait_ge(s_se["w"], 96)

                @block.vector
                def _(eng):
                    count = [0]

                    def step(ins):
                        ins.then_inc(s_se["dve"], 1)
                        count[0] += 1
                        eng.wait_ge(s_se["dve"], count[0])
                    step(eng.tensor_scalar(ym[:].rearrange("p h (t b) -> p h t b", b=IMGS),
                                           YS[:].rearrange("p t h b -> p h t b"), 1.0 / HW, None, ALU.mult))
                    eng.wait_ge(s_se["w"], 96)
                    eng.wait_ge(s_se["pe"], 1)
                    step(eng.tensor_tensor(gate[:, 0], psM[0:B, 0:SE_E], bgt[:], ALU.add))
                    step(eng.tensor_reduce(gs[:, 0:1], gate[:, 0], AX.X, ALU.max, negate=True))
                    eng.wait_ge(s_se["act"], 1)
                    step(eng.reciprocal(gs[:, 2:3], gs[:, 1:2]))
                    step(eng.tensor_scalar(gate[:, 2], gate[:, 1], gs[:, 2:3], None, ALU.mult))
                    eng.wait_ge(s_se["pe"], 3)
                    step(eng.tensor_copy(gT[:], psM[0:SE_E, 64:64 + B]))
                    eng.wait_ge(s_se["pe"], 4)
                    eng.wait_ge(s_se["act"], 2)
                    step(eng.tensor_tensor(hid[:], hid[:], psM[:, 128:128 + B], ALU.mult))
                    eng.wait_ge(s_se["act"], 4)
                    step(eng.tensor_scalar(sg[:], sg[:], 1.0, None, ALU.add))
                    step(eng.reciprocal(SC[:].rearrange("p t h b -> p h t b"),
                                        sg[:].rearrange("p h (t b) -> p h t b", b=IMGS)))

                @block.tensor
                def _(eng):
                    eng.wait_ge(s_se["w"], 96)
                    eng.wait_ge(s_se["dve"], 1)
                    for h in range(2):
                        m = eng.matmul(psM[0:B, 0:SE_E], ym[:, h], wgt[:, h], start=(h == 0), stop=(h == 1))
                    m.then_inc(s_se["pe"], 1)
                    for h in range(2):
                        m = eng.matmul(psO[:, 0:B], w1t[:, h], ym[:, h], start=(h == 0), stop=(h == 1))
                    m.then_inc(s_se["pe"], 1)
                    eng.wait_ge(s_se["dve"], 5)
                    eng.transpose(psM[0:SE_E, 64:64 + B], gate[:, 2], ident[0:B, 0:B]).then_inc(s_se["pe"], 1)
                    eng.wait_ge(s_se["dve"], 6)
                    eng.matmul(psM[:, 128:128 + B], ind_s[0:SE_E, :], gT[:], start=True, stop=True).then_inc(s_se["pe"], 1)
                    eng.wait_ge(s_se["dve"], 7)
                    for h in range(2):
                        dst = psZ[:, h, 0:B]
                        eng.matmul(dst, w2t[:, h * 128:(h + 1) * 128], hid[:], start=True, stop=False)
                        m = eng.matmul(dst, b2t[:, h * 128:(h + 1) * 128], gT[:], start=False, stop=True)
                    m.then_inc(s_se["pe"], 1)

                @block.scalar
                def _(eng):
                    eng.wait_ge(s_se["dve"], 3)
                    eng.activation(gate[:, 1], gate[:, 0], ACT.Exp, bias=gs[:, 0:1], accum_out=gs[:, 1:2]).then_inc(s_se["act"], 1)
                    eng.wait_ge(s_se["pe"], 2)
                    eng.wait_ge(s_se["w"], 96)
                    eng.activation(hid[:], psO[:, 0:B], ACT.Relu, bias=b1t[:, 0:1]).then_inc(s_se["act"], 1)
                    eng.wait_ge(s_se["pe"], 5)
                    for h in range(2):
                        eng.activation(sg[:, h], psZ[:, h, 0:B], ACT.Exp, scale=-1.0).then_inc(s_se["act"], 1)

        hs_d = nc.dram_tensor("hs_d", [T, C, CH], F32)
        wt_d = nc.dram_tensor("wt_d", [T, NH * NE, CH], F32)
        ex_d = nc.dram_tensor("ex_d", [T, SUB, NSUB * NH * NE], F32)
        HE = NH * NE
        f_ctx = phase()

        def sbf(name, shape, dt=F32):
            return f_ctx.enter_context(nc.sbuf_tensor(name, shape, dt))
        wm_s = sbf("wm_s", [128, 2, C])
        bm_s = sbf("bm_s", [128, 2])
        embd = sbf("embd", [128, 4, NE])
        hs = BIG[:, 2 * T * CH:2 * T * CH + 4 * CH].rearrange("p (u h c) -> p u h c", u=2, h=2)
        dl = sbf("dl", [SUB, NSUB * NH, NE])
        exf = sbf("exf", [SUB, 2, NSUB * NH, NE])
        mx = sbf("mx", [SUB, NSUB * NH])
        fn = Norm("f", eps_t)
        FD = {k: sem(f"f_{k}") for k in ("w", "set", "x3", "vst", "lin", "hs", "lgd", "max", "dl", "exp")}
        f_hst = [sem(f"f_hst{u}") for u in range(2)]
        f_wst = [sem(f"f_wst{u}") for u in range(2)]
        with nc.Block() as block:
            @block.sync
            def _(eng):
                eng.dma_start(wm_s[:], wm.rearrange("(h p) e -> p h e", p=128)).then_inc(FD["w"], 16)
                eng.dma_start(bm_s[:], bm).then_inc(FD["w"], 16)
                eng.wait_ge(FD["set"], 1)
                for q in range(4):
                    eng.dma_start(embd[32 * q:32 * q + 32, q], emb).then_inc(FD["w"], 16)
                eng.wait_ge(FD["w"], 96)

            @block.gpsimd
            def _(eng):
                eng.memset(embd[:], 0.0).then_inc(FD["set"], 1)

        with nc.Block() as block:
            @block.vector
            def _(eng):
                def front(k, t, n, u):
                    if k == 0:
                        wait_alone(eng, FD["vst"], t - 1)
                        for h in range(2):
                            for b in range(IMGS):
                                w_ = slice(b * HW, (b + 1) * HW)
                                m = eng.scalar_tensor_tensor(
                                    out=xs[:, u, h, w_], in0=OUT[:, h, at_chunk(t), w_].squeeze(1),
                                    scalar=SC[:, at_chunk(t), h, b], in1=V[:, h, at_chunk(t), w_].squeeze(1),
                                    op0=ALU.mult, op1=ALU.add)
                        m.then_inc(FD["x3"], 1)
                    if k == 1:
                        wait(eng, FD["lin"], t - 1)
                        fn.dve_dev(eng, t, xs[:, u], vv[:, u])
                    if k == 6:
                        fn.dve_norm(eng, t, vv[:, u], vv[:, u]).then_inc(fn.done, 1)

                def back(k, t, n, u):
                    if k == 4:
                        wait_alone(eng, FD["lgd"], t + 1)
                        wait_alone(eng, FD["exp"], t)
                        lgs = psN[0:SUB, 0].rearrange("p (s e) -> p s e", e=NE)
                        eng.tensor_reduce(mx[:], lgs, AX.X, ALU.max).then_inc(FD["max"], 1)
                        wait_alone(eng, FD["max"], t + 1)
                        eng.tensor_tensor(dl[:], lgs, mx[:].unsqueeze(2).to_broadcast([SUB, NSUB * NH, NE]),
                                          ALU.subtract).then_inc(FD["dl"], 1)
                staged(eng, front, back)

            @block.gpsimd
            def _(eng):
                def front(k, t, n, u):
                    if k == 1:
                        wait_alone(eng, FD["x3"], t + 1)
                        eng.tensor_copy(V[:, :, at_chunk(t)].rearrange("p h t c -> p h (t c)"), xs[:, u]).then_inc(FD["vst"], 1)
                staged(eng, front, nothing)

            @block.sync
            def _(eng):
                def back(k, t, n, u):
                    if k == 1:
                        wait(eng, FD["hs"], t + 1)
                        eng.dma_start(hs_d.ap()[at_chunk(t)][0].rearrange("(h p) c -> p h c", h=2),
                                      hs[:, u]).then_inc(f_hst[u], 16)
                    if k == 7:
                        wait(eng, FD["exp"], t + 1)
                        eng.dma_start(ex_d.ap()[at_chunk(t)][0], exf[:, u].rearrange("p s e -> p (s e)")).then_inc(f_wst[u], 16)
                staged(eng, nothing, back)
                for u in range(2):
                    eng.wait_ge(f_hst[u], T // 2 * 16)
                    eng.wait_ge(f_wst[u], T // 2 * 16)

            @block.scalar
            def _(eng):
                def front(k, t, n, u):
                    if k == 1:
                        wait(eng, fn.var, t)
                        fn.act_square(eng, t, vv[:, u])
                    if k == 2:
                        fn.act_rstd(eng, t)

                def back(k, t, n, u):
                    if k == 0:
                        wait(eng, FD["lin"], t + 1)
                        wait_alone(eng, f_hst[u], n * 16)
                        wait_alone(eng, FD["lgd"], t - 1)
                        for m_ in range(2):
                            m = eng.activation(hs[:, u, m_], psS[:, m_, 0:CH], ACT.Identity, bias=bm_s[:, m_:m_ + 1])
                        m.then_inc(FD["hs"], 1)
                    if k == 4:
                        wait_alone(eng, FD["dl"], t + 1)
                        wait_alone(eng, f_wst[u], n * 16)
                        eng.activation(exf[:, u], dl[:], ACT.Exp).then_inc(FD["exp"], 1)
                staged(eng, front, back)

            @block.tensor
            def _(eng):
                def front(k, t, n, u):
                    if k == 1:
                        wait(eng, FD["x3"], t + 1)
                        wait(eng, fn.log, t)
                        fn.pe_mean(eng, t, xs[:, u])
                        fn.pe_var(eng, t)

                def back(k, t, n, u):
                    if k == 0:
                        wait(eng, fn.done, t + 1)
                        wait(eng, FD["hs"], t)
                        for m_ in range(2):
                            for h in range(2):
                                m = eng.matmul(psS[:, m_, 0:CH], wm_s[:, h, m_ * 128:(m_ + 1) * 128], vv[:, u, h],
                                               start=(h == 0), stop=(h == 1))
                        m.then_inc(FD["lin"], 1)
                    if k == 3:
                        wait_alone(eng, FD["hs"], t + 1)
                        wait_alone(eng, FD["dl"], t)
                        for s in range(NSUB):
                            for m_ in range(2):
                                dst = psN[0:SUB, 0, s * HE + m_ * 64:s * HE + m_ * 64 + 64]
                                m = eng.matmul(dst, hs[:, u, m_, s * SUB:(s + 1) * SUB],
                                               embd[:].rearrange("p a e -> p (a e)"), start=True, stop=True)
                        m.then_inc(FD["lgd"], 1)
                staged(eng, front, back)
        f_ctx.close()

        NI, NP, NS = 8, 16, 64
        w1_s = BIG[:, 0:NE * HID].rearrange("p (e i) -> p e i", e=NE)
        w1_r = sb("w1_r", [128, NE, HID], F32R)
        w2_s = sb("w2_s", [HID, NE, HD])
        b1_s = sb("b1_s", [HID, NE])
        b2_s = sb("b2_s", [128, 4])
        wo_s = sb("wo_s", [128, 2, C])
        bo_s = sb("bo_s", [128, 2])
        foldm = sb("fold", [128, HD])
        x_r = sb("x_r", [128, 2, 4, CH], F32R)
        stk = BIG[:, 0:8 * CH].rearrange("p (a q c) -> p a q c", a=2, q=4)
        wb = BIG[:, 8 * CH:16 * CH].rearrange("p (a q c) -> p a q c", a=2, q=4)
        gsum = BIG[:, 16 * CH:24 * CH].rearrange("p (a q c) -> p a q c", a=2, q=4)
        comb = BIG[:, 24 * CH:26 * CH].rearrange("p (a c) -> p a c", a=2)
        fin = BIG[:, 26 * CH:28 * CH].rearrange("p (a c) -> p a c", a=2)
        hid = [xs[:, 0], xs[:, 1], vv[:, 0], vv[:, 1], ex[:], at[:], rz[:], sq[:]]
        Q = {k: sem(f"q_{k}") for k in ("w", "set", "hi", "lo", "mm1", "gel", "mm2", "gs", "fold", "comb",
                                        "wo", "fin", "rt", "tr", "wt")}
        q_ex, q_wst = sem("q_ex"), sem("q_wst")
        q_stk = [sem(f"q_stk{a}") for a in range(2)]
        q_wb = [sem(f"q_wb{a}") for a in range(2)]
        q_st = [sem(f"q_st{a}") for a in range(2)]
        psA, psY, psF = (psN, psS, psZ), psM, psO

        RT2 = 16
        EXP, EQ, M1, L2, M2 = range(5)
        rt = sb("rt", [SUB, 5, NSUB * NH, NE])
        rs16 = sb("rs16", [SUB, 6, NSUB * NH])
        rev16 = sb("rev16", [SUB, NE])
        rev_i = sb("rev_i", [SUB, NE], U32)
        wts = sb("wts", [128, CH])

        def route(eng, r, steps):
            L = lambda i: rt[:, i]
            S_ = lambda i: rs16[:, i]
            many = lambda i: rs16[:, i].unsqueeze(2).to_broadcast([SUB, NSUB * NH, NE])
            revb = rev16[:].unsqueeze(1).to_broadcast([SUB, NSUB * NH, NE])
            for i in steps:
                if i == 0:
                    wait_alone(eng, q_ex, (r + 1) * 16)
                    wait_alone(eng, Q["tr"], r)
                wait_alone(eng, Q["rt"], r * RT2 + i)
                if i == 0:
                    m = eng.tensor_reduce(S_(0), L(EXP), AX.X, ALU.max)
                if i == 1:
                    m = eng.tensor_reduce(S_(4), L(EXP), AX.X, ALU.add)
                if i in (2, 9):
                    m = eng.tensor_tensor(L(EQ), L(EXP if i == 2 else L2), many(0 if i == 2 else 1), ALU.is_equal)
                if i in (3, 10):
                    m = eng.tensor_tensor(L(EQ), L(EQ), revb, ALU.mult)
                if i in (4, 11):
                    m = eng.tensor_reduce(S_(2 if i == 4 else 3), L(EQ), AX.X, ALU.max)
                if i in (5, 12):
                    m = eng.tensor_tensor(L(M1 if i == 5 else M2), L(EQ), many(2 if i == 5 else 3), ALU.is_equal)
                if i == 6:
                    m = eng.reciprocal(S_(5), S_(4))
                if i == 7:
                    m = eng.scalar_tensor_tensor(out=L(L2), in0=L(M1), scalar=NEG, in1=L(EXP), op0=ALU.mult, op1=ALU.add)
                if i == 8:
                    m = eng.tensor_reduce(S_(1), L(L2), AX.X, ALU.max)
                if i == 13:
                    m = eng.tensor_tensor(L(M2), L(M1), L(M2), ALU.add)
                if i == 14:
                    m = eng.tensor_tensor(L(M2), L(EXP), L(M2), ALU.mult)
                if i == 15:
                    m = eng.tensor_tensor(L(M1), L(M2), many(5), ALU.mult)
                m.then_inc(Q["rt"], 1)

        def route_pe(eng, r):
            wait_alone(eng, Q["rt"], (r + 1) * RT2)
            for s in range(NSUB):
                m = eng.transpose(psY[:, s * SUB:(s + 1) * SUB],
                                  rt[:, M1, s * NH:(s + 1) * NH].rearrange("p h e -> p (h e)"), ident[0:SUB, 0:SUB])
            m.then_inc(Q["tr"], 1)

        def route_copy(eng, r):
            wait_alone(eng, Q["tr"], r + 1)
            wait_alone(eng, q_wst, r * 16)
            eng.tensor_copy(wts[:], psY[:, 0:CH]).then_inc(Q["wt"], 1)

        def route_load(eng, r):
            wait(eng, Q["rt"], r * RT2)
            eng.dma_start(rt[:, EXP].rearrange("p s e -> p (s e)"), ex_d.ap()[at_chunk(r)][0]).then_inc(q_ex, 16)

        def route_store(eng, r):
            wait(eng, Q["wt"], r + 1)
            eng.dma_start(wt_d.ap()[at_chunk(r)][0], wts[:]).then_inc(q_wst, 16)

        bufs = [m % 3 for m in range(NS - 1)] + [1]

        def lag(m):
            return next(d for d in range(1, 6) if bufs[(m - d) % NS] == bufs[m])

        def chunks(eng, body, tail):
            body(0)
            with eng.Fori(1, T - 1) as t:
                body(t)
            body(T - 1)
            tail(T)

        def is_last(t):
            return isinstance(t, int) and t == T - 1

        with nc.Block() as block:
            @block.sync
            def _(eng):
                route_load(eng, 0)
                for q in range(4):
                    eng.dma_start(w1_s[32 * q:32 * q + 32], w1).then_inc(Q["w"], 16)
                eng.dma_start(w2_s[:], w2).then_inc(Q["w"], 16)
                eng.dma_start(b1_s[:], b1).then_inc(Q["w"], 16)
                eng.dma_start(b2_s[:], b2).then_inc(Q["w"], 16)
                eng.dma_start(wo_s[:], wo.rearrange("(h p) e -> p h e", p=128)).then_inc(Q["w"], 16)
                eng.dma_start(bo_s[:], bo).then_inc(Q["w"], 16)
                eng.wait_ge(Q["w"], 9 * 16)
                route_store(eng, 0)
                eng.wait_ge(q_wst, 16)

            @block.tensor
            def _(eng):
                route_pe(eng, 0)

            @block.gpsimd
            def _(eng):
                eng.iota(rev_i[:], pattern=[[-1, NE]], base=NE, channel_multiplier=0).then_inc(Q["set"], 1)
                eng.wait_ge(Q["set"], 1)
                eng.tensor_copy(rev16[:], rev_i[:]).then_inc(Q["set"], 1)
                eng.wait_ge(Q["set"], 2)
                eng.memset(foldm[:], 0.0).then_inc(Q["set"], 1)
                for r in range(4):
                    eng.wait_ge(Q["set"], r + 3)
                    eng.affine_select(out=foldm[:], in_=foldm[:], compare_op=ALU.not_equal, fill=1.0,
                                      base=-32 * r, pattern=[[-1, HD]], channel_multiplier=1).then_inc(Q["set"], 1)

            @block.vector
            def _(eng):
                eng.wait_ge(Q["w"], 9 * 16)
                eng.tensor_copy(w1_r[:], w1_s[:]).then_inc(Q["hi"], 1)
                eng.wait_ge(Q["hi"], 1)
                for row in (32, 96):
                    rows = slice(row, row + 32)
                    eng.tensor_tensor(w1_r[rows], w1_s[rows], w1_r[rows].bitcast(F32), ALU.subtract)
                eng.wait_ge(Q["set"], 2)
                route(eng, 0, range(RT2))
                route_copy(eng, 0)

            @block.scalar
            def _(eng):
                eng.preload_act_table_set("gelu_and_others")

        with nc.Block() as block:
            @block.sync
            def _(eng):
                def store(t):
                    for m_ in range(2):
                        wait(eng, Q["fin"], t * 2 - 1 + m_)
                        eng.dma_start(out_v[at_chunk(t - 1)][0, :, m_],
                                      fin[:, m_].rearrange("p (b w) -> p b w", b=IMGS)).then_inc(q_st[m_], 16)

                def body(t):
                    if not is_last(t):
                        route_load(eng, t + 1)
                    wait(eng, q_wst, (t + 1) * 16)
                    for it in range(NI):
                        half, group = it // 4, it % 4
                        if it == 6 and not is_last(t):
                            route_store(eng, t + 1)
                        if group == 0:
                            wait(eng, Q["lo"], 2 * t + half - 1)
                            for r in range(4):
                                eng.dma_start(stk[32 * r:32 * r + 32, half],
                                              hs_d.ap()[at_chunk(t)][0, half * 128:half * 128 + 128].rearrange(
                                                  "(q p) c -> p q c", q=4)).then_inc(q_stk[half], 16)
                        wait(eng, Q["gs"], (t * NI + it - 1) * 4)
                        for e in range(4):
                            src = wt_d.ap()[at_chunk(t)][0].rearrange("(h e) c -> e h c", h=NH)[group * 4 + e]
                            eng.dma_start(wb[32 * e:32 * e + 32, it % 2],
                                          src[half * 4:half * 4 + 4].partition_broadcast(32)).then_inc(q_wb[it % 2], 16)
                        if it == 4 and not (isinstance(t, int) and t == 0):
                            store(t)
                chunks(eng, body, store)
                for m_ in range(2):
                    eng.wait_ge(q_st[m_], 16 * T)

            @block.gpsimd
            def _(eng):
                def body(t):
                    for half in range(2):
                        wait_alone(eng, q_stk[half], (t + 1) * 64)
                        wait_alone(eng, Q["mm1"], (2 * t + half - 1) * (NS // 2))
                        eng.tensor_copy(x_r[:, half], stk[:, half]).then_inc(Q["hi"], 1)
                        wait_alone(eng, Q["hi"], 2 * t + half + 2)
                        eng.tensor_tensor(x_r[64:128, half], stk[64:128, half], x_r[64:128, half].bitcast(F32),
                                          ALU.subtract).then_inc(Q["lo"], 1)
                chunks(eng, body, lambda t: None)

            @block.tensor
            def _(eng):
                def second(t, P, hh):
                    if hh == 0:
                        wait_alone(eng, Q["gel"], t * NS + P * 4 + 4)
                    wait_alone(eng, Q["gs"], (t * NP + P) * 2 + hh)
                    if hh == 0 and P in (3, 5):
                        wait_alone(eng, Q["fin"], t * 2 - 1 + (P - 3) // 2)
                    if hh == 0 and P == 9 and not is_last(t):
                        wait_alone(eng, Q["wt"], t + 2)
                    for e in range(4):
                        mm = eng.matmul(psY[32 * e:32 * e + 32, 0:CH], w2_s[:, (P // 2 % 4) * 4 + e],
                                        hid[(P % 2) * 4 + e][:, hh], start=True, stop=True,
                                        tile_position=(0, 32 * e))
                    mm.then_inc(Q["mm2"], 1)

                def fold(t, it, pair):
                    group = it % 4
                    wait_alone(eng, Q["gs"], (t * NI + it) * 4 + 4)
                    if group == 0 and pair == 0:
                        wait_alone(eng, Q["comb"], t * 2 + it // 4)
                    for q in (2 * pair, 2 * pair + 1):
                        mm = eng.matmul(psF[32 * q:32 * q + 32, 0:CH], foldm[:], gsum[:, it % 2, q],
                                        start=(group == 0), stop=(group == 3), tile_position=(0, 32 * q))
                    mm.then_inc(Q["fold"], 1)

                def last(t, m_):
                    wait_alone(eng, Q["comb"], t * 2)
                    if not (isinstance(t, int) and t == T):
                        wait_alone(eng, Q["gs"], (t * NP + 3 + 2 * m_) * 2)
                    else:
                        wait_alone(eng, Q["gs"], t * NP * 2)
                        wait_alone(eng, Q["fin"], t * 2 - 2 + m_)
                    for h in range(2):
                        mm = eng.matmul(psY[:, 0:CH], wo_s[:, h, m_ * 128:(m_ + 1) * 128], comb[:, h],
                                        start=(h == 0), stop=(h == 1))
                    mm.then_inc(Q["wo"], 1)

                def body(t):
                    first = isinstance(t, int) and t == 0
                    for P in range(NP):
                        half, group, pair = P // 8, P // 2 % 4, P % 2
                        if P % 8 == 0:
                            wait_alone(eng, Q["lo"], 2 * t + half + 1)
                        for e in range(4):
                            m = 4 * P + e
                            wait_alone(eng, Q["gel"], t * NS + m + 1 - lag(m))
                            for hh in range(2):
                                mm = eng.matmul(psA[bufs[m]][:, hh, 0:CH], w1_r[:, group * 4 + e],
                                                x_r[:, half, pair * 2 + hh], start=True, stop=True)
                            mm.then_inc(Q["mm1"], 1)
                            if e in (1, 3):
                                if P > 0:
                                    second(t, P - 1, e // 2)
                                elif not first:
                                    second(t - 1, NP - 1, e // 2)
                            if (P % 2, e) in ((1, 2), (0, 0)):
                                heads = 1 - P % 2
                                it = (P - heads - 3) // 2
                                if it >= 0:
                                    fold(t, it, heads)
                                elif not first:
                                    fold(t - 1, NI + it, heads)
                            if e == 3 and P in (3, 5) and not first:
                                last(t, (P - 3) // 2)
                            if e == 3 and P == 9 and not is_last(t):
                                wait_alone(eng, Q["gs"], (t * NP + P) * 2)
                                route_pe(eng, t + 1)

                def tail(t):
                    fold(t - 1, NI - 2, 1)
                    for hh in range(2):
                        second(t - 1, NP - 1, hh)
                    for pair in range(2):
                        fold(t - 1, NI - 1, pair)
                    for m_ in range(2):
                        last(t, m_)
                chunks(eng, body, tail)

            @block.scalar
            def _(eng):
                def body(t):
                    for m in range(NS):
                        P, e = m // 4, m % 4
                        if e == 0:
                            wait_alone(eng, Q["mm2"], (t * NP + P - 1) * 2)
                        wait_alone(eng, Q["mm1"], t * NS + m + 1)
                        ex_ = (P // 2 % 4) * 4 + e
                        eng.activation(hid[m % 8], psA[bufs[m]][:, :, 0:CH], ACT.Gelu,
                                       bias=b1_s[:, ex_:ex_ + 1]).then_inc(Q["gel"], 1)
                chunks(eng, body, lambda t: None)

            @block.vector
            def _(eng):
                def combine(t, half):
                    wait_alone(eng, Q["fold"], (t * NI + half * 4 + 4) * 2)
                    wait_alone(eng, Q["wo"], t * 2)
                    eng.tensor_copy(comb[:, half], psF[:, 0:CH]).then_inc(Q["comb"], 1)

                def finish(t, m_):
                    wait_alone(eng, Q["wo"], t * 2 - 1 + m_)
                    wait_alone(eng, q_st[m_], (t - 1) * 16)
                    eng.scalar_tensor_tensor(out=fin[:, m_], in0=psY[:, 0:CH], scalar=bo_s[:, m_:m_ + 1],
                                             in1=V[:, m_, at_chunk(t - 1)].rearrange("p t c -> p (t c)"),
                                             op0=ALU.add, op1=ALU.add).then_inc(Q["fin"], 1)

                def body(t):
                    first = isinstance(t, int) and t == 0
                    for P in range(NP):
                        it, pair = P // 2, P % 2
                        if P == 2 and not first:
                            combine(t - 1, 1)
                        if P == 10:
                            combine(t, 0)
                        if P in (3, 5) and not first:
                            finish(t, (P - 3) // 2)
                        if P < RT2 // 2 and not is_last(t):
                            route(eng, t + 1, (2 * P, 2 * P + 1))
                        if P == 9 and not is_last(t):
                            route_copy(eng, t + 1)
                        if pair == 0:
                            wait_alone(eng, q_wb[it % 2], (t * (NI // 2) + it // 2 + 1) * 64)
                            wait_alone(eng, Q["fold"], (t * NI + it - 1) * 2)
                        for hh in range(2):
                            wait_alone(eng, Q["mm2"], (t * NP + P) * 2 + hh + 1)
                            q = pair * 2 + hh
                            eng.scalar_tensor_tensor(out=gsum[:, it % 2, q], in0=psY[:, 0:CH],
                                                     scalar=b2_s[:, it % 4:it % 4 + 1], in1=wb[:, it % 2, q],
                                                     op0=ALU.add, op1=ALU.mult).then_inc(Q["gs"], 1)

                def tail(t):
                    combine(t - 1, 1)
                    for m_ in range(2):
                        finish(t, m_)
                chunks(eng, body, tail)


def arrays(i):
    import numpy as np
    a = {k: np.asarray(v) for k, v in i.items()}
    ac = np.ascontiguousarray
    r = {}
    r["x"] = a["x"].reshape(B, C, HW)
    r["c1T"] = ac(a["L0_conv_c1_centroids"].transpose(0, 2, 1)).reshape(C, KC)
    r["c2T"] = ac(a["L0_conv_c2_centroids"].reshape(8, 8, KC, 9).transpose(1, 3, 0, 2)).reshape(72, 8, KC)
    r["c3T"] = ac(a["L0_conv_c3_centroids"].transpose(0, 2, 1)).reshape(WID, KC)
    r["invts"] = np.stack([a[f"L0_conv_c{n}_invt"].reshape(()) for n in (1, 2, 3)]).reshape(1, 3)
    r["lut1"] = a["L0_conv_c1_lut"].reshape(-1, WID)
    r["lut2"] = a["L0_conv_c2_lut"].reshape(-1, WID)
    r["lut3"] = a["L0_conv_c3_lut"].reshape(-1, C)
    for n in (1, 2, 3):
        r[f"bn{n}"] = np.stack([a[f"L0_conv_bn{n}_g"], a[f"L0_conv_bn{n}_b"]], 1)
    r["routerT"] = ac(a["L0_ffn_router_w"].T)
    r["w_moe"] = a["L0_ffn_expert_weights"]
    r["se_w1T"] = ac(a["L1_conv_W1"].reshape(128, C).T)
    r["se_b1"] = a["L1_conv_b1"].reshape(128, 1)
    r["se_w2T"] = ac(a["L1_conv_W2"].transpose(0, 2, 1)).reshape(128, C)
    r["se_b2"] = a["L1_conv_b2"]
    r["se_wgT"] = ac(a["L1_conv_Wg"].T)
    r["se_bg"] = a["L1_conv_bg"].reshape(1, 8)
    r["wm"] = a["L1_ffn_Wm"]
    r["bm"] = ac(a["L1_ffn_bm"].reshape(2, 128).T)
    r["emb"] = a["L1_ffn_expert_emb"]
    r["w1"] = ac(a["L1_ffn_W1"].transpose(1, 0, 2))
    r["b1"] = ac(a["L1_ffn_b1"].T)
    r["w2"] = ac(a["L1_ffn_W2"].transpose(1, 0, 2))
    r["b2"] = ac(a["L1_ffn_b2"].reshape(4, 4 * HD).T)
    r["wo"] = a["L1_ffn_Wo"]
    r["bo"] = ac(a["L1_ffn_bo"].reshape(2, 128).T)
    return r


def kernel(**inputs):
    import numpy as _np
    import concourse.bacc as _bacc
    from concourse import mybir as _mybir
    from concourse.bass_utils import run_bass_kernel_spmd as _run

    ins = arrays(inputs)
    nc = _bacc.Bacc("TRN2", target_bir_lowering=False, num_devices=1)
    args = [nc.dram_tensor(k, v.shape, _mybir.dt.from_np(v.dtype), kind="ExternalInput").ap() for k, v in ins.items()]
    args.append(nc.dram_tensor("out", (B, C, HW), _mybir.dt.float32, kind="ExternalOutput").ap())
    build(nc, *args)
    r = _run(nc, [ins], core_ids=[0])
    return _np.asarray(r.results[0]["out"]).reshape(B, C, HH, HH)
```

```python
from contextlib import ExitStack

import concourse.bass as bass
from concourse import mybir

F32 = mybir.dt.float32
F32R = mybir.dt.float32r
U32 = mybir.dt.uint32
ALU = mybir.AluOpType
ACT = mybir.ActivationFunctionType
AX = mybir.AxisListType

B, C, HH = 32, 256, 14
HW = HH * HH
IMGS = 2
CH = IMGS * HW
T = B // IMGS
SUB = 98
NSUB = CH // SUB
PADW = 16
PADHW = PADW * PADW
WID = 64
KC = 16
E0 = 32
NH, NE, HD, HID = 8, 16, 32, 128
NEG = -3.0e38
EPS_LN_C, EPS_LN_T = 1e-6, 1e-5


def wait(eng, sem, value):
    if not (isinstance(value, int) and value <= 0):
        eng.wait_ge(sem, value)


def staged(eng, front, back, count=T, slots=1, late=None):
    def step(s, i=0):
        for k in range(slots):
            for lag, part in enumerate((front, back, late)):
                t = s - lag
                if part is not None and (t >= 0 if isinstance(i, int) else True) and t < count:
                    part(k, i * 2 + t, i + t // 2, t % 2)
    first = 4
    for s in range(first):
        step(s)
    with eng.Fori(0, (count - first) // 2) as i:
        step(first, i)
        step(first + 1, i)
    for s in range(count, count + (1 if late is None else 2)):
        step(s)


def at_chunk(t, size=1):
    return slice(t * size, (t + 1) * size) if isinstance(t, int) else bass.ds(t * size, size)


def chunk_of(buf, t):
    return buf[:, :, at_chunk(t)].rearrange("p h t c -> p h (t c)")


def build(nc, x, c1T, c2T, c3T, invts, lut1, lut2, lut3, bn1, bn2, bn3, routerT, w_moe,
          se_w1T, se_b1, se_w2T, se_b2, se_wgT, se_bg, wm, bm, emb, w1, b1, w2, b2, wo, bo, out):
    with ExitStack() as ctx:
        def sb(name, shape, dt=F32):
            return ctx.enter_context(nc.sbuf_tensor(name, shape, dt))

        def sem(name):
            return nc.alloc_semaphore(name=name)

        def phase():
            stack = ctx.enter_context(ExitStack())
            held = nc.snapshot_sems()

            def give_back():
                nc.clear_and_free_semaphores(nc.allocated_since(held))
                nc.all_engine_barrier()
            stack.callback(give_back)
            return stack

        V = sb("V", [128, 2, T, CH])
        BIG = sb("BIG", [128, E0 * 2 * C])
        OUT = BIG[:, 0:2 * T * CH].rearrange("p (h t c) -> p h t c", h=2, t=T)
        YS = sb("YS", [128, T, 2, IMGS])
        xs = sb("xs", [128, 2, 2, CH])
        vv = sb("vv", [128, 2, 2, CH])
        vr = sb("vr", [128, 2, CH], F32R)
        sq = sb("sq", [128, 2, CH])
        rs = sb("rs", [128, CH])
        nm = sb("nm", [7 * PADW, NSUB, 64])
        nmT = sb("nmT", [64, 2, CH], F32R)
        ex = sb("ex", [128, 2, CH])
        at = sb("at", [128, 2, CH])
        rz = sb("rz", [128, 2, CH])
        rh = sb("rh", [128, CH], F32R)
        rS = sb("rS", [128, CH], F32R)
        stats = sb("stats", [128, 2, T, 6])
        aggr = sb("aggr", [128, 2, 2])
        bns = sb("bns", [128, 2])
        bnb = sb("bnb", [128, 2])
        bnt = sb("bnt", [128, 2])
        gb1 = sb("gb1", [64, 2])
        gb2 = sb("gb2", [64, 2])
        gb3 = sb("gb3", [128, 2, 2])
        inv = sb("inv", [128, 3])
        inv2 = sb("inv2", [128, 3])
        mean_w = sb("mean_w", [128, 128])
        ident = sb("ident", [128, 128])
        ones_c = sb("ones_c", [128, 1])
        ones_r = sb("ones_r", [128, 128], F32R)
        z_sel = sb("z_sel", [128, 3, 32])
        b_sel = sb("b_sel", [128, 2, 128])
        b_sel_r = sb("b_sel_r", [128, 2, 128], F32R)
        second8 = sb("second8", [128, 8])
        second16 = sb("second16", [128, 4])
        in8 = sb("in8", [128, 2])
        lows = sb("lows", [128, 1])
        ind = BIG[0:64, 0:1024]
        ind_s = sb("ind_s", [64, 128])
        ind_r = sb("ind_r", [64, 1024], F32R)
        eps_c = sb("eps_c", [128, 1])
        eps_t = sb("eps_t", [128, 1])

        psM = ctx.enter_context(nc.psum_tensor("psM", [128, 512], F32))
        psN = ctx.enter_context(nc.psum_tensor("psN", [128, 2, 512], F32))
        psS = ctx.enter_context(nc.psum_tensor("psS", [128, 2, 512], F32))
        psZ = ctx.enter_context(nc.psum_tensor("psZ", [128, 2, 512], F32))
        psO = ctx.enter_context(nc.psum_tensor("psO", [128, 512], F32))

        ypad_d = nc.dram_tensor("ypad_d", [WID, B * PADHW + 64], F32)
        x_v = x.rearrange("(t b) (h p) w -> t p h b w", b=IMGS, h=2)
        out_v = out.rearrange("(t b) (h p) w -> t p h b w", b=IMGS, h=2)

        s_const = sem("s_const")
        s_go = sem("s_go")

        def wait_alone(eng, s, value):
            if isinstance(value, int):
                wait(eng, s, value)
            else:
                count = eng.snap(eng.to_reg(value))
                eng.wait_ge(s_go, 1)
                eng.wait_ge(s, count)

        def dma_x(eng, t, n, u, free, need, landed):
            wait(eng, free, need)
            for h in range(2):
                src = x_v[t:t + 1] if isinstance(t, int) else x_v[bass.ds(t, 1)]
                eng.dma_start(xs[:, u, h].rearrange("p (b w) -> p b w", b=IMGS),
                              src[0, :, h]).then_inc(landed[u], 16)

        s_set = sem("s_set")
        s_iota = sem("s_iota")
        with nc.Block() as block:
            @block.sync
            def _(eng):
                eng.dma_start(inv[:], invts.partition_broadcast(128)).then_inc(s_const, 16)
                eng.dma_start(gb1[:], bn1).then_inc(s_const, 16)
                eng.dma_start(gb2[:], bn2).then_inc(s_const, 16)
                eng.dma_start(gb3[:], bn3.rearrange("(h p) k -> p h k", p=128)).then_inc(s_const, 16)
                eng.wait_ge(s_const, 64)

            @block.gpsimd
            def _(eng):
                eng.memset(mean_w[:], 1.0 / C)
                eng.memset(ones_c[:], 1.0)
                eng.memset(eps_c[:], EPS_LN_C)
                eng.memset(eps_t[:], EPS_LN_T)
                eng.memset(ident[:], 0.0)
                eng.memset(z_sel[:, 2], 1.0)
                eng.memset(z_sel[:, 0].rearrange("p (x g b) -> p x g b", g=2, b=8)[:, :, 0], 1.0)
                eng.memset(z_sel[:, 1].rearrange("p (x g b) -> p x g b", g=2, b=8)[:, :, 1], 1.0)
                eng.memset(z_sel[:, 0].rearrange("p (x g b) -> p x g b", g=2, b=8)[:, :, 1], 0.0)
                eng.memset(z_sel[:, 1].rearrange("p (x g b) -> p x g b", g=2, b=8)[:, :, 0], 0.0)
                eng.memset(b_sel[:], 0.0)
                eng.memset(second8[:], 1.0)
                eng.memset(second16[:], 1.0)
                eng.memset(ind[:], 1.0).then_inc(s_iota, 1)
                eng.wait_ge(s_iota, 1)
                eng.affine_select(out=ident[:], in_=ident[:], compare_op=ALU.not_equal, fill=1.0, base=0,
                                  pattern=[[-1, 128]], channel_multiplier=1)
                eng.affine_select(out=ind[:], in_=ind[:], compare_op=ALU.is_ge, fill=0.0, base=0,
                                  pattern=[[1, 1024]], channel_multiplier=-KC)
                zv = z_sel[:].rearrange("p j (x b) -> p (j x) b", b=8)
                eng.affine_select(out=zv, in_=zv, compare_op=ALU.is_ge, fill=0.0, base=0,
                                  pattern=[[0, 12], [-KC, 8]], channel_multiplier=1)
                eng.affine_select(out=second8[:], in_=second8[:], compare_op=ALU.is_ge, fill=0.0, base=-8,
                                  pattern=[[-16, 8]], channel_multiplier=1)
                eng.affine_select(out=second16[:], in_=second16[:], compare_op=ALU.is_ge, fill=0.0, base=-16,
                                  pattern=[[-32, 4]], channel_multiplier=1).then_inc(s_iota, 1)
                eng.wait_ge(s_iota, 2)
                eng.affine_select(out=ind[:], in_=ind[:], compare_op=ALU.is_ge, fill=0.0, base=KC - 1,
                                  pattern=[[-1, 1024]], channel_multiplier=KC)
                eng.affine_select(out=zv, in_=zv, compare_op=ALU.is_ge, fill=0.0, base=KC - 1,
                                  pattern=[[0, 12], [KC, 8]], channel_multiplier=-1)
                eng.affine_select(out=second8[:], in_=second8[:], compare_op=ALU.is_ge, fill=0.0, base=15,
                                  pattern=[[16, 8]], channel_multiplier=-1)
                eng.affine_select(out=second16[:], in_=second16[:], compare_op=ALU.is_ge, fill=0.0, base=31,
                                  pattern=[[32, 4]], channel_multiplier=-1).then_inc(s_iota, 1)
                bv = b_sel[:].rearrange("p g (a b) -> p g a b", b=KC)
                for r in range(16):
                    eng.wait_ge(s_iota, 3 + r)
                    eng.affine_select(out=bv, in_=bv, compare_op=ALU.not_equal, fill=1.0, base=-8 * r,
                                      pattern=[[0, 2], [-1, 8], [0, KC]], channel_multiplier=1).then_inc(s_iota, 1)
                eng.tensor_copy(ind_r[:], ind[:])
                eng.tensor_copy(ind_s[:], ind[:, 0:128])
                eng.tensor_copy(ones_r[:], ones_c[:].to_broadcast([128, 128]))

            @block.vector
            def _(eng):
                eng.wait_ge(s_const, 64)
                eng.tensor_scalar(inv2[:], inv[:], 2.0, None, ALU.mult).then_inc(s_set, 1)
                eng.wait_ge(s_set, 1)
                eng.tensor_scalar(inv[:], inv[:], -1.0, None, ALU.mult).then_inc(s_go, 1)
                eng.wait_ge(s_iota, 3)
                eng.tensor_reduce(in8[:, 1:2], second8[:], AX.X, ALU.max)
                eng.tensor_reduce(lows[:], second16[:], AX.X, ALU.max).then_inc(s_set, 1)
                eng.wait_ge(s_set, 2)
                eng.tensor_scalar(lows[:], lows[:], -1.0, None, ALU.mult)
                eng.tensor_scalar(in8[:, 0:1], in8[:, 1:2], -1.0, 1.0, ALU.mult, ALU.add).then_inc(s_set, 1)
                eng.wait_ge(s_set, 3)
                eng.wait_ge(s_iota, 19)
                for g in range(2):
                    eng.tensor_scalar(b_sel_r[:, g], b_sel[:, g], in8[:, g:g + 1], None, ALU.mult)

            @block.scalar
            def _(eng):
                eng.preload_act_table_set("natural_log_exp_and_others")

        class Norm:

            def __init__(self, name, eps, bank=None):
                self.eps = eps
                self.bank = psM[:] if bank is None else bank
                self.mean, self.dev, self.sqr, self.var, self.log, self.rstd, self.done = (
                    sem(f"{name}_{x}") for x in ("mean", "dev", "sqr", "var", "log", "rstd", "done"))

            def pe_mean(self, eng, t, src):
                for h in range(2):
                    m = eng.matmul(self.bank[:, 0:CH], mean_w[:], src[:, h], start=(h == 0), stop=(h == 1))
                m.then_inc(self.mean, 1)

            def dve_dev(self, eng, t, src, dst):
                wait_alone(eng, self.mean, t + 1)
                eng.tensor_tensor(dst, src, self.bank[:, 0:CH].unsqueeze(1).to_broadcast([128, 2, CH]),
                                  ALU.subtract).then_inc(self.dev, 1)

            def act_square(self, eng, t, d):
                wait(eng, self.dev, t + 1)
                eng.activation(sq[:], d, ACT.Square).then_inc(self.sqr, 1)

            def pe_var(self, eng, t):
                wait(eng, self.sqr, t + 1)
                for h in range(2):
                    m = eng.matmul(self.bank[:, 0:CH], mean_w[:], sq[:, h], start=(h == 0), stop=(h == 1))
                m.then_inc(self.var, 1)

            def act_rstd(self, eng, t):
                wait(eng, self.var, t + 1)
                wait(eng, self.done, t)
                eng.activation(rs[:], self.bank[:, 0:CH], ACT.Ln, bias=self.eps[:, 0:1]).then_inc(self.log, 1)
                wait(eng, self.log, t + 1)
                eng.activation(rs[:], rs[:], ACT.Exp, scale=-0.5).then_inc(self.rstd, 1)

            def dve_norm(self, eng, t, d, dst):
                wait_alone(eng, self.rstd, t + 1)
                return eng.tensor_tensor(dst, d, rs[:].unsqueeze(1).to_broadcast([128, 2, CH]), ALU.mult)

        def amm(name, J, KP, ncb, O, which, cT, lut, blocks, extent, n_scores, t_scores, prep, out_half, n0=2, b0=3, SR=SUB):
            cols = ncb * KC
            with phase() as c2:
                def sb2(n, shape, dt=F32):
                    return c2.enter_context(nc.sbuf_tensor(f"{name}_{n}", shape, dt))

                cen = sb2("cen", [KP, blocks, KC])
                per = cols // blocks // KC
                wb = sb2("wb", [KP, blocks, per, KC])
                cb = sb2("cb", [KP, blocks, per, KC])
                wb_r = sb2("wb_r", [KP, blocks, per * KC], F32R)
                cb_r = sb2("cb_r", [KP, blocks, per * KC], F32R)
                lut_s = sb2("lut_s", [128, J, O])
                bias_t = sb2("bias_t", [128, J])
                mem = prep["memory"](sb2)
                exs = mem["exs"]
                S = {x: sem(f"{name}_{x}") for x in (
                    "cen", "w", "bias", "src", "nsc", "max", "tr", "nmt", "sc", "exp", "z", "rec", "hi", "inv",
                    "bc", "mul", "lut", "out", "relu", "vst")}
                ld = [sem(f"{name}_ld{u}") for u in range(2)]
                norm = Norm(name, eps_c, psZ[:, 1]) if prep.get("norm") else None
                env = dict(S=S, ld=ld, norm=norm, mem=mem)

                with nc.Block() as block:
                    @block.sync
                    def _(eng):
                        eng.dma_start(cen[:], cT).then_inc(S["cen"], 16)
                        eng.dma_start(lut_s[:], lut.rearrange("(j p) o -> p j o", p=128)).then_inc(S["cen"], 16)
                        eng.wait_ge(S["cen"], 32)

                    @block.vector
                    def _(eng):
                        eng.memset(nmT[:].bitcast(F32), 0.0)
                        eng.wait_ge(S["cen"], 32)
                        for b in range(blocks):
                            cin = cen[:, b].unsqueeze(1).to_broadcast([KP, per, KC])
                            eng.tensor_scalar(wb[:, b], cin, inv2[0:KP, which:which + 1], None, ALU.mult)
                            m = eng.tensor_tensor(cb[:, b], cin, cin, ALU.mult)
                        m.then_inc(S["w"], 1)
                        eng.wait_ge(S["w"], 1)
                        eng.tensor_scalar(cb[:], cb[:], inv[0:KP, which:which + 1], None, ALU.mult).then_inc(S["w"], 1)
                        eng.wait_ge(S["w"], 4)
                        eng.tensor_copy(wb_r[:], wb[:].rearrange("p b a k -> p b (a k)"))
                        eng.tensor_copy(cb_r[:], cb[:].rearrange("p b a k -> p b (a k)")).then_inc(S["w"], 1)
                        eng.wait_ge(S["bias"], 1)
                        eng.tensor_copy(bias_t[:], psO[:, 0:J]).then_inc(S["bias"], 1)

                    @block.gpsimd
                    def _(eng):
                        eng.wait_ge(S["w"], 2)
                        for w_ in (wb, cb):
                            for b in range(blocks):
                                m = eng.affine_select(out=w_[:, b], in_=w_[:, b], compare_op=ALU.is_ge, fill=0.0,
                                                      base=0, pattern=[[-extent, per], [0, KC]],
                                                      channel_multiplier=1)
                        m.then_inc(S["w"], 1)
                        eng.wait_ge(S["w"], 3)
                        for w_ in (wb, cb):
                            for b in range(blocks):
                                m = eng.affine_select(out=w_[:, b], in_=w_[:, b], compare_op=ALU.is_ge, fill=0.0,
                                                      base=extent - 1, pattern=[[extent, per], [0, KC]],
                                                      channel_multiplier=-1)
                        m.then_inc(S["w"], 1)

                    @block.tensor
                    def _(eng):
                        eng.wait_ge(S["w"], 4)
                        cbf = cb[:].rearrange("p b a k -> p (b a k)")
                        per_tile = 128
                        for j in range(J):
                            m = eng.matmul(psO[:, j:j + 1], cbf[:, j * per_tile:(j + 1) * per_tile],
                                           ones_c[0:KP, :], start=True, stop=True)
                        m.then_inc(S["bias"], 1)

                outs = [psO] if O <= 64 else [psO, psN[:, 1]]
                OP = min(O, 128)
                ZR = 32 * min(J, 4)
                trk = n0 + NSUB
                zk = max(trk + 2, J + 2)
                NBK = max(cols // 512, 1)
                slots = max(zk + 1, J + b0 + 1)

                with nc.Block() as block:
                    @block.sync
                    def _(eng):
                        if "sync" in prep:
                            staged(eng, lambda k, t, n, u: prep["sync"](eng, env, k, t, n, u), None, slots=slots)

                    @block.gpsimd
                    def _(eng):
                        if "pool" in prep:
                            staged(eng, lambda k, t, n, u: prep["pool"](eng, env, k, t, n, u), None, slots=slots)

                    @block.tensor
                    def _(eng):
                        def front(k, t, n, u):
                            if "pe" in prep:
                                prep["pe"](eng, env, k, t, n, u)
                            if n0 <= k < trk:
                                s = k - n0
                                if s == 0 and "landed" not in prep:
                                    wait_alone(eng, S["src"], t + 1)
                                products = list(n_scores(env, u, s))
                                for b, (dst, src, blk, lo, hi) in enumerate(products):
                                    bank, first = b * NBK // len(products), b * NBK % len(products) == 0
                                    if first:
                                        wait_alone(eng, S["max"], (t * NSUB + s - 1) * NBK + bank + 1)
                                    K = src.shape[0]
                                    eng.matmul(dst, src, wb_r[0:K, blk, lo:hi], start=True, stop=False)
                                    m = eng.matmul(dst, ones_r[0:K, 0:SR], cb_r[0:K, blk, lo:hi],
                                                   start=False, stop=True)
                                    if (b + 1) * NBK % len(products) == 0:
                                        m.then_inc(S["nsc"], 1)
                            if k == trk:
                                wait_alone(eng, S["max"], (t * NSUB + NSUB) * NBK)
                                wait_alone(eng, S["rec"], t - 1)
                                for s in range(NSUB):
                                    m = eng.transpose(psM[0:ncb, s * SR:(s + 1) * SR], nm[0:SR, s, 0:ncb],
                                                      ident[0:SR, 0:SR])
                                m.then_inc(S["tr"], 1)

                        def back(k, t, n, u):
                            if k < J:
                                g = t * J + k
                                if k == 0:
                                    wait_alone(eng, S["nmt"], t + 1)
                                    if "landed" in prep:
                                        wait_alone(eng, ld[u], (n + 1) * prep["landed"])
                                wait_alone(eng, S["exp"], g - 1)
                                w_, src = t_scores(env, wb, k, u)
                                eng.matmul(psS[:, k % 2, 0:CH], w_, src, start=True, stop=False)
                                eng.matmul(psS[:, k % 2, 0:CH], ind_r[:, k * 128:(k + 1) * 128],
                                           nmT[:, u, :], start=False, stop=True).then_inc(S["sc"], 1)
                            if k == zk:
                                wait_alone(eng, S["exp"], t * J + J)
                                wait_alone(eng, S["nmt"], min(t + 2, T) if isinstance(t, int) else t + 2)
                                for j in range(J):
                                    q = 32 * (j % 4)
                                    m = eng.matmul(psM[q:q + 32, 0:CH], z_sel[:, j // 4 if J > 4 else 2], exs[:, u, j],
                                                   start=(j < 4), stop=(j + 4 >= J), tile_position=(0, q))
                                m.then_inc(S["z"], 1)

                        def late(k, t, n, u):
                            if b0 <= k < J + b0:
                                j = k - b0
                                if j == 0:
                                    wait_alone(eng, S["inv"], t + 1)
                                if j == 1 and norm:
                                    wait_alone(eng, norm.log, min(t + 3, T) if isinstance(t, int) else t + 3)
                                wait_alone(eng, S["mul"], t * J + j - 1)
                                q = 32 * (j % 4)
                                eng.matmul(psZ[:, j % 2, 0:CH], b_sel_r[q:q + 32, j // 4], rS[q:q + 32],
                                           start=True, stop=True).then_inc(S["bc"], 1)
                            if b0 < k <= J + b0:
                                j = k - b0 - 1
                                wait_alone(eng, S["mul"], t * J + j + 1)
                                if j == 0:
                                    wait_alone(eng, S["out"], t)
                                for o, dst in enumerate(outs):
                                    m = eng.matmul(dst[0:OP, 0:CH], lut_s[:, j, o * 128:o * 128 + OP],
                                                   at[:, j % 2], start=(j == 0), stop=(j == J - 1))
                                m.then_inc(S["lut"], 1)
                        staged(eng, front, back, slots=slots, late=late)

                    @block.vector
                    def _(eng):
                        def front(k, t, n, u):
                            if "dve" in prep:
                                prep["dve"](eng, env, k, t, n, u)
                            if n0 <= k < trk:
                                s = k - n0
                                if s == 0:
                                    wait_alone(eng, S["tr"], t)
                                width = cols // NBK
                                for bank in range(NBK):
                                    wait_alone(eng, S["nsc"], (t * NSUB + s) * NBK + bank + 1)
                                    eng.tensor_reduce(nm[0:SR, s, bank * width // KC:(bank + 1) * width // KC],
                                                      psN[0:SR, bank, 0:width].rearrange("p (c k) -> p c k", k=KC), AX.X,
                                                      ALU.max, negate=True).then_inc(S["max"], 1)

                        def statistics(t):
                            wait_alone(eng, S["out"], t + 1)
                            for o in range(len(outs)):
                                oh = out_half if len(outs) == 1 else o
                                eng.bn_stats(stats[0:OP, o, at_chunk(t)], OUT[0:OP, oh, at_chunk(t)].squeeze(1))

                        def late(k, t, n, u):
                            if k == 0:
                                wait(eng, S["z"], t + 1)
                                eng.reciprocal(rz[0:ZR, 0], psM[0:ZR, 0:CH]).then_inc(S["rec"], 1)
                            if k == min(b0 - 2, 2):
                                wait_alone(eng, S["hi"], t + 1)
                                wait_alone(eng, S["bc"], t * J)
                                eng.scalar_tensor_tensor(out=rS[0:ZR], in0=rh[0:ZR].bitcast(F32), scalar=lows[0:ZR, 0:1],
                                                         in1=rz[0:ZR, 0], op0=ALU.mult, op1=ALU.add).then_inc(S["inv"], 1)
                            if b0 <= k < J + b0:
                                j = k - b0
                                wait(eng, S["bc"], t * J + j + 1)
                                wait(eng, S["lut"], t * J + j - 1)
                                eng.tensor_tensor(at[:, j % 2], exs[:, u, j], psZ[:, j % 2, 0:CH],
                                                  ALU.mult).then_inc(S["mul"], 1)
                            if k == 3 and not (isinstance(t, int) and t == 0):
                                statistics(t - 1)
                        staged(eng, front, None, slots=slots, late=late)
                        statistics(T - 1)

                    @block.scalar
                    def _(eng):
                        def front(k, t, n, u):
                            if "act" in prep:
                                prep["act"](eng, env, k, t, n, u)
                            if k == trk:
                                wait_alone(eng, S["tr"], t + 1)
                                wait_alone(eng, S["sc"], (t - 1) * J)
                                if SR == SUB:
                                    src, dst = psM[0:ncb, 0:CH], nmT[0:ncb, u]
                                else:
                                    src = psM[0:ncb, 0:NSUB * SR].rearrange("p (r w) -> p r w", w=PADW)[:, :, 0:HH]
                                    dst = nmT[0:ncb, u].rearrange("p (r w) -> p r w", w=HH)
                                eng.activation(dst, src, ACT.Copy).then_inc(S["nmt"], 1)

                        def back(k, t, n, u):
                            if k < J:
                                wait_alone(eng, S["sc"], t * J + k + 1)
                                if k == 0:
                                    wait_alone(eng, S["mul"], (t - 1) * J)
                                eng.activation(exs[:, u, k], psS[:, k % 2, 0:CH], ACT.Exp,
                                               bias=bias_t[:, k:k + 1]).then_inc(S["exp"], 1)

                        def late(k, t, n, u):
                            if k == min(b0 - 2, 2):
                                wait(eng, S["rec"], t + 1)
                                wait(eng, S["inv"], t)
                                eng.activation(rh[0:ZR], rz[0:ZR, 0], ACT.Copy).then_inc(S["hi"], 1)
                            if k == J + b0:
                                wait_alone(eng, S["lut"], t * J + J)
                                for o, dst in enumerate(outs):
                                    oh = out_half if len(outs) == 1 else o
                                    m = eng.activation(OUT[0:OP, oh, at_chunk(t)], dst[0:OP, 0:CH].unsqueeze(1), ACT.Copy)
                                m.then_inc(S["out"], 1)
                        staged(eng, front, back, slots=slots, late=late)

        def bn_coefs(name, halves, P, gb):
            s = sem(f"{name}_bn")
            with nc.Block() as block:
                @block.vector
                def _(eng):
                    for h in range(halves):
                        m = eng.bn_aggr(aggr[0:P, h], stats[0:P, h].rearrange("p t k -> p (t k)"))
                    m.then_inc(s, 1)
                    eng.wait_ge(s, 3)
                    g = gb[0:P].unsqueeze(1) if halves == 1 else gb[:]
                    eng.tensor_tensor(bns[0:P, 0:halves], bnt[0:P, 0:halves], g[:, :, 0], ALU.mult).then_inc(s, 1)
                    eng.wait_ge(s, 4)
                    eng.tensor_tensor(bnt[0:P, 0:halves], aggr[0:P, 0:halves, 0], bns[0:P, 0:halves],
                                      ALU.mult).then_inc(s, 1)
                    eng.wait_ge(s, 5)
                    eng.tensor_tensor(bnb[0:P, 0:halves], g[:, :, 1], bnt[0:P, 0:halves], ALU.subtract).then_inc(s, 1)

                @block.scalar
                def _(eng):
                    eng.wait_ge(s, 1)
                    eng.activation(bnt[0:P, 0:halves], aggr[0:P, 0:halves, 1], ACT.Ln,
                                   bias=eps_t[0:P, 0:1]).then_inc(s, 1)
                    eng.wait_ge(s, 2)
                    eng.activation(bnt[0:P, 0:halves], bnt[0:P, 0:halves], ACT.Exp, scale=-0.5).then_inc(s, 1)

        def a_sync(eng, env, k, t, n, u):
            if k == 0:
                dma_x(eng, t, n, u, env["norm"].dev, t - 1, env["ld"])

        def a_pe(eng, env, k, t, n, u):
            if k == 0:
                wait(eng, env["ld"][u], (n + 1) * 32)
                wait(eng, env["S"]["mul"], (t - 2) * 8)
                env["norm"].pe_mean(eng, t, xs[:, u])
            if k == 2:
                env["norm"].pe_var(eng, t)

        def a_dve(eng, env, k, t, n, u):
            if k == 0:
                wait_alone(eng, env["S"]["sc"], (t - 1) * 8)
                wait_alone(eng, env["S"]["vst"], t - 1)
                env["norm"].dve_dev(eng, t, xs[:, u], vv[:, u])
            if k == 2:
                env["norm"].dve_norm(eng, t, vv[:, u], vv[:, u]).then_inc(env["norm"].done, 1)

        def a_act(eng, env, k, t, n, u):
            if k == 0:
                wait(eng, env["norm"].var, t)
                env["norm"].act_square(eng, t, vv[:, u])
            if k == 2:
                env["norm"].act_rstd(eng, t)

        def a_pool(eng, env, k, t, n, u):
            if k == 2:
                wait_alone(eng, env["norm"].done, t + 1)
                wait_alone(eng, env["S"]["nsc"], t * NSUB * 2)
                eng.tensor_copy(vr[:], vv[:, u]).then_inc(env["S"]["src"], 1)
                eng.tensor_copy(V[:, :, at_chunk(t)].rearrange("p h t c -> p h (t c)"), vv[:, u]).then_inc(env["S"]["vst"], 1)

        def a_n(env, u, s):
            for b in range(2):
                yield (psN[0:SUB, b, :], vr[:, b, s * SUB:(s + 1) * SUB], b, 0, 512)

        def a_t(env, wb, j, u):
            q = 32 * (j % 4)
            w_ = wb[:].rearrange("p b a k -> p b (a k)")[q:q + 32, j // 4, (j % 4) * 128:(j % 4) * 128 + 128]
            return w_, vv[q:q + 32, u, j // 4, :]

        amm("a", 8, 128, 64, WID, 0, c1T.rearrange("(h p) k -> p h k", p=128), lut1, 2, 4, a_n, a_t,
            dict(memory=lambda sb2: dict(exs=sb2("exs", [128, 2, 8, CH])), norm=True, sync=a_sync, pe=a_pe, dve=a_dve, act=a_act, pool=a_pool), 0, n0=8, b0=6)
        bn_coefs("a", 1, WID, gb1)

        ypad_rd = nc.dram_tensor("ypad_rd", [WID, B * PADHW + 64], F32)
        ypad_r = BIG[0:WID, T * CH:T * CH + B * PADHW].bitcast(F32R)
        with nc.sbuf_tensor("ypad", [WID, B, PADW, PADW], F32) as ypad:
            s_pad0, s_pad, s_padst = sem("s_pad0"), sem("s_pad"), sem("s_padst")
            with nc.Block() as block:
                @block.vector
                def _(eng):
                    eng.memset(ypad[:], 0.0).then_inc(s_pad0, 1)

                    quarter = B // 4 * PADHW
                    for q in range(4):
                        eng.wait_ge(s_pad, q + 1)
                        cols = slice(q * quarter, (q + 1) * quarter)
                        m = eng.tensor_copy(ypad_r[:, cols], ypad[:].rearrange("p b r w -> p (b r w)")[:, cols])
                    m.then_inc(s_pad0, 1)

                @block.scalar
                def _(eng):
                    eng.wait_ge(s_pad0, 1)
                    for t in range(T):
                        src = OUT[0:WID, 0, t].rearrange("p (b r w) -> p b r w", b=IMGS, r=HH)
                        for b in range(IMGS):
                            m = eng.activation(ypad[:, t * IMGS + b, 1:1 + HH, 1:1 + HH], src[:, b], ACT.Relu,
                                               bias=bnb[0:WID, 0:1], scale=bns[0:WID, 0:1])
                        if t % 4 == 3:
                            m.then_inc(s_pad, 1)

                @block.sync
                def _(eng):
                    eng.wait_ge(s_pad, 4)
                    flat = ypad[:].rearrange("p b r w -> p (b r w)")
                    eng.dma_start(ypad_d.ap()[:, 0:B * PADHW], flat).then_inc(s_padst, 16)
                    eng.dma_start(ypad_d.ap()[:, B * PADHW:], flat[:, 0:64]).then_inc(s_padst, 16)
                    eng.wait_ge(s_pad0, 2)
                    eng.dma_start(ypad_rd.ap()[:, 0:B * PADHW], ypad_r.bitcast(F32)).then_inc(s_padst, 16)
                    eng.dma_start(ypad_rd.ap()[:, B * PADHW:], ypad_r[:, 0:64].bitcast(F32)).then_inc(s_padst, 16)
                    eng.wait_ge(s_padst, 64)

        def b_memory(sb2):
            size = 8 * IMGS * HH * PADW
            exs = OUT[:, 0].rearrange("p (a j) c -> p a j c", a=2)
            free = BIG[0:72, 2 * T * CH:2 * T * CH + size].rearrange("p (g c) -> p g c", g=8)
            return dict(exs=exs, pat=[free, sb2("pat", [72, 8, IMGS * HH * PADW])], pat_r=sb2("pat_r", [72, 8, IMGS * HH * PADW], F32R))

        def b_load(eng, t, src_d, dst, landed):
            for tap in range(9):
                off = (tap // 3) * PADW + tap % 3
                src = src_d.ap()[:, off:off + B * PADHW].rearrange("(g c) (t b r) -> t c g b r", g=8, b=IMGS, r=PADHW)
                src = src[at_chunk(t)][0]
                for b in range(IMGS):
                    eng.dma_start(dst[tap:tap + 64:9, :, b * HH * PADW:(b + 1) * HH * PADW],
                                  src[:, :, b, 0:HH * PADW]).then_inc(landed, 16)

        def b_sync(eng, env, k, t, n, u):
            if k == 0:
                wait(eng, env["S"]["nsc"], t * NSUB * 2)
                b_load(eng, t, ypad_rd, env["mem"]["pat_r"][:].bitcast(F32), env["S"]["src"])
                wait(eng, env["S"]["sc"], (t - 1) * 8)
                b_load(eng, t, ypad_d, env["mem"]["pat"][u], env["ld"][u])

        def b_pe(eng, env, k, t, n, u):
            if k == 4:
                wait_alone(eng, env["S"]["src"], (t + 1) * 16 * 9 * IMGS)

        def b_n(env, u, s):
            flat = psN[0:7 * PADW].rearrange("p a b -> p (a b)")
            for g in range(8):
                v = env["mem"]["pat_r"][:, g, s * 7 * PADW:(s + 1) * 7 * PADW]
                yield (flat[:, g * 128:(g + 1) * 128], v, g, 0, 128)

        def b_t(env, wb, j, u):
            v = env["mem"]["pat"][u][:, j].rearrange("p (r w) -> p r w", w=PADW)[:, :, 0:HH]
            return wb[:, j].rearrange("p a k -> p (a k)"), v

        amm("b", 8, 72, 64, WID, 1, c2T, lut2, 8, 9, b_n, b_t,
            dict(memory=b_memory, sync=b_sync, pe=b_pe, landed=16 * 9 * IMGS), 1, n0=4, b0=6, SR=7 * PADW)
        bn_coefs("b", 1, WID, gb2)

        def c_memory(sb2):
            return dict(exs=sb2("exs", [128, 2, 2, CH]), y=sb2("y", [WID, 2, CH]), y_r=sb2("y_r", [WID, CH], F32R))

        def c_act(eng, env, k, t, n, u):
            if k == 0:
                wait_alone(eng, env["S"]["sc"], (t - 1) * 2)
                ts = slice(t, t + 1) if isinstance(t, int) else bass.ds(t, 1)
                eng.activation(env["mem"]["y"][:, u], OUT[0:WID, 1, ts].rearrange("p t c -> p (t c)"), ACT.Relu,
                               bias=bnb[0:WID, 0:1], scale=bns[0:WID, 0:1]).then_inc(env["S"]["relu"], 1)

        def c_pool(eng, env, k, t, n, u):
            if k == 1:
                wait_alone(eng, env["S"]["relu"], t + 1)
                wait_alone(eng, env["S"]["nsc"], t * NSUB)
                eng.tensor_copy(env["mem"]["y_r"][:], env["mem"]["y"][:, u]).then_inc(env["S"]["src"], 1)

        def c_n(env, u, s):
            yield (psN[0:SUB, 0, 0:256], env["mem"]["y_r"][:, s * SUB:(s + 1) * SUB], 0, 0, 256)

        def c_t(env, wb, j, u):
            w_ = wb[:].rearrange("p b a k -> p (b a k)")[32 * j:32 * j + 32, j * 128:(j + 1) * 128]
            return w_, env["mem"]["y"][32 * j:32 * j + 32, u]

        amm("c", 2, 64, 16, C, 2, c3T.rearrange("p (b k) -> p b k", b=1), lut3, 1, 4, c_n, c_t,
            dict(memory=c_memory, act=c_act, pool=c_pool), 0, n0=2, b0=4)
        bn_coefs("c", 2, 128, gb3)

        NT = T * NSUB
        ROWS = 128
        TILES = -(-2 * B * HW // ROWS) + E0
        TILES += -TILES % 4
        ZQ = 4 * T
        ZF = TILES * ROWS * C // (ZQ * 128)
        xn_d = nc.dram_tensor("xn_d", [NT * SUB, C], F32)
        xg_d = nc.dram_tensor("xg_d", [TILES * ROWS, C], F32)
        yg_d = nc.dram_tensor("yg_d", [TILES * ROWS, C], F32)
        d_ctx = phase()

        def sbd(name, shape, dt=F32):
            return d_ctx.enter_context(nc.sbuf_tensor(name, shape, dt))
        w_moe_s = BIG
        router_s = sbd("router_s", [128, 2, E0])
        before = sbd("before", [SUB, SUB])
        before_r = sbd("before_r", [SUB, SUB], F32R)
        iota_i = sbd("iota_i", [SUB, 192], U32)
        rev = sbd("rev", [SUB, E0])
        xnb = sbd("xnb", [SUB, 2, NSUB, C])
        dl = sbd("dl", [SUB, NSUB, E0])
        mx = sbd("mx", [SUB, NSUB])
        EXA = sbd("EXA", [SUB, NT, E0])
        sc_ = sbd("sc_", [SUB, 6, NT])
        P12 = sbd("P12", [SUB, NT, 2])
        MASK = sbd("MASK", [SUB, NT * E0], F32R)
        zeros = sbd("zeros", [128, ZF])
        SLOT = sbd("SLOT", [SUB, NT, 2], U32)
        EID = sbd("EID", [SUB, TILES], U32)

        pre = [at[:], rz[:]]
        dn = Norm("d", eps_t)
        D = {k: sem(f"d_{k}") for k in ("w", "set", "pre", "relu", "x1", "tr", "ev", "lgd", "max", "dl",
                                        "exp", "pfx", "mid", "zf")}
        d_ld = [sem(f"d_ld{u}") for u in range(2)]
        d_xst = [sem(f"d_xst{u}") for u in range(2)]
        with nc.Block() as block:
            @block.sync
            def _(eng):
                eng.dma_start(router_s[:], routerT.rearrange("(h p) e -> p h e", p=128)).then_inc(D["w"], 16)
                eng.wait_ge(D["w"], 16)

            @block.gpsimd
            def _(eng):
                eng.memset(zeros[:], 0.0)
                eng.memset(before[:], 1.0).then_inc(D["set"], 1)
                eng.iota(iota_i[:, 0:E0], pattern=[[-1, E0]], base=E0, channel_multiplier=0).then_inc(D["set"], 1)
                eng.wait_ge(D["set"], 2)
                eng.affine_select(out=before[:], in_=before[:], compare_op=ALU.is_ge, fill=0.0, base=-1,
                                  pattern=[[1, SUB]], channel_multiplier=-1).then_inc(D["set"], 1)
                eng.tensor_copy(rev[:], iota_i[:, 0:E0])
                eng.wait_ge(D["set"], 3)
                eng.tensor_copy(before_r[:], before[:])

        with nc.Block() as block:
            @block.sync
            def _(eng):
                def front(k, t, n, u):
                    if k == 0:
                        dma_x(eng, t, n, u, D["x1"], t - 1, d_ld)
                        pieces = xg_d.ap().rearrange("r c -> (r c)").rearrange("(t q p f) -> t p q f", t=T, q=4, p=128)
                        for q in range(4):
                            eng.dma_start(pieces[at_chunk(t)][0, :, q], zeros[:]).then_inc(D["zf"], 16)

                def late(k, t, n, u):
                    if k == 4:
                        wait(eng, D["ev"], t * NSUB + NSUB)
                        dst = xn_d.ap().rearrange("(t s p) c -> t p s c", p=SUB, s=NSUB)[at_chunk(t)][0]
                        eng.dma_start(dst, xnb[:, u]).then_inc(d_xst[u], 16)
                staged(eng, front, None, slots=5, late=late)
                eng.wait_ge(D["zf"], ZQ * 16)
                for u in range(2):
                    eng.wait_ge(d_xst[u], T // 2 * 16)

            @block.vector
            def _(eng):
                def front(k, t, n, u):
                    ts = at_chunk(t)
                    if k == 0:
                        for h in range(2):
                            m = eng.scalar_tensor_tensor(out=pre[u][:, h], in0=OUT[:, h, ts].squeeze(1), scalar=bns[:, h:h + 1],
                                                         in1=V[:, h, ts].squeeze(1), op0=ALU.mult, op1=ALU.add)
                        m.then_inc(D["pre"], 1)
                    if k == 1:
                        wait_alone(eng, d_ld[u], (n + 1) * 32)
                        wait_alone(eng, D["relu"], t + 1)
                        eng.tensor_tensor(chunk_of(V, t), xs[:, u], pre[u], ALU.add).then_inc(D["x1"], 1)

                def back(k, t, n, u):
                    if k == 0:
                        wait_alone(eng, D["lgd"], t - 1)
                        dn.dve_dev(eng, t, chunk_of(V, t), vv[:, u])
                    if k == 2:
                        dn.dve_norm(eng, t, vv[:, u], vv[:, u]).then_inc(dn.done, 1)

                def late(k, t, n, u):
                    if k == 4:
                        wait_alone(eng, D["lgd"], t + 1)
                        wait_alone(eng, D["exp"], t)
                        lgs = psN[0:SUB, 0, 0:NSUB * E0].rearrange("p (s e) -> p s e", s=NSUB)
                        eng.tensor_reduce(mx[:], lgs, AX.X, ALU.max).then_inc(D["max"], 1)
                        wait_alone(eng, D["max"], t + 1)
                        eng.tensor_tensor(dl[:], lgs, mx[:].unsqueeze(2).to_broadcast([SUB, NSUB, E0]),
                                          ALU.subtract).then_inc(D["dl"], 1)
                staged(eng, front, back, slots=5, late=late)

            @block.scalar
            def _(eng):
                def front(k, t, n, u):
                    if k == 0:
                        wait(eng, D["pre"], t + 1)
                        for h in range(2):
                            m = eng.activation(pre[u][:, h], pre[u][:, h], ACT.Relu, bias=bnb[:, h:h + 1])
                        m.then_inc(D["relu"], 1)

                def back(k, t, n, u):
                    if k == 0:
                        wait(eng, dn.var, t)
                        dn.act_square(eng, t, vv[:, u])
                    if k == 1:
                        dn.act_rstd(eng, t)

                def late(k, t, n, u):
                    if k < NSUB:
                        wait(eng, D["tr"], t * NSUB + k + 1)
                        if k == 0:
                            wait(eng, d_xst[u], n * 16)
                        eng.activation(xnb[:, u, k], psS[0:SUB, k % 2, 0:C], ACT.Copy).then_inc(D["ev"], 1)
                    if k == 4:
                        wait_alone(eng, D["dl"], t + 1)
                        eng.activation(EXA[:, at_chunk(t, NSUB)], dl[:], ACT.Exp).then_inc(D["exp"], 1)
                staged(eng, front, back, slots=5, late=late)

            @block.tensor
            def _(eng):
                def back(k, t, n, u):
                    if k == 0:
                        wait_alone(eng, D["x1"], t + 1)
                        wait_alone(eng, dn.log, t)
                        dn.pe_mean(eng, t, chunk_of(V, t))
                    if k == 1:
                        dn.pe_var(eng, t)

                def late(k, t, n, u):
                    if k < NSUB:
                        s = k
                        if s == 0:
                            wait_alone(eng, dn.done, t + 1)
                            wait_alone(eng, D["dl"], t)
                        wait_alone(eng, D["ev"], t * NSUB + s - 1)
                        sub = slice(s * SUB, (s + 1) * SUB)
                        for h in range(2):
                            m = eng.transpose(psS[0:SUB, s % 2, h * 128:(h + 1) * 128], vv[:, u, h, sub], ident[:])
                        m.then_inc(D["tr"], 1)
                        for h in range(2):
                            m = eng.matmul(psN[0:SUB, 0, s * E0:(s + 1) * E0], vv[:, u, h, sub], router_s[:, h],
                                           start=(h == 0), stop=(h == 1))
                        if s == NSUB - 1:
                            m.then_inc(D["lgd"], 1)
                staged(eng, None, back, slots=5, late=late)

        NK = B * HW // ROWS + 1
        W = NT * E0

        def area(i):
            return BIG[0:SUB, i * W:(i + 1) * W]
        A, M1, SCAN, M2 = (area(i).rearrange("p (t e) -> p t e", e=E0) for i in range(4))
        NB = W // 512
        TB = NT // NB
        within = [psN[0:SUB, 0], psN[0:SUB, 1], psS[0:SUB, 0], psS[0:SUB, 1]]
        total = [psZ[0:SUB, 0], psZ[0:SUB, 1], psM[0:SUB, :], psO[0:SUB, :]]
        with nc.Block() as block:
            @block.tensor
            def _(eng):
                eng.wait_ge(D["mid"], 12)
                for g in range(NB):
                    eng.matmul(within[g], before_r[:], MASK[:, g * 512:(g + 1) * 512], start=True, stop=True)
                    m = eng.matmul(total[g], ones_r[0:SUB, 0:SUB], MASK[:, g * 512:(g + 1) * 512], start=True, stop=True)
                m.then_inc(D["pfx"], 1)

            @block.gpsimd
            def _(eng):
                eng.iota(iota_i[:, 0:NK], pattern=[[ROWS, NK]], base=0, channel_multiplier=0)
                eng.iota(iota_i[:, NK:NK + TILES], pattern=[[1, TILES]], base=0, channel_multiplier=0).then_inc(D["set"], 1)

            @block.vector
            def _(eng):
                count = [0]

                def step(ins):
                    ins.then_inc(D["mid"], 1)
                    count[0] += 1
                    eng.wait_ge(D["mid"], count[0])

                def many(i):
                    return sc_[:, i].unsqueeze(2).to_broadcast([SUB, NT, E0])
                revb = rev[:].unsqueeze(1).to_broadcast([SUB, NT, E0])
                eng.tensor_reduce(sc_[:, 4], EXA[:], AX.X, ALU.add)
                for j, (src, mask) in enumerate(((EXA[:], M1), (SCAN, M2))):
                    step(eng.tensor_reduce(sc_[:, j], src, AX.X, ALU.max))
                    step(eng.tensor_tensor(A, src, many(j), ALU.is_equal))
                    step(eng.tensor_tensor(A, A, revb, ALU.mult))
                    step(eng.tensor_reduce(sc_[:, 2 + j], A, AX.X, ALU.max))
                    step(eng.tensor_tensor(mask, A, many(2 + j), ALU.is_equal))
                    if j == 0:
                        step(eng.scalar_tensor_tensor(out=SCAN, in0=M1, scalar=NEG, in1=EXA[:], op0=ALU.mult, op1=ALU.add))
                step(eng.tensor_tensor(MASK[:].rearrange("p (t e) -> p t e", e=E0), M1, M2, ALU.add))
                assert count[0] == 12
                step(eng.reciprocal(sc_[:, 5], sc_[:, 4]))
                for j in range(2):
                    eng.tensor_tensor(P12[:, :, j], sc_[:, j], sc_[:, 5], ALU.mult)
                eng.memset(A[:, 0], 0.0)
                eng.wait_ge(D["pfx"], 1)
                for g in range(NB):
                    last = TB - 1 if g == NB - 1 else TB
                    m = eng.tensor_copy(A[:, g * TB + 1:g * TB + 1 + last].rearrange("p t e -> p (t e)"), total[g][:, 0:last * E0])
                step(m)
                src, dst, d = A, SCAN, 1
                while d < NT:
                    eng.tensor_copy(dst[:, 0:d], src[:, 0:d])
                    step(eng.tensor_tensor(dst[:, d:], src[:, d:], src[:, 0:NT - d], ALU.add))
                    src, dst, d = dst, src, 2 * d
                seen, pos = src, dst
                free = 4 * W
                cnt, tl, base, ends = (BIG[0:SUB, free + 32 * i:free + 32 * i + 32] for i in range(4))
                steps_k = BIG[0:SUB, free + 128:free + 128 + NK + TILES]
                lower = BIG[0:SUB, free + 512:free + 512 + E0 * E0].rearrange("p (a b) -> p a b", a=E0)
                big = BIG[0:SUB, free + 512 + E0 * E0:free + 512 + E0 * E0 + E0 * TILES]
                eng.wait_ge(D["set"], 4)
                step(eng.tensor_tensor(cnt, seen[:, NT - 1], total[-1][:, 512 - E0:512], ALU.add))
                step(eng.tensor_copy(steps_k, iota_i[:, 0:NK + TILES]))
                b1_ = big[:, 0:E0 * NK].rearrange("p (e k) -> p e k", e=E0)
                step(eng.tensor_tensor(b1_, cnt.unsqueeze(2).to_broadcast([SUB, E0, NK]),
                                       steps_k[:, 0:NK].unsqueeze(1).to_broadcast([SUB, E0, NK]), ALU.is_gt))
                step(eng.tensor_reduce(tl, b1_, AX.X, ALU.add))
                step(eng.tensor_tensor(lower, rev[:].unsqueeze(1).to_broadcast([SUB, E0, E0]),
                                       rev[:].unsqueeze(2).to_broadcast([SUB, E0, E0]), ALU.is_gt))
                step(eng.tensor_tensor(lower, lower, tl.unsqueeze(1).to_broadcast([SUB, E0, E0]), ALU.mult))
                step(eng.tensor_reduce(base, lower, AX.X, ALU.add))
                step(eng.tensor_tensor(ends, base, tl, ALU.add))
                step(eng.tensor_scalar(base, base, float(ROWS), None, ALU.mult))
                b2_ = big.rearrange("p (t e) -> p t e", e=E0)
                step(eng.tensor_tensor(b2_, ends.unsqueeze(1).to_broadcast([SUB, TILES, E0]),
                                       steps_k[:, NK:NK + TILES].unsqueeze(2).to_broadcast([SUB, TILES, E0]), ALU.is_le))
                te = steps_k[:, 0:TILES]
                step(eng.tensor_reduce(te, b2_, AX.X, ALU.add))
                step(eng.tensor_scalar(te, te, float(E0 - 1), None, ALU.min))
                step(eng.tensor_copy(EID[:], te))
                for g in range(NB):
                    part = slice(g * TB, (g + 1) * TB)
                    m = eng.tensor_tensor(pos[:, part], seen[:, part], within[g].rearrange("p (t e) -> p t e", e=E0), ALU.add)
                step(m)
                step(eng.tensor_tensor(pos, pos, base.unsqueeze(1).to_broadcast([SUB, NT, E0]), ALU.add))
                for j, mask in enumerate((M1, M2)):
                    step(eng.tensor_tensor(mask, mask, pos, ALU.mult))
                    step(eng.tensor_reduce(sc_[:, j], mask, AX.X, ALU.add))
                    step(eng.tensor_copy(SLOT[:, :, j], sc_[:, j]))

        G = {k: sem(f"g_{k}") for k in ("ix",)}
        g_ld = [sem(f"g_ld{u}") for u in range(2)]
        g_sc = [sem(f"g_sc{u}") for u in range(2)]
        idx = sbd("idx", [SUB, 2, NSUB * 2], U32)
        pc = sbd("pc", [SUB, 2, NSUB * 2])
        with nc.Block() as block:
            @block.scalar
            def _(eng):
                for q in range(16):
                    eng.dma_start(w_moe_s[:].rearrange("p (e h c) -> p e h c", e=E0, h=2)[:, 2 * q:2 * q + 2],
                                  w_moe[2 * q:2 * q + 2].rearrange("e (h p) c -> p e h c", p=128)).then_inc(D["w"], 16)
                eng.wait_ge(D["w"], 17 * 16)

            @block.vector
            def _(eng):
                def front(k, t, n, u):
                    if k == 0:
                        wait_alone(eng, g_sc[u], n * 16 * NSUB * 2)
                        eng.tensor_copy(idx[:, u], SLOT[:, at_chunk(t, NSUB)].rearrange("p t j -> p (t j)")).then_inc(G["ix"], 1)
                staged(eng, front, None, slots=1)

            @block.sync
            def _(eng):
                def front(k, t, n, u):
                    if k == 0:
                        wait(eng, g_sc[u], n * 16 * NSUB * 2)
                        src = xn_d.ap().rearrange("(t s p) c -> t p s c", p=SUB, s=NSUB)[at_chunk(t)][0]
                        eng.dma_start(xnb[:, u], src).then_inc(g_ld[u], 16)
                staged(eng, front, None, slots=1)

            @block.gpsimd
            def _(eng):
                def front(k, t, n, u):
                    if k == 0:
                        wait_alone(eng, G["ix"], t + 1)
                        wait_alone(eng, g_ld[u], (n + 1) * 16)
                        for s in range(NSUB):
                            for j in range(2):
                                eng.indirect_dma_start(
                                    xg_d.ap(), bass.IndirectOffsetOnAxis(ap=idx[:, u, 2 * s + j:2 * s + j + 1], axis=0),
                                    xnb[:, u, s], None).then_inc(g_sc[u], 16)
                staged(eng, front, None, slots=1)
                for u in range(2):
                    eng.wait_ge(g_sc[u], T // 2 * 16 * NSUB * 2)

        X = {k: sem(f"x_{k}") for k in ("tr", "ev", "mm", "y")}
        x_ld = [sem(f"x_ld{u}") for u in range(2)]
        x_st = [sem(f"x_st{u}") for u in range(2)]
        PAIRS = TILES // 2
        xr = vv[:].rearrange("p u h c -> p (u h c)")[:, 0:4 * C].rearrange("p (u r c) -> p u r c", u=2, r=2)
        xt = xs[:].rearrange("p u h c -> p (u h c)")[:, 0:4 * C].rearrange("p (u r c) -> p u r c", u=2, r=2)
        yr = [b[:].rearrange("p h c -> p (h c)")[:, 0:2 * C] for b in (ex, sq)]
        with nc.Block() as block:
            @block.sync
            def _(eng):
                def front(k, t, n, u):
                    wait(eng, X["tr"], t - 1)
                    eng.dma_start(xr[:, u], xg_d.ap()[at_chunk(t, 2 * ROWS)].rearrange("(r p) c -> p r c", p=ROWS)).then_inc(x_ld[u], 16)

                staged(eng, front, None, PAIRS, 1)

            @block.tensor
            def _(eng):
                def front(k, t, n, u):
                    wait_alone(eng, x_ld[u], (n + 1) * 16)
                    wait_alone(eng, X["ev"], t - 1)
                    for r in range(2):
                        for h in range(2):
                            m = eng.transpose(psS[:, u, (2 * r + h) * 128:(2 * r + h + 1) * 128],
                                              xr[:, u, r, h * 128:(h + 1) * 128], ident[:])
                    m.then_inc(X["tr"], 1)

                def back(k, t, n, u):
                    _, experts = nc.values_load_multi_w_load_instructions(
                        EID[0:1, at_chunk(t, 2)], [mybir.EngineType.PE], min_val=0, max_val=E0 - 1)
                    wait(eng, X["ev"], t + 1)
                    wait(eng, X["y"], t - 1)
                    for r, e in enumerate(experts):
                        for h in range(2):
                            m = eng.matmul(psZ[:, u, r * C:(r + 1) * C], xt[:, u, r, h * 128:(h + 1) * 128],
                                           w_moe_s[:, bass.ds(e * (2 * C) + h * C, C)], start=(h == 0), stop=(h == 1))
                    m.then_inc(X["mm"], 1)
                staged(eng, front, back, PAIRS, 1)

            @block.scalar
            def _(eng):
                def front(k, t, n, u):
                    wait(eng, X["tr"], t + 1)
                    wait(eng, X["mm"], t - 1)
                    eng.activation(xt[:, u].rearrange("p r c -> p (r c)"), psS[:, u], ACT.Copy).then_inc(X["ev"], 1)

                def late(k, t, n, u):
                    wait(eng, X["y"], t + 1)
                    eng.dma_start(yg_d.ap()[at_chunk(t, 2 * ROWS)].rearrange("(r p) c -> p r c", p=ROWS),
                                  yr[u].rearrange("p (r c) -> p r c", r=2)).then_inc(x_st[u], 16)
                staged(eng, front, None, PAIRS, 1, late=late)
                for u in range(2):
                    eng.wait_ge(x_st[u], PAIRS // 2 * 16)

            @block.vector
            def _(eng):
                def back(k, t, n, u):
                    wait(eng, X["mm"], t + 1)
                    wait(eng, x_st[u], n * 16)
                    eng.tensor_copy(yr[u], psZ[:, u]).then_inc(X["y"], 1)
                staged(eng, None, back, PAIRS, 1)

        gn = Norm("h", eps_c)
        H = {k: sem(f"h_{k}") for k in ("ix", "pc", "y0", "y", "tr", "x2")}
        h_g = [sem(f"h_g{u}") for u in range(2)]
        gath = sbd("gath", [SUB, 2, NSUB * 2, C])
        yn = xnb
        with nc.Block() as block:
            @block.gpsimd
            def _(eng):
                def front(k, t, n, u):
                    if k == 0:
                        wait_alone(eng, H["ix"], t + 1)
                        wait_alone(eng, H["y"], t - 1)
                        for s in range(NSUB):
                            for j in range(2):
                                i = 2 * s + j
                                eng.indirect_dma_start(gath[:, u, i], None, yg_d.ap(),
                                                       bass.IndirectOffsetOnAxis(ap=idx[:, u, i:i + 1], axis=0)).then_inc(h_g[u], 16)

                staged(eng, front, None, slots=1)

            @block.vector
            def _(eng):
                def front(k, t, n, u):
                    if k == 0:
                        wait_alone(eng, h_g[u], n * 16 * NSUB * 2)
                        eng.tensor_copy(idx[:, u], SLOT[:, at_chunk(t, NSUB)].rearrange("p t j -> p (t j)")).then_inc(H["ix"], 1)
                        eng.tensor_copy(pc[:, u], P12[:, at_chunk(t, NSUB)].rearrange("p t j -> p (t j)")).then_inc(H["pc"], 1)

                def back(k, t, n, u):
                    if k == 1:
                        wait_alone(eng, h_g[u], (n + 1) * 16 * NSUB * 2)
                        wait_alone(eng, H["tr"], t - 1)
                        wait_alone(eng, H["pc"], t + 1)
                        for s in range(NSUB):
                            m = eng.tensor_scalar(yn[:, u, s], gath[:, u, 2 * s], pc[:, u, 2 * s:2 * s + 1], None, ALU.mult)
                        m.then_inc(H["y0"], 1)
                        wait_alone(eng, H["y0"], t + 1)
                        for s in range(NSUB):
                            m = eng.scalar_tensor_tensor(out=yn[:, u, s], in0=gath[:, u, 2 * s + 1],
                                                         scalar=pc[:, u, 2 * s + 1:2 * s + 2], in1=yn[:, u, s],
                                                         op0=ALU.mult, op1=ALU.add)
                        m.then_inc(H["y"], 1)
                    if k == 4:
                        wait_alone(eng, H["tr"], t + 1)
                        eng.tensor_tensor(chunk_of(V, t), chunk_of(V, t), psN[:, :, 0:CH], ALU.add).then_inc(H["x2"], 1)

                def late(k, t, n, u):
                    if k == 0:
                        gn.dve_dev(eng, t, chunk_of(V, t), vv[:, u])
                    if k == 2:
                        y = chunk_of(OUT, t)
                        gn.dve_norm(eng, t, vv[:, u], y).then_inc(gn.done, 1)
                        wait_alone(eng, gn.done, t + 1)
                        for h in range(2):
                            eng.tensor_reduce(YS[:, at_chunk(t), h].rearrange("p t b -> p (t b)"),
                                              y[:, h].rearrange("p (b w) -> p b w", b=IMGS), AX.X, ALU.add)
                staged(eng, front, back, slots=5, late=late)

            @block.scalar
            def _(eng):
                def late(k, t, n, u):
                    if k == 0:
                        wait(eng, gn.var, t)
                        gn.act_square(eng, t, vv[:, u])
                    if k == 1:
                        gn.act_rstd(eng, t)
                staged(eng, None, None, slots=5, late=late)

            @block.tensor
            def _(eng):
                def back(k, t, n, u):
                    if k == 3:
                        wait_alone(eng, H["y"], t + 1)
                        wait_alone(eng, H["x2"], t)
                        for s in range(NSUB):
                            for h in range(2):
                                m = eng.transpose(psN[:, h, s * SUB:(s + 1) * SUB], yn[:, u, s, h * 128:(h + 1) * 128],
                                                  ident[0:SUB, 0:SUB])
                        m.then_inc(H["tr"], 1)

                def late(k, t, n, u):
                    if k == 0:
                        wait_alone(eng, H["x2"], t + 1)
                        wait_alone(eng, gn.log, t)
                        gn.pe_mean(eng, t, chunk_of(V, t))
                    if k == 1:
                        gn.pe_var(eng, t)
                staged(eng, None, back, slots=5, late=late)
        d_ctx.close()

        SE_E = 8
        SC = sb("SC", [128, T, 2, IMGS])
        s_se = {k: sem(f"se_{k}") for k in ("w", "dve", "pe", "act")}
        with ExitStack() as c3:
            def sb3(name, shape):
                return c3.enter_context(nc.sbuf_tensor(name, shape, F32))
            w1t = sb3("w1t", [128, 2, 128])
            wgt = sb3("wgt", [128, 2, SE_E])
            w2t = sb3("w2t", [128, C])
            b1t = sb3("b1t", [128, 1])
            b2t = sb3("b2t", [SE_E, C])
            bgt = sb3("bgt", [B, SE_E])
            ym = sb3("ym", [128, 2, B])
            hid = sb3("hid", [128, B])
            gate = sb3("gate", [B, 3, SE_E])
            gs = sb3("gs", [B, 3])
            gT = sb3("gT", [SE_E, B])
            sg = sb3("sg", [128, 2, B])
            with nc.Block() as block:
                @block.sync
                def _(eng):
                    eng.dma_start(w1t[:], se_w1T.rearrange("(h p) e -> p h e", p=128)).then_inc(s_se["w"], 16)
                    eng.dma_start(wgt[:], se_wgT.rearrange("(h p) e -> p h e", p=128)).then_inc(s_se["w"], 16)
                    eng.dma_start(w2t[:], se_w2T).then_inc(s_se["w"], 16)
                    eng.dma_start(b1t[:], se_b1).then_inc(s_se["w"], 16)
                    eng.dma_start(b2t[:], se_b2).then_inc(s_se["w"], 16)
                    eng.dma_start(bgt[:], se_bg.partition_broadcast(B)).then_inc(s_se["w"], 16)
                    eng.wait_ge(s_se["w"], 96)

                @block.vector
                def _(eng):
                    count = [0]

                    def step(ins):
                        ins.then_inc(s_se["dve"], 1)
                        count[0] += 1
                        eng.wait_ge(s_se["dve"], count[0])
                    step(eng.tensor_scalar(ym[:].rearrange("p h (t b) -> p h t b", b=IMGS),
                                           YS[:].rearrange("p t h b -> p h t b"), 1.0 / HW, None, ALU.mult))
                    eng.wait_ge(s_se["w"], 96)
                    eng.wait_ge(s_se["pe"], 1)
                    step(eng.tensor_tensor(gate[:, 0], psM[0:B, 0:SE_E], bgt[:], ALU.add))
                    step(eng.tensor_reduce(gs[:, 0:1], gate[:, 0], AX.X, ALU.max, negate=True))
                    eng.wait_ge(s_se["act"], 1)
                    step(eng.reciprocal(gs[:, 2:3], gs[:, 1:2]))
                    step(eng.tensor_scalar(gate[:, 2], gate[:, 1], gs[:, 2:3], None, ALU.mult))
                    eng.wait_ge(s_se["pe"], 3)
                    step(eng.tensor_copy(gT[:], psM[0:SE_E, 64:64 + B]))
                    eng.wait_ge(s_se["pe"], 4)
                    eng.wait_ge(s_se["act"], 2)
                    step(eng.tensor_tensor(hid[:], hid[:], psM[:, 128:128 + B], ALU.mult))
                    eng.wait_ge(s_se["act"], 4)
                    step(eng.tensor_scalar(sg[:], sg[:], 1.0, None, ALU.add))
                    step(eng.reciprocal(SC[:].rearrange("p t h b -> p h t b"),
                                        sg[:].rearrange("p h (t b) -> p h t b", b=IMGS)))

                @block.tensor
                def _(eng):
                    eng.wait_ge(s_se["w"], 96)
                    eng.wait_ge(s_se["dve"], 1)
                    for h in range(2):
                        m = eng.matmul(psM[0:B, 0:SE_E], ym[:, h], wgt[:, h], start=(h == 0), stop=(h == 1))
                    m.then_inc(s_se["pe"], 1)
                    for h in range(2):
                        m = eng.matmul(psO[:, 0:B], w1t[:, h], ym[:, h], start=(h == 0), stop=(h == 1))
                    m.then_inc(s_se["pe"], 1)
                    eng.wait_ge(s_se["dve"], 5)
                    eng.transpose(psM[0:SE_E, 64:64 + B], gate[:, 2], ident[0:B, 0:B]).then_inc(s_se["pe"], 1)
                    eng.wait_ge(s_se["dve"], 6)
                    eng.matmul(psM[:, 128:128 + B], ind_s[0:SE_E, :], gT[:], start=True, stop=True).then_inc(s_se["pe"], 1)
                    eng.wait_ge(s_se["dve"], 7)
                    for h in range(2):
                        dst = psZ[:, h, 0:B]
                        eng.matmul(dst, w2t[:, h * 128:(h + 1) * 128], hid[:], start=True, stop=False)
                        m = eng.matmul(dst, b2t[:, h * 128:(h + 1) * 128], gT[:], start=False, stop=True)
                    m.then_inc(s_se["pe"], 1)

                @block.scalar
                def _(eng):
                    eng.wait_ge(s_se["dve"], 3)
                    eng.activation(gate[:, 1], gate[:, 0], ACT.Exp, bias=gs[:, 0:1], accum_out=gs[:, 1:2]).then_inc(s_se["act"], 1)
                    eng.wait_ge(s_se["pe"], 2)
                    eng.wait_ge(s_se["w"], 96)
                    eng.activation(hid[:], psO[:, 0:B], ACT.Relu, bias=b1t[:, 0:1]).then_inc(s_se["act"], 1)
                    eng.wait_ge(s_se["pe"], 5)
                    for h in range(2):
                        eng.activation(sg[:, h], psZ[:, h, 0:B], ACT.Exp, scale=-1.0).then_inc(s_se["act"], 1)

        hs_d = nc.dram_tensor("hs_d", [T, C, CH], F32)
        wt_d = nc.dram_tensor("wt_d", [T, NH * NE, CH], F32)
        ex_d = nc.dram_tensor("ex_d", [T, SUB, NSUB * NH * NE], F32)
        HE = NH * NE
        f_ctx = phase()

        def sbf(name, shape, dt=F32):
            return f_ctx.enter_context(nc.sbuf_tensor(name, shape, dt))
        wm_s = sbf("wm_s", [128, 2, C])
        bm_s = sbf("bm_s", [128, 2])
        embd = sbf("embd", [128, 4, NE])
        hs = BIG[:, 2 * T * CH:2 * T * CH + 4 * CH].rearrange("p (u h c) -> p u h c", u=2, h=2)
        dl = sbf("dlf", [SUB, NSUB * NH, NE])
        exf = sbf("exf", [SUB, 2, NSUB * NH, NE])
        mx = sbf("mxf", [SUB, NSUB * NH])
        fn = Norm("f", eps_t)
        FD = {k: sem(f"f_{k}") for k in ("w", "set", "x3", "lin", "hs", "lgd", "max", "dl", "exp")}
        f_hst = [sem(f"f_hst{u}") for u in range(2)]
        f_wst = [sem(f"f_wst{u}") for u in range(2)]
        with nc.Block() as block:
            @block.sync
            def _(eng):
                eng.dma_start(wm_s[:], wm.rearrange("(h p) e -> p h e", p=128)).then_inc(FD["w"], 16)
                eng.dma_start(bm_s[:], bm).then_inc(FD["w"], 16)
                eng.wait_ge(FD["set"], 1)
                for q in range(4):
                    eng.dma_start(embd[32 * q:32 * q + 32, q], emb).then_inc(FD["w"], 16)
                eng.wait_ge(FD["w"], 96)

            @block.gpsimd
            def _(eng):
                eng.memset(embd[:], 0.0).then_inc(FD["set"], 1)

        with nc.Block() as block:
            @block.vector
            def _(eng):
                def front(k, t, n, u):
                    if k == 0:
                        for h in range(2):
                            for b in range(IMGS):
                                w_ = slice(b * HW, (b + 1) * HW)
                                x3 = V[:, h, at_chunk(t), w_].squeeze(1)
                                m = eng.scalar_tensor_tensor(
                                    out=x3, in0=OUT[:, h, at_chunk(t), w_].squeeze(1),
                                    scalar=SC[:, at_chunk(t), h, b], in1=x3, op0=ALU.mult, op1=ALU.add)
                        m.then_inc(FD["x3"], 1)

                def back(k, t, n, u):
                    if k == 0:
                        wait_alone(eng, FD["lin"], t - 1)
                        fn.dve_dev(eng, t, chunk_of(V, t), vv[:, u])
                    if k == 2:
                        fn.dve_norm(eng, t, vv[:, u], vv[:, u]).then_inc(fn.done, 1)

                def late(k, t, n, u):
                    if k == 3:
                        wait_alone(eng, FD["lgd"], t + 1)
                        wait_alone(eng, FD["exp"], t)
                        lgs = psN[0:SUB, 0].rearrange("p (s e) -> p s e", e=NE)
                        eng.tensor_reduce(mx[:], lgs, AX.X, ALU.max).then_inc(FD["max"], 1)
                        wait_alone(eng, FD["max"], t + 1)
                        eng.tensor_tensor(dl[:], lgs, mx[:].unsqueeze(2).to_broadcast([SUB, NSUB * NH, NE]),
                                          ALU.subtract).then_inc(FD["dl"], 1)
                staged(eng, front, back, slots=5, late=late)

            @block.sync
            def _(eng):
                def late(k, t, n, u):
                    if k == 1:
                        wait(eng, FD["hs"], t + 1)
                        eng.dma_start(hs_d.ap()[at_chunk(t)][0].rearrange("(h p) c -> p h c", h=2),
                                      hs[:, u]).then_inc(f_hst[u], 16)
                    if k == 4:
                        wait(eng, FD["exp"], t + 1)
                        eng.dma_start(ex_d.ap()[at_chunk(t)][0], exf[:, u].rearrange("p s e -> p (s e)")).then_inc(f_wst[u], 16)
                staged(eng, None, None, slots=5, late=late)
                for u in range(2):
                    eng.wait_ge(f_hst[u], T // 2 * 16)
                    eng.wait_ge(f_wst[u], T // 2 * 16)

            @block.scalar
            def _(eng):
                def back(k, t, n, u):
                    if k == 0:
                        wait(eng, fn.var, t)
                        fn.act_square(eng, t, vv[:, u])
                    if k == 1:
                        fn.act_rstd(eng, t)

                def late(k, t, n, u):
                    if k == 0:
                        wait_alone(eng, FD["lin"], t + 1)
                        wait_alone(eng, f_hst[u], n * 16)
                        wait_alone(eng, FD["lgd"], t - 1)
                        for m_ in range(2):
                            m = eng.activation(hs[:, u, m_], psS[:, m_, 0:CH], ACT.Identity, bias=bm_s[:, m_:m_ + 1])
                        m.then_inc(FD["hs"], 1)
                    if k == 4:
                        wait_alone(eng, FD["dl"], t + 1)
                        wait_alone(eng, f_wst[u], n * 16)
                        eng.activation(exf[:, u], dl[:], ACT.Exp).then_inc(FD["exp"], 1)
                staged(eng, None, back, slots=5, late=late)

            @block.tensor
            def _(eng):
                def back(k, t, n, u):
                    if k == 0:
                        wait_alone(eng, FD["x3"], t + 1)
                        wait_alone(eng, fn.log, t)
                        fn.pe_mean(eng, t, chunk_of(V, t))
                    if k == 1:
                        fn.pe_var(eng, t)

                def late(k, t, n, u):
                    if k == 0:
                        wait(eng, fn.done, t + 1)
                        wait(eng, FD["hs"], t)
                        for m_ in range(2):
                            for h in range(2):
                                m = eng.matmul(psS[:, m_, 0:CH], wm_s[:, h, m_ * 128:(m_ + 1) * 128], vv[:, u, h],
                                               start=(h == 0), stop=(h == 1))
                        m.then_inc(FD["lin"], 1)
                    if k == 2:
                        wait_alone(eng, FD["hs"], t + 1)
                        wait_alone(eng, FD["dl"], t)
                        for s in range(NSUB):
                            for m_ in range(2):
                                dst = psN[0:SUB, 0, s * HE + m_ * 64:s * HE + m_ * 64 + 64]
                                m = eng.matmul(dst, hs[:, u, m_, s * SUB:(s + 1) * SUB],
                                               embd[:].rearrange("p a e -> p (a e)"), start=True, stop=True)
                        m.then_inc(FD["lgd"], 1)
                staged(eng, None, back, slots=5, late=late)
        f_ctx.close()

        NI, NP, NS = 8, 16, 64
        w1_s = BIG[:, 0:NE * HID].rearrange("p (e i) -> p e i", e=NE)
        w1_r = sb("w1_r", [128, NE, HID], F32R)
        w2_s = sb("w2_s", [HID, NE, HD])
        b1_s = sb("b1_s", [HID, NE])
        b2_s = sb("b2_s", [128, 4])
        wo_s = sb("wo_s", [128, 2, C])
        bo_s = sb("bo_s", [128, 2])
        foldm = sb("fold", [128, HD])
        x_r = sb("x_r", [128, 2, 4, CH], F32R)
        stk = BIG[:, 0:8 * CH].rearrange("p (a q c) -> p a q c", a=2, q=4)
        wb = BIG[:, 8 * CH:16 * CH].rearrange("p (a q c) -> p a q c", a=2, q=4)
        gsum = BIG[:, 16 * CH:24 * CH].rearrange("p (a q c) -> p a q c", a=2, q=4)
        comb = BIG[:, 24 * CH:26 * CH].rearrange("p (a c) -> p a c", a=2)
        fin = BIG[:, 26 * CH:28 * CH].rearrange("p (a c) -> p a c", a=2)
        gacc = BIG[:, 28 * CH:36 * CH].rearrange("p (a q c) -> p a q c", a=2, q=4)
        hid = [xs[:, 0], xs[:, 1], vv[:, 0], vv[:, 1], ex[:], at[:], rz[:], sq[:]]
        Q = {k: sem(f"q_{k}") for k in ("w", "set", "hi", "lo", "mm1", "gel", "mm2", "gs", "acc", "fold", "comb",
                                        "wo", "fin", "rt", "tr", "wt")}
        q_ex, q_wst = sem("q_ex"), sem("q_wst")
        q_stk = [sem(f"q_stk{a}") for a in range(2)]
        q_wb = [sem(f"q_wb{a}") for a in range(2)]
        q_st = [sem(f"q_st{a}") for a in range(2)]
        psA, psY = (psN, psS, psZ), (psM, psO)

        RT2 = 16
        EXP, EQ, M1, L2, M2 = range(5)
        rt = sb("rt", [SUB, 5, NSUB * NH, NE])
        rs16 = sb("rs16", [SUB, 6, NSUB * NH])
        rev16 = sb("rev16", [SUB, NE])
        rev_i = sb("rev_i", [SUB, NE], U32)
        wts = sb("wts", [128, CH])

        def route(eng, r, steps):
            L = lambda i: rt[:, i]
            S_ = lambda i: rs16[:, i]
            many = lambda i: rs16[:, i].unsqueeze(2).to_broadcast([SUB, NSUB * NH, NE])
            revb = rev16[:].unsqueeze(1).to_broadcast([SUB, NSUB * NH, NE])
            for i in steps:
                if i == 0:
                    wait_alone(eng, q_ex, (r + 1) * 16)
                    wait_alone(eng, Q["tr"], r)
                wait_alone(eng, Q["rt"], r * RT2 + i)
                if i == 0:
                    m = eng.tensor_reduce(S_(0), L(EXP), AX.X, ALU.max)
                if i == 1:
                    m = eng.tensor_reduce(S_(4), L(EXP), AX.X, ALU.add)
                if i in (2, 9):
                    m = eng.tensor_tensor(L(EQ), L(EXP if i == 2 else L2), many(0 if i == 2 else 1), ALU.is_equal)
                if i in (3, 10):
                    m = eng.tensor_tensor(L(EQ), L(EQ), revb, ALU.mult)
                if i in (4, 11):
                    m = eng.tensor_reduce(S_(2 if i == 4 else 3), L(EQ), AX.X, ALU.max)
                if i in (5, 12):
                    m = eng.tensor_tensor(L(M1 if i == 5 else M2), L(EQ), many(2 if i == 5 else 3), ALU.is_equal)
                if i == 6:
                    m = eng.reciprocal(S_(5), S_(4))
                if i == 7:
                    m = eng.scalar_tensor_tensor(out=L(L2), in0=L(M1), scalar=NEG, in1=L(EXP), op0=ALU.mult, op1=ALU.add)
                if i == 8:
                    m = eng.tensor_reduce(S_(1), L(L2), AX.X, ALU.max)
                if i == 13:
                    m = eng.tensor_tensor(L(M2), L(M1), L(M2), ALU.add)
                if i == 14:
                    m = eng.tensor_tensor(L(M2), L(EXP), L(M2), ALU.mult)
                if i == 15:
                    m = eng.tensor_tensor(L(M1), L(M2), many(5), ALU.mult)
                m.then_inc(Q["rt"], 1)

        def route_pe(eng, r):
            wait_alone(eng, Q["rt"], (r + 1) * RT2)
            for s in range(NSUB):
                m = eng.transpose(psY[1][:, s * SUB:(s + 1) * SUB],
                                  rt[:, M1, s * NH:(s + 1) * NH].rearrange("p h e -> p (h e)"), ident[0:SUB, 0:SUB])
            m.then_inc(Q["tr"], 1)

        def route_copy(eng, r):
            wait_alone(eng, Q["tr"], r + 1)
            wait_alone(eng, q_wst, r * 16)
            eng.tensor_copy(wts[:], psY[1][:, 0:CH]).then_inc(Q["wt"], 1)

        def route_load(eng, r):
            wait(eng, Q["rt"], r * RT2)
            eng.dma_start(rt[:, EXP].rearrange("p s e -> p (s e)"), ex_d.ap()[at_chunk(r)][0]).then_inc(q_ex, 16)

        def route_store(eng, r):
            wait(eng, Q["wt"], r + 1)
            eng.dma_start(wt_d.ap()[at_chunk(r)][0], wts[:]).then_inc(q_wst, 16)

        bufs = [m % 3 for m in range(NS - 1)] + [1]

        def lag(m):
            return next(d for d in range(1, 6) if bufs[(m - d) % NS] == bufs[m])

        def chunks(eng, body, tail):
            body(0)
            body(1)
            with eng.Fori(2, T - 1) as t:
                body(t)
            body(T - 1)
            tail(T)

        def is_last(t):
            return isinstance(t, int) and t == T - 1

        with nc.Block() as block:
            @block.sync
            def _(eng):
                route_load(eng, 0)
                for q in range(4):
                    eng.dma_start(w1_s[32 * q:32 * q + 32], w1).then_inc(Q["w"], 16)
                eng.dma_start(w2_s[:], w2).then_inc(Q["w"], 16)
                eng.dma_start(b1_s[:], b1).then_inc(Q["w"], 16)
                eng.dma_start(b2_s[:], b2).then_inc(Q["w"], 16)
                eng.dma_start(wo_s[:], wo.rearrange("(h p) e -> p h e", p=128)).then_inc(Q["w"], 16)
                eng.dma_start(bo_s[:], bo).then_inc(Q["w"], 16)
                eng.wait_ge(Q["w"], 9 * 16)
                route_store(eng, 0)
                eng.wait_ge(q_wst, 16)

            @block.tensor
            def _(eng):
                route_pe(eng, 0)

            @block.gpsimd
            def _(eng):
                eng.iota(rev_i[:], pattern=[[-1, NE]], base=NE, channel_multiplier=0).then_inc(Q["set"], 1)
                eng.wait_ge(Q["set"], 1)
                eng.tensor_copy(rev16[:], rev_i[:]).then_inc(Q["set"], 1)
                eng.wait_ge(Q["set"], 2)
                eng.memset(foldm[:], 0.0).then_inc(Q["set"], 1)
                for r in range(4):
                    eng.wait_ge(Q["set"], r + 3)
                    eng.affine_select(out=foldm[:], in_=foldm[:], compare_op=ALU.not_equal, fill=1.0,
                                      base=-32 * r, pattern=[[-1, HD]], channel_multiplier=1).then_inc(Q["set"], 1)

            @block.vector
            def _(eng):
                eng.wait_ge(Q["w"], 9 * 16)
                eng.tensor_copy(w1_r[:], w1_s[:]).then_inc(Q["hi"], 1)
                eng.wait_ge(Q["hi"], 1)
                for row in (32, 96):
                    rows = slice(row, row + 32)
                    eng.tensor_tensor(w1_r[rows], w1_s[rows], w1_r[rows].bitcast(F32), ALU.subtract)
                eng.wait_ge(Q["set"], 2)
                route(eng, 0, range(RT2))
                route_copy(eng, 0)

            @block.scalar
            def _(eng):
                eng.preload_act_table_set("gelu_and_others")

        with nc.Block() as block:
            @block.sync
            def _(eng):
                def store(t):
                    for m_ in range(2):
                        wait(eng, Q["fin"], t * 2 - 1 + m_)
                        eng.dma_start(out_v[at_chunk(t - 1)][0, :, m_],
                                      fin[:, m_].rearrange("p (b w) -> p b w", b=IMGS)).then_inc(q_st[m_], 16)

                def heads_load(t, half):
                    wait(eng, Q["lo"], 2 * t + half - 1)
                    for r in range(4):
                        eng.dma_start(stk[32 * r:32 * r + 32, half],
                                      hs_d.ap()[at_chunk(t)][0, half * 128:half * 128 + 128].rearrange(
                                          "(q p) c -> p q c", q=4)).then_inc(q_stk[half], 16)

                def body(t):
                    if isinstance(t, int) and t == 0:
                        heads_load(0, 0)
                    if not is_last(t):
                        route_load(eng, t + 1)
                    wait(eng, q_wst, (t + 1) * 16)
                    for it in range(NI):
                        half, group = it // 4, it % 4
                        if it == 6 and not is_last(t):
                            route_store(eng, t + 1)
                        if it == 1:
                            heads_load(t, 1)
                        if it == 5 and not is_last(t):
                            heads_load(t + 1, 0)
                        wait(eng, Q["gs"], (t * NI + it - 1) * 4)
                        for e in range(4):
                            src = wt_d.ap()[at_chunk(t)][0].rearrange("(h e) c -> e h c", h=NH)[group * 4 + e]
                            eng.dma_start(wb[32 * e:32 * e + 32, it % 2],
                                          src[half * 4:half * 4 + 4].partition_broadcast(32)).then_inc(q_wb[it % 2], 16)
                        if it == 4 and not (isinstance(t, int) and t == 0):
                            store(t)
                chunks(eng, body, store)
                for m_ in range(2):
                    eng.wait_ge(q_st[m_], 16 * T)

            @block.gpsimd
            def _(eng):
                def split(t, half):
                    wait_alone(eng, q_stk[half], (t + 1) * 64)
                    wait_alone(eng, Q["mm1"], (2 * t + half - 1) * (NS // 2))
                    eng.tensor_copy(x_r[:, half], stk[:, half]).then_inc(Q["hi"], 1)
                    wait_alone(eng, Q["hi"], 2 * t + half + 2)
                    eng.tensor_tensor(x_r[64:128, half], stk[64:128, half], x_r[64:128, half].bitcast(F32),
                                      ALU.subtract).then_inc(Q["lo"], 1)
                    wait_alone(eng, Q["lo"], 2 * t + half + 1)

                def body(t):
                    if isinstance(t, int) and t == 0:
                        split(0, 0)
                    for P in range(NP):
                        half, it, q = P // 8, P // 2, P % 2 * 2
                        if P == 2:
                            split(t, 1)
                        if P == 10 and not is_last(t):
                            split(t + 1, 0)
                        wait_alone(eng, Q["gs"], (t * NP + P + 1) * 2)
                        src, dst = gsum[:, it % 2, q:q + 2], gacc[:, half, q:q + 2]
                        if it % 4 == 0:
                            wait_alone(eng, Q["fold"], 2 * t + half - 1)
                            m = eng.tensor_copy(dst, src)
                        else:
                            wait_alone(eng, Q["acc"], t * NP + P - 1)
                            m = eng.tensor_tensor(dst, dst, src, ALU.add)
                        m.then_inc(Q["acc"], 1)
                chunks(eng, body, lambda t: None)

            @block.tensor
            def _(eng):
                def second(t, P, hh):
                    if hh == 0:
                        wait_alone(eng, Q["gel"], t * NS + P * 4 + 4)
                    wait_alone(eng, Q["gs"], (t * NP + P) * 2 + hh - 1)
                    for e in range(4):
                        mm = eng.matmul(psY[hh][32 * e:32 * e + 32, 0:CH], w2_s[:, (P // 2 % 4) * 4 + e],
                                        hid[(P % 2) * 4 + e][:, hh], start=True, stop=True,
                                        tile_position=(0, 32 * e))
                    mm.then_inc(Q["mm2"], 1)

                def fold(t, half):
                    wait_alone(eng, Q["acc"], t * NP + half * 8 + 8)
                    for q in range(4):
                        mm = eng.matmul(psY[1][32 * q:32 * q + 32, 0:CH], foldm[:], gacc[:, half, q],
                                        start=True, stop=True, tile_position=(0, 32 * q))
                    mm.then_inc(Q["fold"], 1)

                def last(t, m_):
                    wait_alone(eng, Q["comb"], t * 2)
                    for h in range(2):
                        mm = eng.matmul(psY[1][:, 0:CH], wo_s[:, h, m_ * 128:(m_ + 1) * 128], comb[:, h],
                                        start=(h == 0), stop=(h == 1))
                    mm.then_inc(Q["wo"], 1)

                def body(t):
                    first = isinstance(t, int) and t == 0
                    extra = {11: (lambda: fold(t, 0), Q["comb"], 2 * t + 1)}
                    if not first:
                        extra[2] = lambda: fold(t - 1, 1), Q["comb"], 2 * t
                        extra[4] = lambda: last(t, 0), Q["fin"], 2 * t - 1
                        extra[6] = lambda: last(t, 1), Q["fin"], 2 * t
                    if not is_last(t):
                        extra[9] = lambda: route_pe(eng, t + 1), Q["wt"], t + 2
                    for P in range(NP):
                        half, group, pair = P // 8, P // 2 % 4, P % 2
                        if P % 8 == 0:
                            wait_alone(eng, Q["lo"], 2 * t + half + 1)
                        for e in range(4):
                            m = 4 * P + e
                            wait_alone(eng, Q["gel"], t * NS + m + 1 - lag(m))
                            for hh in range(2):
                                mm = eng.matmul(psA[bufs[m]][:, hh, 0:CH], w1_r[:, group * 4 + e],
                                                x_r[:, half, pair * 2 + hh], start=True, stop=True)
                            mm.then_inc(Q["mm1"], 1)
                            if e in (1, 3):
                                if e == 3 and P in extra:
                                    wait_alone(eng, extra[P][1], extra[P][2])
                                if P > 0:
                                    second(t, P - 1, e // 2)
                                elif not first:
                                    second(t - 1, NP - 1, e // 2)
                                if e == 1 and P in extra:
                                    wait_alone(eng, Q["gs"], (t * NP + P - 1) * 2)
                                    extra[P][0]()

                def tail(t):
                    for hh in range(2):
                        second(t - 1, NP - 1, hh)
                    wait_alone(eng, Q["gs"], t * NP * 2)
                    fold(t - 1, 1)
                    for m_ in range(2):
                        wait_alone(eng, Q["comb"] if m_ == 0 else Q["fin"], 2 * t if m_ == 0 else 2 * t - 1)
                        last(t, m_)
                chunks(eng, body, tail)

            @block.scalar
            def _(eng):
                def body(t):
                    for m in range(NS):
                        P, e = m // 4, m % 4
                        if e == 0:
                            wait_alone(eng, Q["mm2"], (t * NP + P - 1) * 2)
                        wait_alone(eng, Q["mm1"], t * NS + m + 1)
                        ex_ = (P // 2 % 4) * 4 + e
                        eng.activation(hid[m % 8], psA[bufs[m]][:, :, 0:CH], ACT.Gelu,
                                       bias=b1_s[:, ex_:ex_ + 1]).then_inc(Q["gel"], 1)
                chunks(eng, body, lambda t: None)

            @block.vector
            def _(eng):
                def combine(t, half):
                    wait_alone(eng, Q["fold"], t * 2 + half + 1)
                    wait_alone(eng, Q["wo"], t * 2)
                    eng.tensor_copy(comb[:, half], psY[1][:, 0:CH]).then_inc(Q["comb"], 1)

                def finish(t, m_):
                    wait_alone(eng, Q["wo"], t * 2 - 1 + m_)
                    wait_alone(eng, q_st[m_], (t - 1) * 16)
                    eng.scalar_tensor_tensor(out=fin[:, m_], in0=psY[1][:, 0:CH], scalar=bo_s[:, m_:m_ + 1],
                                             in1=V[:, m_, at_chunk(t - 1)].rearrange("p t c -> p (t c)"),
                                             op0=ALU.add, op1=ALU.add).then_inc(Q["fin"], 1)

                def body(t):
                    first = isinstance(t, int) and t == 0
                    extra = {10: lambda: combine(t, 0)}
                    if not first:
                        extra[1] = lambda: combine(t - 1, 1)
                        extra[3] = lambda: finish(t, 0)
                        extra[5] = lambda: finish(t, 1)
                    if not is_last(t):
                        extra[8] = lambda: route_copy(eng, t + 1)
                    for P in range(NP):
                        it, pair = P // 2, P % 2
                        if P < RT2 // 2 and not is_last(t):
                            route(eng, t + 1, (2 * P, 2 * P + 1))
                        if pair == 0:
                            wait_alone(eng, q_wb[it % 2], (t * (NI // 2) + it // 2 + 1) * 64)
                        wait_alone(eng, Q["acc"], t * NP + P - 3)
                        for hh in range(2):
                            wait_alone(eng, Q["mm2"], (t * NP + P) * 2 + hh + 1)
                            q = pair * 2 + hh
                            eng.scalar_tensor_tensor(out=gsum[:, it % 2, q], in0=psY[hh][:, 0:CH],
                                                     scalar=b2_s[:, it % 4:it % 4 + 1], in1=wb[:, it % 2, q],
                                                     op0=ALU.add, op1=ALU.mult).then_inc(Q["gs"], 1)
                            if hh == 0 and P in extra:
                                extra[P]()

                def tail(t):
                    combine(t - 1, 1)
                    for m_ in range(2):
                        finish(t, m_)
                chunks(eng, body, tail)


def arrays(i):
    import numpy as np
    a = {k: np.asarray(v) for k, v in i.items()}
    ac = np.ascontiguousarray
    r = {}
    r["x"] = a["x"].reshape(B, C, HW)
    r["c1T"] = ac(a["L0_conv_c1_centroids"].transpose(0, 2, 1)).reshape(C, KC)
    r["c2T"] = ac(a["L0_conv_c2_centroids"].reshape(8, 8, KC, 9).transpose(1, 3, 0, 2)).reshape(72, 8, KC)
    r["c3T"] = ac(a["L0_conv_c3_centroids"].transpose(0, 2, 1)).reshape(WID, KC)
    r["invts"] = np.stack([a[f"L0_conv_c{n}_invt"].reshape(()) for n in (1, 2, 3)]).reshape(1, 3)
    r["lut1"] = a["L0_conv_c1_lut"].reshape(-1, WID)
    r["lut2"] = a["L0_conv_c2_lut"].reshape(-1, WID)
    r["lut3"] = a["L0_conv_c3_lut"].reshape(-1, C)
    for n in (1, 2, 3):
        r[f"bn{n}"] = np.stack([a[f"L0_conv_bn{n}_g"], a[f"L0_conv_bn{n}_b"]], 1)
    r["routerT"] = ac(a["L0_ffn_router_w"].T)
    r["w_moe"] = a["L0_ffn_expert_weights"]
    r["se_w1T"] = ac(a["L1_conv_W1"].reshape(128, C).T)
    r["se_b1"] = a["L1_conv_b1"].reshape(128, 1)
    r["se_w2T"] = ac(a["L1_conv_W2"].transpose(0, 2, 1)).reshape(128, C)
    r["se_b2"] = a["L1_conv_b2"]
    r["se_wgT"] = ac(a["L1_conv_Wg"].T)
    r["se_bg"] = a["L1_conv_bg"].reshape(1, 8)
    r["wm"] = a["L1_ffn_Wm"]
    r["bm"] = ac(a["L1_ffn_bm"].reshape(2, 128).T)
    r["emb"] = a["L1_ffn_expert_emb"]
    r["w1"] = ac(a["L1_ffn_W1"].transpose(1, 0, 2))
    r["b1"] = ac(a["L1_ffn_b1"].T)
    r["w2"] = ac(a["L1_ffn_W2"].transpose(1, 0, 2))
    r["b2"] = ac(a["L1_ffn_b2"].reshape(4, 4 * HD).T)
    r["wo"] = a["L1_ffn_Wo"]
    r["bo"] = ac(a["L1_ffn_bo"].reshape(2, 128).T)
    return r


def kernel(**inputs):
    import numpy as _np
    import concourse.bacc as _bacc
    from concourse import mybir as _mybir
    from concourse.bass_utils import run_bass_kernel_spmd as _run

    ins = arrays(inputs)
    nc = _bacc.Bacc("TRN2", target_bir_lowering=False, num_devices=1)
    args = [nc.dram_tensor(k, v.shape, _mybir.dt.from_np(v.dtype), kind="ExternalInput").ap() for k, v in ins.items()]
    args.append(nc.dram_tensor("out", (B, C, HW), _mybir.dt.float32, kind="ExternalOutput").ap())
    build(nc, *args)
    r = _run(nc, [ins], core_ids=[0])
    return _np.asarray(r.results[0]["out"]).reshape(B, C, HH, HH)
```
